# Optimizing a Trainium2 kernel written in Bass

```python
import numpy as np
import jax
import jax.numpy as jnp

def _softmax(x, axis=-1):
    return jax.nn.softmax(x, axis=axis)

def _gelu(x):
    return jax.nn.gelu(x, approximate=True)

def _silu(x):
    return jax.nn.silu(x)

def _sigmoid(x):
    return jax.nn.sigmoid(x)

def _layernorm(x, axis=-1, eps=1e-05):
    m = jnp.mean(x, axis=axis, keepdims=True)
    v = jnp.var(x, axis=axis, keepdims=True)
    return (x - m) / jnp.sqrt(v + eps)

def _scatter_add(tgt, idx, src, axis=0):
    return tgt.at[idx].add(src)

def _segment_sum(src, seg, n):
    return jax.ops.segment_sum(src, seg, n)
kernel_name = 'mk_flamingo_gated_d4_seqx_r4_44e1f3'

def setup_inputs(seed: int=0):
    np.random.seed(seed)
    _w = jnp.asarray

    def _rec_inputs():
        import jax
        import jax.numpy as jnp
        _rk = jax.random.key(seed)
        x = -0.0002928 + 1 * jax.random.normal(jax.random.fold_in(_rk, 1), (2, 1024, 256), jnp.float32)
        _lenS = 1024 - jax.random.randint(jax.random.fold_in(_rk, 7), (2,), 0, max(1, 1024 // 4) + 1, jnp.int32)
        _lenS2 = 77 - jax.random.randint(jax.random.fold_in(_rk, 8), (2,), 0, max(1, 77 // 4) + 1, jnp.int32)
        _ctx_1024P = jax.random.normal(jax.random.fold_in(_rk, 11), (2, 16, 256), jnp.float32)
        _ctx_1024c = jax.random.dirichlet(jax.random.fold_in(_rk, 511), 0.3 * jnp.ones((16,), jnp.float32), (2, 77))
        _ctx_1024t = jnp.einsum('bsk,bkd->bsd', _ctx_1024c, _ctx_1024P)
        _ctx_1024t = _ctx_1024t * jax.lax.rsqrt(jnp.mean(jnp.square(_ctx_1024t)) + 1e-12) * 0.953939
        ctx_1024 = -1.39393e-06 + 0.999914 * (_ctx_1024t + 0.3 * jax.random.normal(jax.random.fold_in(_rk, 611), (2, 77, 256), jnp.float32))
        _validS = jnp.arange(1024)[None, :] < _lenS[:, None]
        _validS2 = jnp.arange(77)[None, :] < _lenS2[:, None]
        _causal = jnp.tril(jnp.ones((1024, 1024), dtype=bool))
        mask_BxSxS2_bk1 = jnp.broadcast_to(_validS2[:, None, :], (2, 1024, 77))
        mask_BxS2_bf1 = jnp.ones((2, 77), dtype=bool)
        _g = jax.random.normal(jax.random.fold_in(_rk, 9001), (2, 4), jnp.float32)
        _g = jnp.sign(_g) * jnp.maximum(jnp.abs(_g), 1.0) + (_g == 0) * 1.0
        g_xattn = _g[0]
        g_ffn = _g[1]
        return (x, ctx_1024, mask_BxSxS2_bk1, mask_BxS2_bf1, g_xattn, g_ffn)
    x, ctx_1024, mask_BxSxS2_bk1, mask_BxS2_bf1, g_xattn, g_ffn = _rec_inputs()

    def _L0_xattn_setup():
        import jax, jax.numpy as jnp
        import numpy as np
        DIM = 256
        HEADS = 16
        DIM_HEAD = 64
        INNER = HEADS * DIM_HEAD
        B, N = (2, 512)
        key = jax.random.key(seed)
        ks = jax.random.split(key, 8)
        q = jax.random.normal(ks[0], (B, N, DIM), dtype=jnp.float32)
        k = jax.random.normal(ks[1], (B, N, DIM), dtype=jnp.float32)
        v = jax.random.normal(ks[2], (B, N, DIM), dtype=jnp.float32)
        causal = jnp.triu(jnp.ones((N, N), dtype=jnp.bool_), k=1)
        mask = jnp.broadcast_to(causal, (B, N, N))
        s = 0.02
        Wq = jax.random.normal(ks[3], (DIM, INNER), dtype=jnp.float32) * s
        Wk = jax.random.normal(ks[4], (DIM, INNER), dtype=jnp.float32) * s
        Wv = jax.random.normal(ks[5], (DIM, INNER), dtype=jnp.float32) * s
        Wo = jax.random.normal(ks[6], (INNER, DIM), dtype=jnp.float32) * s
        bo = jnp.zeros((DIM,), dtype=jnp.float32)
        return {'q': q, 'k': k, 'v': v, 'mask': mask, 'Wq': Wq, 'Wk': Wk, 'Wv': Wv, 'Wo': Wo, 'bo': bo}
    _L0_xattn_all = _L0_xattn_setup()
    _L0_xattn_in = {k: v for k, v in _L0_xattn_all.items() if k in ('Wq', 'Wk', 'Wv', 'Wo', 'bo')}
    del _L0_xattn_all

    def _L0_ffn_setup():
        import jax, jax.numpy as jnp
        import numpy as np
        HIDDEN = 256
        INNER = 1024

        def _weight_quant(w):
            scale = 1.0 / jnp.clip(jnp.mean(jnp.abs(w)), 1e-05)
            wq = jnp.clip(jnp.round(w * scale), -1.0, 1.0) / scale
            return w + jax.lax.stop_gradient(wq - w)

        def _act_quant(x):
            scale = 127.0 / jnp.clip(jnp.max(jnp.abs(x), axis=-1, keepdims=True), 1e-05)
            xq = jnp.clip(jnp.round(x * scale), -128.0, 127.0) / scale
            return x + jax.lax.stop_gradient(xq - x)

        def _bitlinear(x, w):
            return jnp.einsum('bsi,oi->bso', _act_quant(x), _weight_quant(w))
        key = jax.random.key(seed)
        k0, k1, k2, k3 = jax.random.split(key, 4)
        x = jax.random.normal(k0, (4, 512, HIDDEN), dtype=jnp.float32)
        w_gate = jax.random.normal(k1, (INNER, HIDDEN), dtype=jnp.float32) / np.sqrt(HIDDEN)
        w_up = jax.random.normal(k2, (INNER, HIDDEN), dtype=jnp.float32) / np.sqrt(HIDDEN)
        w_down = jax.random.normal(k3, (HIDDEN, INNER), dtype=jnp.float32) / np.sqrt(INNER)
        return {'x': x, 'w_gate': w_gate, 'w_up': w_up, 'w_down': w_down}
    _L0_ffn_all = _L0_ffn_setup()
    _L0_ffn_in = {k: v for k, v in _L0_ffn_all.items() if k in ('w_gate', 'w_up', 'w_down')}
    del _L0_ffn_all

    def _L1_xattn_setup():
        import jax, jax.numpy as jnp
        import numpy as np
        HEADS = 8
        DIM_HEAD = 64
        key = jax.random.key(seed)
        ks = jax.random.split(key, 9)
        B, N1, N2, D = (4, 512, 512, 256)
        inner = HEADS * DIM_HEAD
        s_in = 1.0 / np.sqrt(D)
        s_inner = 1.0 / np.sqrt(inner)
        return {'x1': jax.random.normal(ks[0], (B, N1, D), jnp.float32), 'x2': jax.random.normal(ks[1], (B, N2, D), jnp.float32), 'Wq1': jax.random.normal(ks[2], (D, inner), jnp.float32) * s_in, 'Wk1': jax.random.normal(ks[3], (D, inner), jnp.float32) * s_in, 'Wv1': jax.random.normal(ks[4], (D, inner), jnp.float32) * s_in, 'Wk2': jax.random.normal(ks[5], (D, inner), jnp.float32) * s_in, 'Wv2': jax.random.normal(ks[6], (D, inner), jnp.float32) * s_in, 'Wo': jax.random.normal(ks[7], (inner, D), jnp.float32) * s_inner, 'bo': jnp.zeros((D,), jnp.float32)}
    _L1_xattn_all = _L1_xattn_setup()
    _L1_xattn_in = {k: v for k, v in _L1_xattn_all.items() if k in ('Wq1', 'Wk1', 'Wv1', 'Wk2', 'Wv2', 'Wo', 'bo')}
    del _L1_xattn_all

    def _L1_ffn_setup():
        import jax, jax.numpy as jnp
        import numpy as np
        N_EXPERTS = 16
        TOP_K = 4
        HIDDEN = 256
        INTER = 128
        B, S = (2, 256)
        key = jax.random.key(seed)
        k1, k2, k3, k4, k5 = jax.random.split(key, 5)
        return {'hidden_states': jax.random.normal(k1, (B, S, HIDDEN), dtype=jnp.float32), 'gate_w': jax.random.normal(k2, (N_EXPERTS, HIDDEN), dtype=jnp.float32) * 0.02, 'w1': jax.random.normal(k3, (N_EXPERTS, HIDDEN, INTER), dtype=jnp.float32) * 0.02, 'w3': jax.random.normal(k4, (N_EXPERTS, HIDDEN, INTER), dtype=jnp.float32) * 0.02, 'w2': jax.random.normal(k5, (N_EXPERTS, INTER, HIDDEN), dtype=jnp.float32) * 0.02}
    _L1_ffn_all = _L1_ffn_setup()
    _L1_ffn_in = {k: v for k, v in _L1_ffn_all.items() if k in ('gate_w', 'w1', 'w3', 'w2')}
    del _L1_ffn_all

    def _L2_xattn_setup():
        import jax, jax.numpy as jnp
        import numpy as np
        DIM = 256
        HEADS = 16
        DIM_HEAD = 64
        INNER = HEADS * DIM_HEAD
        EPS = 1e-05

        def layer_norm(x, gamma, beta):
            mu = jnp.mean(x, axis=-1, keepdims=True)
            var = jnp.var(x, axis=-1, keepdims=True)
            return (x - mu) * jax.lax.rsqrt(var + EPS) * gamma + beta
        key = jax.random.key(seed)
        ks = jax.random.split(key, 8)
        b, n, m = (8, 1024, 64)
        x = jax.random.normal(ks[0], (b, n, DIM), dtype=jnp.float32)
        latents = jax.random.normal(ks[1], (b, m, DIM), dtype=jnp.float32)
        mask = jnp.ones((b, n), dtype=bool)
        s = 0.02
        Wq = jax.random.normal(ks[2], (DIM, INNER), dtype=jnp.float32) * s
        Wkv = jax.random.normal(ks[3], (DIM, 2 * INNER), dtype=jnp.float32) * s
        Wout = jax.random.normal(ks[4], (INNER, DIM), dtype=jnp.float32) * s
        g_x = jnp.ones((DIM,), jnp.float32)
        b_x = jnp.zeros((DIM,), jnp.float32)
        g_l = jnp.ones((DIM,), jnp.float32)
        b_l = jnp.zeros((DIM,), jnp.float32)
        g_o = jnp.ones((DIM,), jnp.float32)
        b_o = jnp.zeros((DIM,), jnp.float32)
        return {'x': x, 'latents': latents, 'mask': mask, 'g_x': g_x, 'b_x': b_x, 'g_l': g_l, 'b_l': b_l, 'Wq': Wq, 'Wkv': Wkv, 'Wout': Wout, 'g_o': g_o, 'b_o': b_o}
    _L2_xattn_all = _L2_xattn_setup()
    _L2_xattn_in = {k: v for k, v in _L2_xattn_all.items() if k in ('g_x', 'b_x', 'g_l', 'b_l', 'Wq', 'Wkv', 'Wout', 'g_o', 'b_o')}
    del _L2_xattn_all

    def _L2_ffn_setup():
        import jax, jax.numpy as jnp
        import numpy as np
        DIM = 256

        def _reference_tuple_inner(x, W_r, W_k, W_v, mu_r, mu_k):
            B, T, C = x.shape
            x_prev = jnp.concatenate([jnp.zeros((B, 1, C), x.dtype), x[:, :-1, :]], axis=1)
            xr = mu_r * x + (1.0 - mu_r) * x_prev
            xk = mu_k * x + (1.0 - mu_k) * x_prev
            r = jax.nn.sigmoid(jnp.einsum('btc,dc->btd', xr, W_r))
            k = jnp.einsum('btc,dc->btd', xk, W_k)
            k_act = jnp.square(jax.nn.relu(k))
            out = r * jnp.einsum('btc,dc->btd', k_act, W_v)
            new_state = x[:, -1, :]
            return (out, new_state)
        key = jax.random.key(seed)
        ks = jax.random.split(key, 6)
        B, T, C = (8, 512, DIM)
        x = jax.random.normal(ks[0], (B, T, C), dtype=jnp.float32)
        s = 1.0 / np.sqrt(C)
        W_r = jax.random.uniform(ks[1], (C, C), jnp.float32, -s, s)
        W_k = jax.random.uniform(ks[2], (C, C), jnp.float32, -s, s)
        W_v = jax.random.uniform(ks[3], (C, C), jnp.float32, -s, s)
        mu_r = jax.random.uniform(ks[4], (C,), jnp.float32)
        mu_k = jax.random.uniform(ks[5], (C,), jnp.float32)
        return {'x': x, 'W_r': W_r, 'W_k': W_k, 'W_v': W_v, 'mu_r': mu_r, 'mu_k': mu_k}
    _L2_ffn_all = _L2_ffn_setup()
    _L2_ffn_in = {k: v for k, v in _L2_ffn_all.items() if k in ('W_r', 'W_k', 'W_v', 'mu_r', 'mu_k')}
    del _L2_ffn_all

    def _L3_xattn_setup():
        import jax, jax.numpy as jnp
        import numpy as np
        D_MODEL = 256
        NUM_HEADS = 16
        DEPTH = D_MODEL // NUM_HEADS
        key = jax.random.key(seed)
        ks = jax.random.split(key, 6)
        B, S = (2, 512)
        scale = 1.0 / np.sqrt(D_MODEL)
        return {'q': jax.random.normal(ks[0], (B, S, D_MODEL), jnp.float32), 'k': jax.random.normal(ks[1], (B, S, D_MODEL), jnp.float32), 'v': jax.random.normal(ks[2], (B, S, D_MODEL), jnp.float32), 'wq': jax.random.normal(ks[3], (D_MODEL, D_MODEL), jnp.float32) * scale, 'wk': jax.random.normal(ks[4], (D_MODEL, D_MODEL), jnp.float32) * scale, 'wv': jax.random.normal(ks[5], (D_MODEL, D_MODEL), jnp.float32) * scale}
    _L3_xattn_all = _L3_xattn_setup()
    _L3_xattn_in = {k: v for k, v in _L3_xattn_all.items() if k in ('wq', 'wk', 'wv')}
    del _L3_xattn_all

    def _L3_ffn_setup():
        import jax, jax.numpy as jnp
        import numpy as np
        B, T, D, H, R, N = (16, 256, 256, 64, 64, 8)
        key = jax.random.key(seed)
        ks = jax.random.split(key, 8)
        s = lambda k, shape, fan: jax.random.normal(k, shape, jnp.float32) / np.sqrt(fan)
        return {'x': jax.random.normal(ks[0], (B, T, D), jnp.float32), 'W_base': s(ks[1], (D, D), D), 'b_base': jnp.zeros((D,), jnp.float32), 'W_enc': s(ks[2], (N, D, H), D), 'b_enc': jnp.zeros((N, H), jnp.float32), 'W_dec': s(ks[3], (N, H, D), H), 'b_dec': jnp.zeros((N, D), jnp.float32), 'W_down': s(ks[4], (N, D, R), D), 'b_down': jnp.zeros((N, R), jnp.float32), 'W_up': s(ks[5], (N, R, D), R), 'b_up': jnp.zeros((N, D), jnp.float32), 'connected_idx': jnp.arange(N, dtype=jnp.int32)}
    _L3_ffn_all = _L3_ffn_setup()
    _L3_ffn_in = {k: v for k, v in _L3_ffn_all.items() if k in ('W_base', 'b_base', 'W_enc', 'b_enc', 'W_dec', 'b_dec', 'W_down', 'b_down', 'W_up', 'b_up', 'connected_idx')}
    del _L3_ffn_all
    return {'x': x, 'ctx_1024': ctx_1024, 'mask_BxSxS2_bk1': mask_BxSxS2_bk1, 'mask_BxS2_bf1': mask_BxS2_bf1, 'g_xattn': g_xattn, 'g_ffn': g_ffn, 'L0_xattn_Wq': _L0_xattn_in['Wq'], 'L0_xattn_Wk': _L0_xattn_in['Wk'], 'L0_xattn_Wv': _L0_xattn_in['Wv'], 'L0_xattn_Wo': _L0_xattn_in['Wo'], 'L0_xattn_bo': _L0_xattn_in['bo'], 'L0_ffn_w_gate': _L0_ffn_in['w_gate'], 'L0_ffn_w_up': _L0_ffn_in['w_up'], 'L0_ffn_w_down': _L0_ffn_in['w_down'], 'L1_xattn_Wq1': _L1_xattn_in['Wq1'], 'L1_xattn_Wk1': _L1_xattn_in['Wk1'], 'L1_xattn_Wv1': _L1_xattn_in['Wv1'], 'L1_xattn_Wk2': _L1_xattn_in['Wk2'], 'L1_xattn_Wv2': _L1_xattn_in['Wv2'], 'L1_xattn_Wo': _L1_xattn_in['Wo'], 'L1_xattn_bo': _L1_xattn_in['bo'], 'L1_ffn_gate_w': _L1_ffn_in['gate_w'], 'L1_ffn_w1': _L1_ffn_in['w1'], 'L1_ffn_w3': _L1_ffn_in['w3'], 'L1_ffn_w2': _L1_ffn_in['w2'], 'L2_xattn_g_x': _L2_xattn_in['g_x'], 'L2_xattn_b_x': _L2_xattn_in['b_x'], 'L2_xattn_g_l': _L2_xattn_in['g_l'], 'L2_xattn_b_l': _L2_xattn_in['b_l'], 'L2_xattn_Wq': _L2_xattn_in['Wq'], 'L2_xattn_Wkv': _L2_xattn_in['Wkv'], 'L2_xattn_Wout': _L2_xattn_in['Wout'], 'L2_xattn_g_o': _L2_xattn_in['g_o'], 'L2_xattn_b_o': _L2_xattn_in['b_o'], 'L2_ffn_W_r': _L2_ffn_in['W_r'], 'L2_ffn_W_k': _L2_ffn_in['W_k'], 'L2_ffn_W_v': _L2_ffn_in['W_v'], 'L2_ffn_mu_r': _L2_ffn_in['mu_r'], 'L2_ffn_mu_k': _L2_ffn_in['mu_k'], 'L3_xattn_wq': _L3_xattn_in['wq'], 'L3_xattn_wk': _L3_xattn_in['wk'], 'L3_xattn_wv': _L3_xattn_in['wv'], 'L3_ffn_W_base': _L3_ffn_in['W_base'], 'L3_ffn_b_base': _L3_ffn_in['b_base'], 'L3_ffn_W_enc': _L3_ffn_in['W_enc'], 'L3_ffn_b_enc': _L3_ffn_in['b_enc'], 'L3_ffn_W_dec': _L3_ffn_in['W_dec'], 'L3_ffn_b_dec': _L3_ffn_in['b_dec'], 'L3_ffn_W_down': _L3_ffn_in['W_down'], 'L3_ffn_b_down': _L3_ffn_in['b_down'], 'L3_ffn_W_up': _L3_ffn_in['W_up'], 'L3_ffn_b_up': _L3_ffn_in['b_up'], 'L3_ffn_connected_idx': _L3_ffn_in['connected_idx']}

def reference(x, ctx_1024, mask_BxSxS2_bk1, mask_BxS2_bf1, g_xattn, g_ffn, L0_xattn_Wq, L0_xattn_Wk, L0_xattn_Wv, L0_xattn_Wo, L0_xattn_bo, L0_ffn_w_gate, L0_ffn_w_up, L0_ffn_w_down, L1_xattn_Wq1, L1_xattn_Wk1, L1_xattn_Wv1, L1_xattn_Wk2, L1_xattn_Wv2, L1_xattn_Wo, L1_xattn_bo, L1_ffn_gate_w, L1_ffn_w1, L1_ffn_w3, L1_ffn_w2, L2_xattn_g_x, L2_xattn_b_x, L2_xattn_g_l, L2_xattn_b_l, L2_xattn_Wq, L2_xattn_Wkv, L2_xattn_Wout, L2_xattn_g_o, L2_xattn_b_o, L2_ffn_W_r, L2_ffn_W_k, L2_ffn_W_v, L2_ffn_mu_r, L2_ffn_mu_k, L3_xattn_wq, L3_xattn_wk, L3_xattn_wv, L3_ffn_W_base, L3_ffn_b_base, L3_ffn_W_enc, L3_ffn_b_enc, L3_ffn_W_dec, L3_ffn_b_dec, L3_ffn_W_down, L3_ffn_b_down, L3_ffn_W_up, L3_ffn_b_up, L3_ffn_connected_idx):
    import jax
    import jax.numpy as jnp

    def _L0_xattn_ref(q, k, v, mask, Wq, Wk, Wv, Wo, bo):
        import jax, jax.numpy as jnp
        import numpy as np
        DIM = 256
        HEADS = 16
        DIM_HEAD = 64
        INNER = HEADS * DIM_HEAD
        B, N = (2, 512)
        h, d = (HEADS, DIM_HEAD)
        scale = d ** (-0.5)
        b, n, _ = q.shape

        def heads_split(x):
            return x.reshape(b, -1, h, d).transpose(0, 2, 1, 3)
        qh = heads_split(q @ Wq)
        kh = heads_split(k @ Wk)
        vh = heads_split(v @ Wv)
        dots = jnp.einsum('bhid,bhjd->bhij', qh, kh) * scale
        mask_value = -jnp.finfo(dots.dtype).max
        dots = jnp.where(mask[:, None, :, :], mask_value, dots)
        attn = jax.nn.softmax(dots, axis=-1)
        out = jnp.einsum('bhij,bhjd->bhid', attn, vh)
        out = out.transpose(0, 2, 1, 3).reshape(b, n, h * d)
        out = out @ Wo + bo
        return out

    def _L0_ffn_ref(x, w_gate, w_up, w_down):
        import jax, jax.numpy as jnp
        import numpy as np
        HIDDEN = 256
        INNER = 1024

        def _weight_quant(w):
            scale = 1.0 / jnp.clip(jnp.mean(jnp.abs(w)), 1e-05)
            wq = jnp.clip(jnp.round(w * scale), -1.0, 1.0) / scale
            return w + jax.lax.stop_gradient(wq - w)

        def _act_quant(x):
            scale = 127.0 / jnp.clip(jnp.max(jnp.abs(x), axis=-1, keepdims=True), 1e-05)
            xq = jnp.clip(jnp.round(x * scale), -128.0, 127.0) / scale
            return x + jax.lax.stop_gradient(xq - x)

        def _bitlinear(x, w):
            return jnp.einsum('bsi,oi->bso', _act_quant(x), _weight_quant(w))
        gate = jax.nn.silu(_bitlinear(x, w_gate))
        up = _bitlinear(x, w_up)
        return _bitlinear(gate * up, w_down)

    def _L1_xattn_ref(x1, x2, Wq1, Wk1, Wv1, Wk2, Wv2, Wo, bo):
        import jax, jax.numpy as jnp
        import numpy as np
        HEADS = 8
        DIM_HEAD = 64
        h, d = (HEADS, DIM_HEAD)
        scale = d ** (-0.5)
        B, N1, _ = x1.shape
        N2 = x2.shape[1]

        def split_heads(t, n):
            return t.reshape(B, n, h, d)
        q1 = split_heads(x1 @ Wq1, N1)
        k1 = split_heads(x1 @ Wk1, N1)
        v1 = split_heads(x1 @ Wv1, N1)
        k2 = split_heads(x2 @ Wk2, N2)
        v2 = split_heads(x2 @ Wv2, N2)
        k = jnp.concatenate([k1, k2], axis=1)
        v = jnp.concatenate([v1, v2], axis=1)
        sim = jnp.einsum('bihd,bjhd->bhij', q1.astype(jnp.float32), k.astype(jnp.float32)) * scale
        attn = jax.nn.softmax(sim, axis=-1)
        out = jnp.einsum('bhij,bjhd->bihd', attn, v)
        out = out.reshape(B, N1, h * d)
        return out @ Wo + bo

    def _L1_ffn_ref(hidden_states, gate_w, w1, w3, w2):
        import jax, jax.numpy as jnp
        import numpy as np
        N_EXPERTS = 16
        TOP_K = 4
        HIDDEN = 256
        INTER = 128
        B, S = (2, 256)
        'DeepseekV3 MoE adapter forward: router -> sparse scores -> expert GLU MLP -> combine.'
        b, s, h = hidden_states.shape
        x = hidden_states.reshape(-1, h)
        logits = jnp.einsum('th,eh->te', x, gate_w)
        probs = jax.nn.softmax(logits, axis=-1)
        topk_w, topk_idx = jax.lax.top_k(probs, TOP_K)
        topk_w = topk_w / jnp.sum(topk_w, axis=-1, keepdims=True)
        one_hot = (topk_idx[..., None] == jnp.arange(N_EXPERTS)).astype(topk_w.dtype)
        scores = jnp.einsum('tk,tke->te', topk_w, one_hot)
        g = jnp.einsum('th,ehi->tei', x, w1)
        u = jnp.einsum('th,ehi->tei', x, w3)
        act = jax.nn.silu(g) * u
        expert_out = jnp.einsum('tei,eih->teh', act, w2)
        out = jnp.einsum('teh,te->th', expert_out, scores)
        return out.reshape(b, s, h)

    def _L2_xattn_ref(x, latents, mask, g_x, b_x, g_l, b_l, Wq, Wkv, Wout, g_o, b_o):
        import jax, jax.numpy as jnp
        import numpy as np
        DIM = 256
        HEADS = 16
        DIM_HEAD = 64
        INNER = HEADS * DIM_HEAD
        EPS = 1e-05

        def layer_norm(x, gamma, beta):
            mu = jnp.mean(x, axis=-1, keepdims=True)
            var = jnp.var(x, axis=-1, keepdims=True)
            return (x - mu) * jax.lax.rsqrt(var + EPS) * gamma + beta
        scale = DIM_HEAD ** (-0.5)
        xn = layer_norm(x, g_x, b_x)
        ln = layer_norm(latents, g_l, b_l)
        b, m = (ln.shape[0], ln.shape[1])
        q = jnp.einsum('bnd,de->bne', ln, Wq)
        kv_in = jnp.concatenate([xn, ln], axis=1)
        kv = jnp.einsum('bnd,de->bne', kv_in, Wkv)
        k, v = jnp.split(kv, 2, axis=-1)

        def split_heads(t):
            return t.reshape(t.shape[0], t.shape[1], HEADS, DIM_HEAD).transpose(0, 2, 1, 3)
        q, k, v = (split_heads(q), split_heads(k), split_heads(v))
        q = q * scale
        sim = jnp.einsum('bhid,bhjd->bhij', q, k)
        full_mask = jnp.concatenate([mask, jnp.ones((b, m), dtype=bool)], axis=1)
        max_neg = -jnp.finfo(sim.dtype).max
        sim = jnp.where(full_mask[:, None, None, :], sim, max_neg)
        attn = jax.nn.softmax(sim, axis=-1)
        out = jnp.einsum('bhij,bhjd->bhid', attn, v)
        out = out.transpose(0, 2, 1, 3).reshape(b, m, INNER)
        out = jnp.einsum('bne,ed->bnd', out, Wout)
        return layer_norm(out, g_o, b_o)

    def _L2_ffn_ref(x, W_r, W_k, W_v, mu_r, mu_k):
        import jax, jax.numpy as jnp
        import numpy as np
        DIM = 256

        def _reference_tuple_inner(x, W_r, W_k, W_v, mu_r, mu_k):
            B, T, C = x.shape
            x_prev = jnp.concatenate([jnp.zeros((B, 1, C), x.dtype), x[:, :-1, :]], axis=1)
            xr = mu_r * x + (1.0 - mu_r) * x_prev
            xk = mu_k * x + (1.0 - mu_k) * x_prev
            r = jax.nn.sigmoid(jnp.einsum('btc,dc->btd', xr, W_r))
            k = jnp.einsum('btc,dc->btd', xk, W_k)
            k_act = jnp.square(jax.nn.relu(k))
            out = r * jnp.einsum('btc,dc->btd', k_act, W_v)
            new_state = x[:, -1, :]
            return (out, new_state)
        return _reference_tuple_inner(x, W_r, W_k, W_v, mu_r, mu_k)[0]

    def _L3_xattn_ref(q, k, v, wq, wk, wv):
        import jax, jax.numpy as jnp
        import numpy as np
        D_MODEL = 256
        NUM_HEADS = 16
        DEPTH = D_MODEL // NUM_HEADS
        B, S, _ = q.shape

        def split(x):
            return x.reshape(B, -1, NUM_HEADS, DEPTH).transpose(0, 2, 1, 3)
        Q = split(q @ wq.T)
        K = split(k @ wk.T)
        V = split(v @ wv.T)
        scores = jnp.einsum('bhqd,bhkd->bhqk', Q, K) / np.sqrt(DEPTH).astype(np.float32)
        attn = jax.nn.softmax(scores, axis=-1)
        out = jnp.einsum('bhqk,bhkd->bhqd', attn, V)
        return out.transpose(0, 2, 1, 3).reshape(B, S, D_MODEL)

    def _L3_ffn_ref(x, W_base, b_base, W_enc, b_enc, W_dec, b_dec, W_down, b_down, W_up, b_up, connected_idx):
        import jax, jax.numpy as jnp
        import numpy as np
        B, T, D, H, R, N = (16, 256, 256, 64, 64, 8)
        base = jnp.einsum('btd,de->bte', x, W_base) + b_base
        h = jax.nn.relu(jnp.einsum('btd,ndh->nbth', x, W_enc) + b_enc[:, None, None, :])
        recon = jnp.einsum('nbth,nhd->nbtd', h, W_dec) + b_dec[:, None, None, :]
        losses = jnp.mean((recon - x[None]) ** 2, axis=(2, 3))
        top1 = jnp.argmin(losses, axis=0)
        adp = connected_idx[top1]
        Wd, bd = (W_down[adp], b_down[adp])
        Wu, bu = (W_up[adp], b_up[adp])
        mid = jax.nn.relu(jnp.einsum('btd,bdr->btr', x, Wd) + bd[:, None, :])
        adapter_out = jnp.einsum('btr,brd->btd', mid, Wu) + bu[:, None, :]
        return base + adapter_out
    x = x + jnp.tanh(g_xattn[0]) * _L0_xattn_ref(_layernorm(x, axis=-1), ctx_1024, ctx_1024, mask_BxSxS2_bk1, L0_xattn_Wq, L0_xattn_Wk, L0_xattn_Wv, L0_xattn_Wo, L0_xattn_bo)
    x = x + jnp.tanh(g_ffn[0]) * _L0_ffn_ref(_layernorm(x, axis=-1), L0_ffn_w_gate, L0_ffn_w_up, L0_ffn_w_down)
    x = x + jnp.tanh(g_xattn[1]) * _L1_xattn_ref(_layernorm(x, axis=-1), ctx_1024, L1_xattn_Wq1, L1_xattn_Wk1, L1_xattn_Wv1, L1_xattn_Wk2, L1_xattn_Wv2, L1_xattn_Wo, L1_xattn_bo)
    x = x + jnp.tanh(g_ffn[1]) * _L1_ffn_ref(_layernorm(x, axis=-1), L1_ffn_gate_w, L1_ffn_w1, L1_ffn_w3, L1_ffn_w2)
    x = x + jnp.tanh(g_xattn[2]) * _L2_xattn_ref(ctx_1024, _layernorm(x, axis=-1), mask_BxS2_bf1, L2_xattn_g_x, L2_xattn_b_x, L2_xattn_g_l, L2_xattn_b_l, L2_xattn_Wq, L2_xattn_Wkv, L2_xattn_Wout, L2_xattn_g_o, L2_xattn_b_o)
    x = x + jnp.tanh(g_ffn[2]) * _L2_ffn_ref(_layernorm(x, axis=-1), L2_ffn_W_r, L2_ffn_W_k, L2_ffn_W_v, L2_ffn_mu_r, L2_ffn_mu_k)
    x = x + jnp.tanh(g_xattn[3]) * _L3_xattn_ref(_layernorm(x, axis=-1), ctx_1024, ctx_1024, L3_xattn_wq, L3_xattn_wk, L3_xattn_wv)
    x = x + jnp.tanh(g_ffn[3]) * _L3_ffn_ref(_layernorm(x, axis=-1), L3_ffn_W_base, L3_ffn_b_base, L3_ffn_W_enc, L3_ffn_b_enc, L3_ffn_W_dec, L3_ffn_b_dec, L3_ffn_W_down, L3_ffn_b_down, L3_ffn_W_up, L3_ffn_b_up, L3_ffn_connected_idx)
    return x

_drawn_inputs = setup_inputs


def setup_inputs(seed=0):
    import zlib

    import numpy as np

    out = dict(_drawn_inputs(seed))
    spreads = {'L0_xattn_bo': (0.0, 0.1),
     'L1_xattn_bo': (0.0, 0.1),
     'L2_xattn_g_x': (1.0, 0.589),
     'L2_xattn_b_x': (0.0, 1.135),
     'L2_xattn_g_l': (1.0, 0.6),
     'L2_xattn_b_l': (0.0, 0.1),
     'L2_xattn_g_o': (1.0, 0.577),
     'L2_xattn_b_o': (0.0, 0.568),
     'L3_ffn_b_base': (0.0, 0.488),
     'L3_ffn_b_enc': (0.0, 0.1),
     'L3_ffn_b_dec': (0.0, 0.1),
     'L3_ffn_b_down': (0.0, 0.792),
     'L3_ffn_b_up': (0.0, 0.523)}
    factors = {'L0_xattn_Wq': 8.0,
     'L0_xattn_Wk': 8.0,
     'L1_xattn_Wk2': 2.753,
     'L1_ffn_gate_w': 8.0,
     'L1_ffn_w1': 8.0,
     'L1_ffn_w3': 8.0,
     'L1_ffn_w2': 8.0,
     'L2_ffn_W_r': 4.634,
     'L2_ffn_mu_r': 8.0,
     'L2_ffn_mu_k': 2.669,
     'L2_xattn_Wq': 4.399}
    for name, (base, spread) in spreads.items():
        noise = np.random.default_rng([zlib.crc32(name.encode()), seed]).standard_normal(out[name].shape)
        drawn = base * np.exp(spread * noise) if base else spread * noise
        out[name] = jnp.asarray(drawn.astype(out[name].dtype))
    for name, factor in factors.items():
        out[name] = (out[name] * factor).astype(out[name].dtype)
    return out
```

```python
from contextlib import ExitStack, contextmanager

import concourse.bass as bass
from concourse import mybir

ALU = mybir.AluOpType
ACT = mybir.ActivationFunctionType
AX = mybir.AxisListType
F32 = mybir.dt.float32
F32R = mybir.dt.float32r
BF16 = mybir.dt.bfloat16
I32 = mybir.dt.int32
U8 = mybir.dt.uint8

P = 128
NB = 2
N = 1024
D = 256
DC = D // P
TT = N // P
HALF = 512
NHALF = N // HALF
J = 77
JP = J + 1
HEADS = 16
HJ = HEADS * JP
HJC = -(-HJ // P)
BANK_HEADS = [(0, 6), (6, 11), (11, 16)]
KEYS = N + J
KEYSP = N + JP
KC = TT + 1
DH = 64
EPS = 1e-5
MAGIC = 12582912.0
RSQRT_SEED = 1597463007.0
NEWTON = 3
MASK_PART = 2.0 ** 120
NEG_MAX = -3.4028234663852886e38
STAT_STEPS = 4 + 3 * NEWTON + 1
EXPERTS = 16
TOP_K = 4
INTER = 128
EG = 4
AE = 8
AH = 64
INNER = 1024
LAYERS = 4


class Chain:

    def __init__(self, eng, sem):
        self.eng, self.sem, self.n = eng, sem, 0

    def step(self, ins):
        ins.then_inc(self.sem, 1)
        self.n += 1

    def settle(self):
        self.eng.wait_ge(self.sem, self.n)


def flamingo_kernel(nc, A, out):
    with ExitStack() as life:
        def sb(name, shape, dt=F32):
            return scope.enter_context(nc.sbuf_tensor(name, shape, dt))

        sem_scope = ExitStack()
        layer_signals = []

        def semaphore(name):
            return sem_scope.enter_context(nc.semaphore(name))

        def signal(name):
            s = semaphore(name)
            layer_signals.append(s)
            return s

        @contextmanager
        def buffers():
            nonlocal scope
            with ExitStack() as scope:
                yield
            scope = life

        scope = life
        X = sb("X", [P, TT, D])
        XN = sb("XN", [P, TT, D])
        XTh = sb("XTh", [P, DC, N], F32R)
        XTl = sb("XTl", [P, DC, N], F32R)
        C = sb("C", [P, D])
        CN = sb("CN", [P, D])
        CTh = sb("CTh", [P, DC, JP], F32R)
        CTl = sb("CTl", [P, DC, JP], F32R)
        CNT = sb("CNT", [P, DC, JP])
        CNTh = sb("CNTh", [P, DC, JP], F32R)
        CNTl = sb("CNTl", [P, DC, JP], F32R)
        ident = sb("ident", [P, P])
        identb = sb("identb", [P, P], BF16)
        ones = sb("ones", [P, P])
        gates = sb("gates", [P, 2 * LAYERS])
        tg = sb("tg", [P, 2 * LAYERS])
        stats = sb("stats", [P, TT, 6])
        mv = sb("mv", [P, TT, 2])
        var = sb("var", [P, TT])
        rstd = sb("rstd", [P, TT])
        ntmp = sb("ntmp", [P, TT])
        nmr = sb("nmr", [P, TT])
        gl = sb("gl", [P, DC, 4])
        mus = sb("mus", [P, DC, 2])
        htg2 = sb("half_gate2", [P, 1])
        omm = sb("omm", [P, DC, 2])
        benc = sb("b_enc_cols", [P, AE // 2])
        bdec = sb("b_dec_cols", [P, AE, DC])
        bdown = sb("b_down_cols", [P, AE])
        cidx_i = sb("connected_i", [P, AE], I32)
        cidx = sb("connected", [P, AE])
        rowb = sb("rowb", [P, 6, D])
        BO0, BO1, GO, BO, BBASE, SPARE = range(6)

        wq = [sb(f"ternary{n}", [P, DC * INNER], BF16) for n in range(3)]
        wabs = sb("weight_abs_sums", [P, 3])
        wmean = sb("weight_mean", [P, 3])
        winv = sb("weight_inv_mean", [P, 3])

        PA = life.enter_context(nc.psum_tensor("PA", [P, 3 * HALF], F32))
        PB = life.enter_context(nc.psum_tensor("PB", [P, 3 * HALF], F32))
        PT = life.enter_context(nc.psum_tensor("PT", [P, HALF], F32))
        PV = life.enter_context(nc.psum_tensor("PV", [P, HALF], F32))
        BANKS = [PA[:, 0:512], PA[:, 512:1024], PA[:, 1024:1536],
                 PB[:, 0:512], PB[:, 512:1024], PB[:, 1024:1536], PT[:, :], PV[:, :]]

        LAYER_STAGES = [["load", "ln0x", "prep0", "attn0", "ln0f", "bitq", "bit"],
                        ["ln1x", "attn1", "ln1f", "router", "moe"],
                        ["ln2x", "attn2", "out2", "ln2f", "rwkv"],
                        ["ln3x", "prep3", "attn3", "ln3f", "route", "adapt"]]
        LAYER_STAGES.append(["store"])
        ends = {k: life.enter_context(nc.semaphore(f"{k}_stage_end")) for k in ("pe", "act", "dve", "pool", "sp")}

        def turn_signals(name):
            return (semaphore(f"{name}_arrived"), {k: semaphore(f"{name}_go_{k}") for k in ends if k != "pool"})

        def end_turn(eng, me, turn, signals):
            arrived, go = turn
            eng.drain().then_inc(arrived, 1)
            if me == "pool":
                eng.wait_ge(arrived, len(ends))
                for s in (*signals, arrived):
                    eng.sem_clear(s)
                for k in go:
                    eng.sem_inc(go[k], 1)
            else:
                eng.wait_ge(go[me], 1)
                eng.sem_clear(go[me])

        layer_turn = (life.enter_context(nc.semaphore("layer_arrived")),
                      {k: life.enter_context(nc.semaphore(f"layer_go_{k}")) for k in ends if k != "pool"})
        signals_of = []

        def next_layer():
            nonlocal sem_scope, layer_signals
            signals_of.append(layer_signals + list(ends.values()))
            sem_scope.close()
            sem_scope, layer_signals = ExitStack(), []

        def run(eng, me, b, parts):
            for stages, signals in zip(LAYER_STAGES, signals_of[:len(LAYER_STAGES) - 1] + signals_of[-1:]):
                for s, name in enumerate(stages):
                    if s:
                        for other in ends:
                            if other != me:
                                eng.wait_ge(ends[other], s)
                    if name in parts:
                        parts[name](eng, b)
                    eng.drain().then_inc(ends[me], 1)
                end_turn(eng, me, layer_turn, signals)

        pe_parts, act_parts, dve_parts, pool_parts, sp_parts = {}, {}, {}, {}, {}

        def part(table, name):
            def keep(f):
                table[name] = f
                return f
            return keep

        def mm3(pe, acc, lh, ll, rh, rl, first, last):
            pe.matmul(acc, lh, rh, start=first, stop=False)
            pe.matmul(acc, ll, rh, start=False, stop=False)
            return pe.matmul(acc, lh, rl, start=False, stop=last)

        const_dma = life.enter_context(nc.semaphore("const_loaded"))
        const_set = life.enter_context(nc.semaphore("const_set"))
        omm_set = life.enter_context(nc.semaphore("omm_set"))
        tg_set = life.enter_context(nc.semaphore("tg_set"))

        def col(ap):
            return ap.rearrange("(c p) -> p c", p=P)

        const_loads = [
            (gates[:, 0:LAYERS], A["g_xattn"].rearrange("(a n) -> a n", a=1).broadcast_to([P, LAYERS])),
            (gates[:, LAYERS:], A["g_ffn"].rearrange("(a n) -> a n", a=1).broadcast_to([P, LAYERS])),
            (gl[:, :, 0], col(A["L2_xattn_g_x"])), (gl[:, :, 1], col(A["L2_xattn_b_x"])),
            (gl[:, :, 2], col(A["L2_xattn_g_l"])), (gl[:, :, 3], col(A["L2_xattn_b_l"])),
            (mus[:, :, 0], col(A["L2_ffn_mu_r"])), (mus[:, :, 1], col(A["L2_ffn_mu_k"])),
            (cidx_i[:], A["L3_ffn_connected_idx"].rearrange("(a n) -> a n", a=1).broadcast_to([P, AE])),
        ] + [(benc[r * AH:(r + 1) * AH, :], A["L3_ffn_b_enc"].rearrange("(k r) h -> r h k", r=2)[r])
             for r in range(2)
        ] + [(bdec[:, :, c], A["L3_ffn_b_dec"].rearrange("n (c p) -> c p n", p=P)[c]) for c in range(DC)
        ] + [(bdown[r * AH:(r + 1) * AH, :], A["L3_ffn_b_down"].rearrange("n h -> h n")) for r in range(2)
        ] + [(rowb[:, k, :], A[name].rearrange("(a n) -> a n", a=1).broadcast_to([P, D]))
             for k, name in ((BO0, "L0_xattn_bo"), (BO1, "L1_xattn_bo"), (GO, "L2_xattn_g_o"),
                             (BO, "L2_xattn_b_o"), (BBASE, "L3_ffn_b_base"))]

        def sp_consts(sp):
            for dst, src in const_loads:
                sp.dma_start(dst, src, allow_slow_non_contiguous=True).then_inc(const_dma, 16)

        def pool_consts(pool):
            pool.memset(ident[:], 0.0).then_inc(const_set, 1)
            pool.memset(ones[:], 1.0).then_inc(const_set, 1)
            pool.memset(C[:], 0.0).then_inc(const_set, 1)
            pool.memset(CN[:], 0.0).then_inc(const_set, 1)
            pool.memset(CNT[:], 0.0).then_inc(const_set, 1)
            pool.wait_ge(const_set, 5)
            pool.affine_select(out=ident[:], in_=ident[:], compare_op=ALU.not_equal, fill=1.0, base=0,
                               pattern=[[-1, P]], channel_multiplier=1).then_inc(const_set, 1)
            pool.wait_ge(const_set, 6)
            pool.tensor_copy(identb[:], ident[:]).then_inc(const_set, 1)

        def act_consts(act):
            act.wait_ge(const_dma, 16 * len(const_loads))
            act.activation(tg[:], gates[:], ACT.Tanh).then_inc(tg_set, 1)

        def dve_consts(dve):
            dve.wait_ge(const_dma, 16 * len(const_loads))
            dve.tensor_scalar(omm[:], mus[:], -1.0, 1.0, ALU.mult, ALU.add).then_inc(omm_set, 1)
            dve.wait_ge(tg_set, 1)
            dve.tensor_scalar(htg2[:], tg[:, LAYERS + 2:LAYERS + 3], 0.5, None, ALU.mult).then_inc(omm_set, 1)
            dve.tensor_copy(cidx[:], cidx_i[:]).then_inc(omm_set, 1)
            for k, g in ((BO0, 0), (BO1, 1), (GO, 2), (BO, 2)):
                dve.tensor_scalar(rowb[:, k, :], rowb[:, k, :], tg[:, g:g + 1], None,
                                  ALU.mult).then_inc(omm_set, 1)

        load_x = signal("x_loaded")
        load_c = signal("ctx_loaded")
        CTX_STEPS = STAT_STEPS + 1
        ctx_chain = signal("ctx_norm_steps")
        ctx_ps = signal("ctx_transposed")
        ctx_hi = signal("ctx_hi")
        ctx_lo = signal("ctx_lo")

        def norm_stats(dve, chain, src, tiles, rows=P):
            for t in range(tiles):
                ins = dve.bn_stats(stats[0:rows, t, :], src(t))
            chain.step(ins)
            chain.settle()
            for t in range(tiles):
                ins = dve.bn_aggr(mv[0:rows, t, :], stats[0:rows, t, :])
            chain.step(ins)
            chain.settle()
            v, y, w = var[0:rows, 0:tiles], rstd[0:rows, 0:tiles], ntmp[0:rows, 0:tiles]
            chain.step(dve.tensor_scalar(v, mv[0:rows, 0:tiles, 1], EPS, None, ALU.add))
            chain.settle()
            chain.step(dve.tensor_scalar(y.bitcast(I32), v.bitcast(I32), -0.5, RSQRT_SEED, ALU.mult, ALU.add))
            chain.settle()
            for _ in range(NEWTON):
                chain.step(dve.tensor_tensor(w, y, y, ALU.mult))
                chain.settle()
                chain.step(dve.scalar_tensor_tensor(w, w, -0.5, v, ALU.mult, ALU.mult))
                chain.settle()
                chain.step(dve.scalar_tensor_tensor(y, w, 1.5, y, ALU.add, ALU.mult))
                chain.settle()
            chain.step(dve.scalar_tensor_tensor(nmr[0:rows, 0:tiles], mv[0:rows, 0:tiles, 0], -1.0, y,
                                                ALU.mult, ALU.mult))
            chain.settle()

        @part(sp_parts, "load")
        def _(sp, b):
            sp.dma_start(X[:], A["x"][bass.ds(b * N, N), :].rearrange("(t p) d -> p t d", p=P)
                         ).then_inc(load_x, 16)
            sp.dma_start(C[0:J, :], A["ctx_1024"][bass.ds(b * J, J), :]).then_inc(load_c, 16)
            sp.wait_ge(load_x, 16)

        @part(dve_parts, "load")
        def _(dve, b):
            dve.wait_ge(load_c, 16)
            chain = Chain(dve, ctx_chain)
            norm_stats(dve, chain, lambda t: C[0:J, :], 1, J)
            chain.step(dve.tensor_scalar(CN[0:J, :], C[0:J, :], rstd[0:J, 0:1], nmr[0:J, 0:1], ALU.mult, ALU.add))
            dve.wait_ge(ctx_hi, 1)
            dve.tensor_tensor(CTl[:, :, :], PA[:, 0:DC * JP].rearrange("p (c j) -> p c j", c=DC),
                              CTh[:, :, :].bitcast(F32), ALU.subtract).then_inc(ctx_lo, 1)
            dve.wait_ge(ctx_hi, 3)
            dve.tensor_tensor(CNTl[:, :, :], CNT[:, :, :], CNTh[:, :, :].bitcast(F32),
                              ALU.subtract).then_inc(ctx_lo, 1)

        @part(pe_parts, "load")
        def _(pe, b):
            pe.wait_ge(load_c, 16)
            for c in range(DC):
                ins = pe.transpose(PA[:, c * JP:(c + 1) * JP], C[0:JP, c * P:(c + 1) * P], ident[0:JP, 0:JP])
            ins.then_inc(ctx_ps, 1)
            pe.wait_ge(ctx_chain, CTX_STEPS)
            for c in range(DC):
                ins = pe.transpose(PB[:, c * JP:(c + 1) * JP], CN[0:JP, c * P:(c + 1) * P], ident[0:JP, 0:JP])
            ins.then_inc(ctx_ps, 1)

        @part(act_parts, "load")
        def _(act, b):
            act.wait_ge(ctx_ps, 1)
            act.activation(CTh[:, :, :], PA[:, 0:DC * JP].rearrange("p (c j) -> p c j", c=DC),
                           ACT.Copy).then_inc(ctx_hi, 1)
            act.wait_ge(ctx_ps, 2)
            for c in range(DC):
                ins = act.activation(CNT[:, c, 0:J], PB[:, c * JP:c * JP + J], ACT.Identity,
                                     scale=gl[:, c, 0:1], bias=gl[:, c, 1:2])
            ins.then_inc(ctx_hi, 1)
            act.wait_ge(ctx_hi, 2)
            act.activation(CNTh[:, :, :], CNT[:, :, :], ACT.Copy).then_inc(ctx_hi, 1)

        QUADS = [(c, h) for c in range(DC) for h in range(NHALF)]
        LN_STEPS = STAT_STEPS + 1

        def apply_norm(dve, chain, src):
            for t in range(TT):
                ins = dve.tensor_scalar(XN[:, t, :], src[:, t, :], rstd[:, t:t + 1], nmr[:, t:t + 1],
                                        ALU.mult, ALU.add)
            chain.step(ins)

        def ln_stage(name, feature_major=True, XF=None, gamma=None):
            steps = LN_STEPS * (2 if gamma is not None else 1)
            chain_of = signal(name + "_steps")
            ps = signal(name + "_transposed")
            full = signal(name + "_full") if XF is not None else None
            hi = signal(name + "_hi")
            lo = signal(name + "_lo")

            @part(dve_parts, name)
            def _(dve, b):
                chain = Chain(dve, chain_of)
                norm_stats(dve, chain, lambda t: X[:, t, :], TT)
                apply_norm(dve, chain, X)
                if gamma is not None:
                    chain.settle()
                    norm_stats(dve, chain, lambda t: XN[:, t, :], TT)
                    apply_norm(dve, chain, XN)
                if feature_major:
                    for q, (c, h) in enumerate(QUADS):
                        cols = slice(h * HALF, (h + 1) * HALF)
                        dve.wait_ge(hi, q + 1)
                        dve.tensor_tensor(XTl[:, c, cols], BANKS[q] if XF is None else XF[:, c, cols],
                                          XTh[:, c, cols].bitcast(F32), ALU.subtract).then_inc(lo, 1)

            if not feature_major:
                return

            @part(pe_parts, name)
            def _(pe, b):
                pe.wait_ge(chain_of, steps)
                for q, (c, h) in enumerate(QUADS):
                    for i in range(4):
                        ins = pe.transpose(BANKS[q][:, i * P:(i + 1) * P],
                                           XN[:, 4 * h + i, c * P:(c + 1) * P], ident[:])
                    ins.then_inc(ps, 1)

            @part(act_parts, name)
            def _(act, b):
                for q, (c, h) in enumerate(QUADS):
                    cols = slice(h * HALF, (h + 1) * HALF)
                    act.wait_ge(ps, q + 1)
                    src = BANKS[q]
                    if XF is not None:
                        if gamma is not None:
                            ins = act.activation(XF[:, c, cols], src, ACT.Identity,
                                                 scale=gl[:, c, gamma:gamma + 1],
                                                 bias=gl[:, c, gamma + 1:gamma + 2])
                        else:
                            ins = act.activation(XF[:, c, cols], src, ACT.Copy)
                        ins.then_inc(full, 1)
                        act.wait_ge(full, q + 1)
                        src = XF[:, c, cols]
                    act.activation(XTh[:, c, cols], src, ACT.Copy).then_inc(hi, 1)

        def context_attention(k, group_heads, weights, scale, gate, masked, bias_row):
            prep, main = f"prep{k}", f"attn{k}"
            groups = HEADS // group_heads
            w = group_heads * JP
            segs = [(0, w)] if w <= HALF else [(0, w // 2), (w // 2, w)]
            n_parts = len(weights)
            AHi = sb(f"scores_w_hi{k}", [P, DC, HJ], F32R)
            ALo = sb(f"scores_w_lo{k}", [P, DC, HJ], F32R)
            VWh = sb(f"out_w_hi{k}", [P, HJC, D], F32R)
            VWl = sb(f"out_w_lo{k}", [P, HJC, D], F32R)
            with buffers():
                heads_of_rows = sb(f"head_mask{k}", [P, group_heads])
                raw = sb(f"prep_raw{k}", [P, n_parts, D])
                wh = sb(f"prep_wh{k}", [P, n_parts, D], F32R)
                wl = sb(f"prep_wl{k}", [P, n_parts, D], F32R)
                KB = sb(f"k_blocks{k}", [P, group_heads, JP])
                VB = sb(f"v_blocks{k}", [P, group_heads, JP])
                KBh = sb(f"k_blocks_hi{k}", [P, w], F32R)
                KBl = sb(f"k_blocks_lo{k}", [P, w], F32R)
                VBh = sb(f"v_blocks_hi{k}", [P, w], F32R)
                VBl = sb(f"v_blocks_lo{k}", [P, w], F32R)
                VWT = sb(f"out_w_t{k}", [P, DC, HJC * P])
            KBv, VBv = KB[:, :, :].rearrange("p h j -> p (h j)"), VB[:, :, :].rearrange("p h j -> p (h j)")
            has_wo = n_parts == 4
            raw_in = signal(prep + "_weights_in")
            mask_steps = signal(prep + "_mask_steps")
            split = signal(prep + "_weights_split")
            kv_ps = signal(prep + "_kv_ready")
            blocks = signal(prep + "_blocks")
            blocks_hi = signal(prep + "_blocks_hi")
            blocks_lo = signal(prep + "_blocks_lo")
            a_ps = signal(prep + "_products")
            a_hi = signal(prep + "_products_hi")
            a_lo = signal(prep + "_products_lo")
            vw_ps = signal(prep + "_vw_transposed")
            vw_hi = signal(prep + "_vw_hi")
            vw_lo = signal(prep + "_vw_lo")

            a_bank = {(c, s): [BANKS[0], BANKS[1], BANKS[3], BANKS[4]][c * len(segs) + s]
                      for c in range(DC) for s in range(len(segs))}
            v_bank = [BANKS[3], BANKS[4]]

            def group_loop(eng, body):
                for g in range(groups):
                    body(g)

            def cols(tensor, c, g, s0, s1):
                return tensor[:, c, g * w + s0:g * w + s1]

            @part(sp_parts, prep)
            def _(sp, b):
                def body(g):
                    if g:
                        sp.wait_ge(split, g * 2)
                    for i, source in enumerate(weights):
                        dst, src = source(raw, i, g)
                        sp.dma_start(dst, src).then_inc(raw_in, 16)
                group_loop(sp, body)

            @part(pool_parts, prep)
            def _(pool, b):
                m = heads_of_rows[:]
                rows = P // group_heads
                pool.memset(m, 1.0).then_inc(mask_steps, 1)
                pool.memset(VWT[:], 0.0).then_inc(mask_steps, 1)
                pool.wait_ge(mask_steps, 2)
                pool.affine_select(out=m, in_=m, compare_op=ALU.is_ge, fill=0.0, base=0,
                                   pattern=[[-rows, group_heads]], channel_multiplier=1
                                   ).then_inc(mask_steps, 1)
                pool.wait_ge(mask_steps, 3)
                pool.affine_select(out=m, in_=m, compare_op=ALU.is_ge, fill=0.0, base=rows - 1,
                                   pattern=[[rows, group_heads]], channel_multiplier=-1
                                   ).then_inc(mask_steps, 1)

                def body(g):
                    pool.wait_ge(raw_in, (g + 1) * (16 * n_parts))
                    if g:
                        pool.wait_ge(a_ps, g)
                    pool.tensor_scalar(wh[:], raw[:], 1.0, 0.0, ALU.mult, ALU.add).then_inc(split, 1)
                    pool.wait_ge(split, g * 2 + 1)
                    pool.tensor_tensor(wl[:], raw[:], wh[:].bitcast(F32), ALU.subtract).then_inc(split, 1)
                group_loop(pool, body)

            @part(pe_parts, prep)
            def _(pe, b):
                def body(g):
                    pe.wait_ge(split, g * 2 + 2)
                    if g:
                        pe.wait_ge(blocks, g * 2)
                    for i, col0 in ((0, 0), (1, P)):
                        for c in range(DC):
                            e = slice(c * P, (c + 1) * P)
                            ins = mm3(pe, PT[:, col0:col0 + JP], wh[:, i, e], wl[:, i, e],
                                      CTh[:, c, :], CTl[:, c, :], c == 0, c == DC - 1)
                    ins.then_inc(kv_ps, 1)
                    pe.wait_ge(blocks_lo, g * 2 + 2)
                    if g:
                        pe.wait_ge(a_lo, g)
                    for c in range(DC):
                        e = slice(c * P, (c + 1) * P)
                        for s, (s0, s1) in enumerate(segs):
                            ins = mm3(pe, a_bank[c, s][:, 0:s1 - s0], wh[:, 2, e], wl[:, 2, e],
                                      KBh[:, s0:s1], KBl[:, s0:s1], True, True)
                        if has_wo:
                            ins = mm3(pe, [BANKS[2], BANKS[5]][c][:, 0:w], wh[:, 3, e], wl[:, 3, e],
                                      VBh[:], VBl[:], True, True)
                    ins.then_inc(a_ps, 1)
                group_loop(pe, body)
                if has_wo:
                    pe.wait_ge(a_lo, groups)
                pe.wait_ge(a_hi, groups)
                pe.wait_ge(a_lo, groups)
                for n in range(HJC // 2):
                    for i in range(2):
                        for c in range(DC):
                            col0 = i * D + c * P
                            ins = pe.transpose(BANKS[n][:, col0:col0 + P],
                                               VWT[:, c, (2 * n + i) * P:(2 * n + i + 1) * P], ident[:])
                    ins.then_inc(vw_ps, 1)

            @part(dve_parts, prep)
            def _(dve, b):
                dve.wait_ge(mask_steps, 4)
                own = heads_of_rows[:, :].unsqueeze(2).broadcast_to([P, group_heads, JP])

                def body(g):
                    dve.wait_ge(kv_ps, g + 1)
                    if g:
                        dve.wait_ge(blocks_hi, g * 2)
                    if g:
                        dve.wait_ge(blocks_lo, g * 2)
                    for blk, col0 in ((KB, 0), (VB, P)):
                        dve.tensor_tensor(blk[:], PT[:, col0:col0 + JP].unsqueeze(1).broadcast_to(
                            [P, group_heads, JP]), own, ALU.mult).then_inc(blocks, 1)
                    for n, (lo, full, hi_) in enumerate(((KBl, KBv, KBh), (VBl, VBv, VBh))):
                        dve.wait_ge(blocks_hi, g * 2 + n + 1)
                        dve.tensor_tensor(lo[:], full, hi_[:].bitcast(F32), ALU.subtract
                                          ).then_inc(blocks_lo, 1)
                    dve.wait_ge(a_hi, g + 1)
                    for c in range(DC):
                        for s, (s0, s1) in enumerate(segs):
                            ins = dve.tensor_tensor(cols(ALo, c, g, s0, s1), a_bank[c, s][:, 0:s1 - s0],
                                                    cols(AHi, c, g, s0, s1).bitcast(F32), ALU.subtract)
                    ins.then_inc(a_lo, 1)
                group_loop(dve, body)
                for n in range(HJC // 2):
                    dve.wait_ge(vw_hi, n + 1)
                    dve.tensor_tensor(VWl[:, 2 * n:2 * n + 2, :], BANKS[n].rearrange("p (i d) -> p i d", i=2),
                                      VWh[:, 2 * n:2 * n + 2, :].bitcast(F32), ALU.subtract
                                      ).then_inc(vw_lo, 1)

            @part(act_parts, prep)
            def _(act, b):
                act.wait_ge(mask_steps, 2)

                def body(g):
                    if g:
                        act.wait_ge(a_ps, g)
                    for n, (hi_, full) in enumerate(((KBh, KBv), (VBh, VBv))):
                        act.wait_ge(blocks, g * 2 + n + 1)
                        act.activation(hi_[:], full, ACT.Copy).then_inc(blocks_hi, 1)
                    if not has_wo:
                        act.activation(cols(VWT, g, g, 0, w), VBv, ACT.Copy)
                    act.wait_ge(a_ps, g + 1)
                    for c in range(DC):
                        for s, (s0, s1) in enumerate(segs):
                            ins = act.activation(cols(AHi, c, g, s0, s1), a_bank[c, s][:, 0:s1 - s0], ACT.Copy)
                        if has_wo:
                            ins = act.activation(cols(VWT, c, g, 0, w), [BANKS[2], BANKS[5]][c][:, 0:w], ACT.Copy)
                    ins.then_inc(a_hi, 1)
                group_loop(act, body)
                for n in range(HJC // 2):
                    act.wait_ge(vw_ps, n + 1)
                    act.activation(VWh[:, 2 * n:2 * n + 2, :], BANKS[n].rearrange("p (i d) -> p i d", i=2),
                                   ACT.Copy).then_inc(vw_hi, 1)

            NP = 3
            with buffers():
                SB = [sb(f"scores{k}_{i}", [P, HEADS, JP]) for i in range(2)]
                PR = [sb(f"probs{k}_{i}", [P, HJC * P]) for i in range(NP)]
                PTh = [sb(f"probs_t_hi{k}_{i}", [P, HJC, P], F32R) for i in range(2)]
                PTl = [sb(f"probs_t_lo{k}_{i}", [P, HJC, P], F32R) for i in range(2)]
                mx = sb(f"row_max{k}", [P, 2, HEADS])
                sm = sb(f"row_sum{k}", [P, NP, HEADS])
                rs = sb(f"row_inv{k}", [P, NP, HEADS])
                mask8 = sb(f"mask_bytes{k}", [P, TT, J], U8) if masked else None
                mneg = sb(f"mask_add{k}", [P, TT, J]) if masked else None
            PRv = [p_[:, 0:HJ].rearrange("p (h j) -> p h j", h=HEADS) for p_ in PR]
            SPS = [PA, PB]
            ROUNDS = [(0, 4), (4, 8), (8, HJC)]
            mask_in = signal(main + "_mask_in")
            mask_done = signal(main + "_mask_ready")
            cleared = signal(main + "_probs_cleared")
            biased = signal(main + "_bias_added")
            s_ps = signal(main + "_scores_ready")
            s_out = signal(main + "_scores_copied")
            mx_done = signal(main + "_max")
            sub_done = signal(main + "_shifted")
            ex_done = signal(main + "_exp")
            sum_done = signal(main + "_sum")
            inv_done = signal(main + "_inv")
            p_done = signal(main + "_probs_ready")
            t_ps = signal(main + "_probs_transposed")
            t_hi = signal(main + "_probs_t_hi")
            t_lo = signal(main + "_probs_t_lo")
            o_ps = signal(main + "_out_ready")
            x_done = signal(main + "_residual")
            LAG = 2
            NR = len(ROUNDS)

            def bank_view(buf, n):
                h0, h1 = BANK_HEADS[n]
                return buf[:, n * HALF:n * HALF + (h1 - h0) * JP].rearrange("p (h j) -> p h j", j=JP)[:, :, 0:J]

            if masked:
                @part(sp_parts, main)
                def _(sp, b):
                    sp.dma_start(mask8[:], A["mask_BxSxS2_bk1"][bass.ds(b * N, N), :].rearrange(
                        "(t p) j -> p t j", p=P)).then_inc(mask_in, 16)

            @part(pe_parts, main)
            def _(pe, b):
                for i in range(TT + LAG + 1):
                    j, o = i - LAG, i - LAG - 1
                    for r in range(NR):
                        if 0 <= j < TT:
                            if r == 0:
                                pe.wait_ge(p_done, j + 1)
                            if j or r:
                                pe.wait_ge(t_lo, NR * j + r)
                            c0, c1 = ROUNDS[r]
                            for c in range(c0, c1):
                                ins = pe.transpose(PT[:, (c - c0) * P:(c - c0 + 1) * P],
                                                   PR[j % NP][:, c * P:(c + 1) * P], ident[:])
                            ins.then_inc(t_ps, 1)
                        if i < TT:
                            if r == 0 and i >= 2:
                                pe.wait_ge(s_out, i - 1)
                            h0, h1 = BANK_HEADS[r]
                            for c in range(DC):
                                tok = slice(i * P, (i + 1) * P)
                                ins = mm3(pe, SPS[i % 2][:, r * HALF:r * HALF + (h1 - h0) * JP],
                                          XTh[:, c, tok], XTl[:, c, tok],
                                          AHi[:, c, h0 * JP:h1 * JP], ALo[:, c, h0 * JP:h1 * JP],
                                          c == 0, c == DC - 1)
                            if r == NR - 1:
                                ins.then_inc(s_ps, 1)
                    if 0 <= o < TT:
                        pe.wait_ge(t_lo, NR * (o + 1))
                        if o:
                            pe.wait_ge(x_done, o)
                        for c in range(HJC):
                            ins = mm3(pe, PV[:, 0:D], PTh[o % 2][:, c, :], PTl[o % 2][:, c, :],
                                      VWh[:, c, :], VWl[:, c, :], c == 0, c == HJC - 1)
                        ins.then_inc(o_ps, 1)

            @part(act_parts, main)
            def _(act, b):
                act.wait_ge(cleared, 1)
                for i in range(TT + LAG):
                    j = i - LAG
                    if 0 <= j < TT:
                        for r, (c0, c1) in enumerate(ROUNDS):
                            act.wait_ge(t_ps, NR * j + r + 1)
                            if r == 0 and j >= 2:
                                act.wait_ge(o_ps, j - 1)
                            act.activation(PTh[j % 2][:, c0:c1, :].rearrange("p c q -> p (c q)"),
                                           PT[:, 0:(c1 - c0) * P], ACT.Copy).then_inc(t_hi, 1)
                    if i < TT and not masked:
                        act.wait_ge(s_ps, i + 1)
                        if i >= 2:
                            act.wait_ge(ex_done, i - 1)
                        for n, (h0, h1) in enumerate(BANK_HEADS):
                            ins = act.activation(SB[i % 2][:, h0:h1, 0:J], bank_view(SPS[i % 2], n), ACT.Copy)
                        ins.then_inc(s_out, 1)
                    if i < TT:
                        act.wait_ge(sub_done, i + 1)
                        if i >= NP:
                            act.wait_ge(t_ps, NR * (i - NP + 1))
                        act.activation(PRv[i % NP][:, :, 0:J], SB[i % 2][:, :, 0:J], ACT.Exp,
                                       scale=scale).then_inc(ex_done, 1)

            @part(dve_parts, main)
            def _(dve, b):
                if masked:
                    dve.wait_ge(mask_in, 16)
                    dve.tensor_scalar(mneg[:], mask8[:], NEG_MAX, None, ALU.mult).then_inc(mask_done, 1)
                    dve.wait_ge(mask_done, 1)
                if bias_row is not None:
                    dve.wait_ge(biased, 1)
                for i in range(TT + LAG + 1):
                    j = i - LAG
                    if 0 <= j < TT:
                        for r, (c0, c1) in enumerate(ROUNDS):
                            dve.wait_ge(t_hi, NR * j + r + 1)
                            dve.tensor_tensor(PTl[j % 2][:, c0:c1, :].rearrange("p c q -> p (c q)"),
                                              PT[:, 0:(c1 - c0) * P],
                                              PTh[j % 2][:, c0:c1, :].rearrange("p c q -> p (c q)").bitcast(F32),
                                              ALU.subtract).then_inc(t_lo, 1)
                    if i < TT:
                        if masked:
                            dve.wait_ge(s_ps, i + 1)
                            if i >= 2:
                                dve.wait_ge(ex_done, i - 1)
                            for n, (h0, h1) in enumerate(BANK_HEADS):
                                ins = dve.tensor_tensor(
                                    SB[i % 2][:, h0:h1, 0:J], bank_view(SPS[i % 2], n),
                                    mneg[:, i, :].unsqueeze(1).broadcast_to([P, h1 - h0, J]), ALU.add)
                            ins.then_inc(s_out, 1)
                        dve.wait_ge(s_out, i + 1)
                        if i >= 2:
                            dve.wait_ge(sub_done, i - 1)
                        dve.tensor_reduce(mx[:, i % 2, :], SB[i % 2][:, :, 0:J], AX.X, ALU.max
                                          ).then_inc(mx_done, 1)
                    if 1 <= i <= TT:
                        q = i - 1
                        dve.wait_ge(ex_done, q + 1)
                        if q >= NP:
                            dve.wait_ge(inv_done, q - NP + 1)
                        dve.tensor_reduce(sm[:, q % NP, :], PRv[q % NP][:, :, 0:J], AX.X, ALU.add
                                          ).then_inc(sum_done, 1)
                        dve.wait_ge(sum_done, q + 1)
                        if q >= NP:
                            dve.wait_ge(p_done, q - NP + 1)
                        dve.reciprocal(rs[:, q % NP, :], sm[:, q % NP, :]).then_inc(inv_done, 1)
                    o = i - LAG - 1
                    if 0 <= o < TT:
                        dve.wait_ge(o_ps, o + 1)
                        dve.scalar_tensor_tensor(X[:, o, :], PV[:, 0:D], tg[:, gate:gate + 1], X[:, o, :],
                                                 ALU.mult, ALU.add).then_inc(x_done, 1)

            @part(pool_parts, main)
            def _(pool, b):
                for p_ in PR:
                    ins = pool.memset(p_[:], 0.0)
                ins.then_inc(cleared, 1)
                if bias_row is not None:
                    pool.tensor_tensor(X[:], X[:], rowb[:, bias_row, :].unsqueeze(1).broadcast_to([P, TT, D]),
                                       ALU.add).then_inc(biased, 1)
                for i in range(TT + 1):
                    if i < TT:
                        pool.wait_ge(mx_done, i + 1)
                        s_ = SB[i % 2][:, :, 0:J]
                        pool.tensor_tensor(s_, s_, mx[:, i % 2, :].unsqueeze(2).broadcast_to([P, HEADS, J]),
                                           ALU.subtract).then_inc(sub_done, 1)
                    if i >= 1:
                        q = i - 1
                        pool.wait_ge(inv_done, q + 1)
                        p_ = PRv[q % NP][:, :, 0:J]
                        pool.tensor_tensor(p_, p_, rs[:, q % NP, :].unsqueeze(2).broadcast_to([P, HEADS, J]),
                                           ALU.mult).then_inc(p_done, 1)

        def by_rows(name):
            return lambda raw, i, g: (raw[:, i, :], A[name][g * P:(g + 1) * P, :])

        def by_cols(name):
            return lambda raw, i, g: (raw[:, i, :].rearrange("p (c e) -> p c e", c=DC),
                                      A[name].rearrange("(c p) e -> p c e", p=P)[:, :, g * P:(g + 1) * P])

        ln_stage("ln0x")
        with buffers():
            context_attention(0, 2, [by_cols("L0_xattn_Wk"), by_cols("L0_xattn_Wv"),
                                     by_rows("L0_xattn_WqT"), by_rows("L0_xattn_Wo")],
                              DH ** -0.5, 0, True, BO0)

        QW = [("L0_ffn_gT", DC, INNER), ("L0_ffn_uT", DC, INNER), ("L0_ffn_dT", INNER // P, D)]
        WCOLS = DC * INNER
        IC = INNER // P
        ln_stage("ln0f", feature_major=False)
        with buffers():
            wraw = [sb(f"ternary_raw{n}", [P, WCOLS]) for n in range(3)]
        bit_scope = ExitStack()
        scope = bit_scope
        XQ = sb("x_ints_f", [P, TT, D])
        XQb = sb("x_ints", [P, TT, D], BF16)
        XQT = sb("x_ints_t", [P, DC, N], BF16)
        amax = sb("x_abs_max", [P, TT])
        ainv = sb("x_inv_max", [P, TT])
        TH = [sb(f"bit_tanh{i}", [P, INNER]) for i in range(2)]
        GA = [sb(f"bit_gate{i}", [P, INNER]) for i in range(2)]
        HH = [sb(f"bit_hidden{i}", [P, INNER]) for i in range(2)]
        HQ = [sb(f"bit_hidden_ints{i}", [P, INNER], BF16) for i in range(2)]
        HT = [sb(f"bit_hidden_t{i}", [P, IC, P], BF16) for i in range(2)]
        cg = sb("bit_gate_scale", [P, TT])
        hcg = sb("bit_half_gate_scale", [P, TT])
        cgu = sb("bit_product_scale", [P, TT])
        hmax = sb("hidden_abs_max", [P, TT])
        hclip = sb("hidden_clipped_max", [P, TT])
        hinv = sb("hidden_inv_max", [P, TT])
        hout = sb("hidden_out_scale", [P, TT])
        bit_scope.close()
        scope = life

        bw_in = [life.enter_context(nc.semaphore(f"bit_weight{n}_in")) for n in range(3)]
        bw_sum = life.enter_context(nc.semaphore("bit_weight_sum"))
        bw_steps = life.enter_context(nc.semaphore("bit_weight_steps"))
        bq_steps = signal("bitq_dve_steps")
        bx_ints = signal("bit_x_ints")
        bx_ps = signal("bit_x_transposed")
        bx_t = signal("bit_x_t_copied")

        def sp_ternary(sp):
            for n, (name, c, w) in enumerate(QW):
                sp.dma_start(wraw[n][:].rearrange("p (c w) -> p c w", c=c),
                             A[name].rearrange("(c p) w -> p c w", p=P)).then_inc(bw_in[n], 16)

        def dve_ternary(dve):
            chain = Chain(dve, bw_steps)
            for n in range(3):
                dve.wait_ge(bw_in[n], 16)
                chain.step(dve.tensor_reduce(wabs[:, n:n + 1], wraw[n][:], AX.X, ALU.add,
                                             apply_absolute_value=True))
            dve.wait_ge(bw_sum, 1)
            chain.step(dve.tensor_scalar(wmean[:], PV[:, 0:3], 1.0 / (INNER * D), EPS, ALU.mult, ALU.max))
            chain.settle()
            chain.step(dve.reciprocal(winv[:], wmean[:]))
            chain.settle()
            for n in range(3):
                chain.step(dve.tensor_scalar(wraw[n][:], wraw[n][:], winv[:, n:n + 1], 1.0, ALU.mult, ALU.min))
            chain.settle()
            for n in range(3):
                chain.step(dve.tensor_scalar(wraw[n][:], wraw[n][:], -1.0, MAGIC, ALU.max, ALU.add))
            chain.settle()
            for n in range(3):
                chain.step(dve.tensor_scalar(wq[n][:], wraw[n][:], -MAGIC, None, ALU.add))
            chain.settle()

        def pe_ternary(pe):
            pe.wait_ge(bw_steps, 3)
            pe.matmul(PV[:, 0:3], ones[:], wabs[:], start=True, stop=True).then_inc(bw_sum, 1)

        @part(dve_parts, "bitq")
        def _(dve, b):
            chain = Chain(dve, bq_steps)
            chain.step(dve.tensor_reduce(amax[:], XN[:], AX.X, ALU.max, apply_absolute_value=True))
            chain.settle()
            chain.step(dve.tensor_scalar(amax[:], amax[:], EPS, None, ALU.max))
            chain.settle()
            chain.step(dve.reciprocal(ainv[:], amax[:]))
            chain.settle()
            chain.step(dve.tensor_scalar(ainv[:], ainv[:], 127.0, None, ALU.mult))
            chain.settle()
            for t in range(TT):
                ins = dve.tensor_scalar(XQ[:, t, :], XN[:, t, :], ainv[:, t:t + 1], MAGIC, ALU.mult, ALU.add)
            chain.step(ins)
            chain.settle()
            dve.tensor_scalar(XQb[:], XQ[:], -MAGIC, 127.0, ALU.add, ALU.min).then_inc(bx_ints, 1)
            chain.step(dve.tensor_scalar(cg[:], amax[:], wmean[:, 0:1], 1.0 / 127.0, ALU.mult, ALU.mult))
            chain.settle()
            chain.step(dve.tensor_scalar(hcg[:], cg[:], 0.5, None, ALU.mult))
            chain.settle()
            chain.step(dve.tensor_scalar(cgu[:], amax[:], wmean[:, 1:2], 1.0 / 127.0, ALU.mult, ALU.mult))
            chain.settle()
            chain.step(dve.tensor_tensor(cgu[:], cgu[:], hcg[:], ALU.mult))

        @part(pe_parts, "bitq")
        def _(pe, b):
            pe.wait_ge(bx_ints, 1)
            for q, (c, h) in enumerate(QUADS):
                for i in range(4):
                    ins = pe.transpose(BANKS[q + 1].bitcast(BF16)[:, i * P:(i + 1) * P],
                                       XQb[:, 4 * h + i, c * P:(c + 1) * P], identb[:])
                ins.then_inc(bx_ps, 1)

        @part(act_parts, "bitq")
        def _(act, b):
            for q, (c, h) in enumerate(QUADS):
                act.wait_ge(bx_ps, q + 1)
                act.activation(XQT[:, c, h * HALF:(h + 1) * HALF], BANKS[q + 1].bitcast(BF16)[:, 0:HALF],
                               ACT.Copy).then_inc(bx_t, 1)

        bg_ps = signal("bit_gate_up")
        b_tanh = signal("bit_tanh")
        b_gate = signal("bit_gate")
        b_hid = signal("bit_hidden")
        b_small = signal("bit_small_steps")
        b_hscale = signal("bit_hidden_scale")
        b_round = signal("bit_rounded")
        b_hq = signal("bit_hidden_ints")
        b_htp = signal("bit_hidden_transposed")
        b_ht = signal("bit_hidden_t")
        b_out = signal("bit_out")
        b_x = signal("bit_residual")

        @part(pe_parts, "bit")
        def _(pe, b):
            wv = [wq[n][:].rearrange("p (c w) -> p c w", c=c) for n, (_, c, _) in enumerate(QW)]
            for i in range(TT + 3):
                if i < TT:
                    if i:
                        pe.wait_ge(b_hid, i)
                    for n, buf in ((0, PA), (1, PB)):
                        for s in range(INNER // HALF):
                            for c in range(DC):
                                ins = pe.matmul(buf[:, s * HALF:(s + 1) * HALF], XQT[:, c, i * P:(i + 1) * P],
                                                wv[n][:, c, s * HALF:(s + 1) * HALF], start=c == 0, stop=c == DC - 1)
                    ins.then_inc(bg_ps, 1)
                j = i - 2
                if 0 <= j < TT:
                    pe.wait_ge(b_hq, j + 1)
                    if j:
                        pe.wait_ge(b_ht, j)
                    for c in range(IC):
                        ins = pe.transpose(PT[:].bitcast(BF16)[:, c * P:(c + 1) * P],
                                           HQ[j % 2][:, c * P:(c + 1) * P], identb[:])
                    ins.then_inc(b_htp, 1)
                o = i - 3
                if 0 <= o < TT:
                    pe.wait_ge(b_ht, o + 1)
                    if o:
                        pe.wait_ge(b_x, o)
                    for c in range(IC):
                        ins = pe.matmul(PV[:, 0:D], HT[o % 2][:, c, :], wv[2][:, c, :], start=c == 0, stop=c == IC - 1)
                    ins.then_inc(b_out, 1)

        @part(act_parts, "bit")
        def _(act, b):
            for i in range(TT + 2):
                j = i - 2
                if 0 <= j < TT:
                    act.wait_ge(b_htp, j + 1)
                    if j >= 2:
                        act.wait_ge(b_out, j - 1)
                    act.activation(HT[j % 2][:].rearrange("p c q -> p (c q)"), PT[:].bitcast(BF16), ACT.Copy
                                   ).then_inc(b_ht, 1)
                if i < TT:
                    act.wait_ge(bg_ps, i + 1)
                    if i >= 2:
                        act.wait_ge(b_gate, i - 1)
                    act.activation(TH[i % 2][:], PA[:, 0:INNER], ACT.Tanh, scale=hcg[:, i:i + 1]).then_inc(b_tanh, 1)

        @part(dve_parts, "bit")
        def _(dve, b):
            small = Chain(dve, b_small)
            for i in range(TT + 3):
                if i < TT:
                    t1 = slice(i, i + 1)
                    dve.wait_ge(b_tanh, i + 1)
                    if i >= 2:
                        dve.wait_ge(b_hid, i - 1)
                    dve.scalar_tensor_tensor(GA[i % 2][:], TH[i % 2][:], 1.0, PA[:, 0:INNER], ALU.add, ALU.mult
                                             ).then_inc(b_gate, 1)
                    dve.wait_ge(b_gate, i + 1)
                    if i >= 2:
                        dve.wait_ge(b_round, i - 1)
                    dve.scalar_tensor_tensor(HH[i % 2][:], GA[i % 2][:], cgu[:, t1], PB[:, 0:INNER],
                                             ALU.mult, ALU.mult).then_inc(b_hid, 1)
                    dve.wait_ge(b_hid, i + 1)
                    small.step(dve.tensor_reduce(hmax[:, t1], HH[i % 2][:], AX.X, ALU.max, apply_absolute_value=True))
                    small.settle()
                    small.step(dve.tensor_scalar(hclip[:, t1], hmax[:, t1], EPS, None, ALU.max))
                    small.settle()
                    small.step(dve.reciprocal(hinv[:, t1], hclip[:, t1]))
                    small.settle()
                    dve.tensor_scalar(hinv[:, t1], hinv[:, t1], 127.0, None, ALU.mult).then_inc(b_hscale, 1)
                    small.step(dve.tensor_scalar(hout[:, t1], hclip[:, t1], wmean[:, 2:3], 1.0 / 127.0,
                                                 ALU.mult, ALU.mult))
                    small.settle()
                    small.step(dve.tensor_scalar(hout[:, t1], hout[:, t1], tg[:, LAYERS:LAYERS + 1], None, ALU.mult))
                q = i - 1
                if 0 <= q < TT:
                    dve.wait_ge(b_round, q + 1)
                    if q >= 2:
                        dve.wait_ge(b_htp, q - 1)
                    dve.tensor_scalar(HQ[q % 2][:], HH[q % 2][:], -MAGIC, 127.0, ALU.add, ALU.min).then_inc(b_hq, 1)
                o = i - 3
                if 0 <= o < TT:
                    dve.wait_ge(b_out, o + 1)
                    dve.scalar_tensor_tensor(X[:, o, :], PV[:, 0:D], hout[:, o:o + 1], X[:, o, :],
                                             ALU.mult, ALU.add).then_inc(b_x, 1)

        @part(pool_parts, "bit")
        def _(pool, b):
            for i in range(TT):
                pool.wait_ge(b_hscale, i + 1)
                pool.tensor_scalar(HH[i % 2][:], HH[i % 2][:], hinv[:, i:i + 1], MAGIC, ALU.mult, ALU.add
                                   ).then_inc(b_round, 1)

        def hi_of(eng, hi, src):
            return eng.tensor_scalar(hi, src, 1.0, 0.0, ALU.mult, ALU.add)

        next_layer()
        def latent_attention(k, heads, weights, ctx, out_to, gate, bias_row, mask=None):
            st = f"attn{k}"
            pairs = heads // 2
            n_w = len(weights)
            own_ctx = n_w == 6
            Ch, Cl = ctx
            SEG = [(0, HALF), (HALF, N), (N, KEYSP)]
            ROUNDS = [(0, 4), (4, 8), (8, KC)]
            LAG, NPB = 3, 4
            UNITS = 2 * TT
            FIRST = slice(0, DH)
            SECOND = slice(DH, P)
            ROWS = [FIRST, SECOND]
            with buffers():
                raw = sb(f"qkvo_raw{k}", [P, n_w, D])
                wh = sb(f"qkvo_hi{k}", [P, n_w, D], F32R)
                wl = sb(f"qkvo_lo{k}", [P, n_w, D], F32R)
                QS = [sb(f"q_stack{k}_{i}", [P, N], F32R) for i in range(2)]
                KH = [sb(f"k_hi{k}_{i}", [P, KEYSP], F32R) for i in range(2)]
                KL = [sb(f"k_lo{k}_{i}", [P, KEYSP], F32R) for i in range(2)]
                V = sb(f"v{k}", [P, KC, P])
                PR = [sb(f"p{k}_{i}", [P, KC * P]) for i in range(NPB)]
                PTS = [[sb(f"p_t{k}_{i}_{h}", [P, KC, P]) for h in range(2)] for i in range(2)]
                OTh = sb(f"o_t_hi{k}", [P, N], F32R)
                OTl = sb(f"o_t_lo{k}", [P, N], F32R)
                nmax = sb(f"neg_max{k}", [P, NPB])
                rsum = sb(f"row_sums{k}", [P, NPB, 2])
                rtot = sb(f"row_totals{k}", [P, NPB])
                SCX = sb(f"ctx_scores{k}", [P, UNITS, JP])
                ncmax = sb(f"neg_max_ctx{k}", [P, UNITS])
                ntmax = sb(f"neg_max_tok{k}", [P, NPB])
                rinv = sb(f"row_invs{k}", [P, NPB])
                Y = sb(f"attn_out{k}", [P, TT, D]) if out_to is None else None
                mask8 = sb(f"ctx_mask{k}", [P, J], U8) if mask else None
                mrow = sb(f"ctx_mask_add{k}", [P, JP], F32R) if mask else None
                mpad = sb(f"ctx_mask_row{k}", [P, JP]) if mask else None
                onesr = sb(f"ones_r{k}", [P, P], F32R) if mask else None
            dest = X if out_to is not None else Y
            loop_signals = []

            def in_loop(name):
                s = semaphore(f"{st}_{name}")
                loop_signals.append(s)
                return s

            w_first = signal(st + "_first_weights")
            w_in = in_loop("weights_in")
            w_hi = in_loop("weights_hi")
            w_lo = in_loop("weights_lo")
            k_ps, q_ps, v_ps = in_loop("k_projected"), in_loop("q_projected"), in_loop("v_projected")
            kq_hi, kq_lo, v_sb = in_loop("kq_hi"), in_loop("kq_lo"), in_loop("v_copied")
            s_ps = in_loop("scores")
            c_ps, c_sb, c_max = in_loop("ctx_scores"), in_loop("ctx_scores_copied"), in_loop("ctx_max")
            ec_done = in_loop("exp_ctx")
            t_max, total = in_loop("token_max"), in_loop("row_total")
            m_done, e_done, i_done, p_done = (in_loop("neg_max"), in_loop("exp"), in_loop("inv_sum"),
                                              in_loop("probs_scaled"))
            t_ps, t_act, t_dve = in_loop("probs_t"), in_loop("probs_t_act"), in_loop("probs_t_dve")
            pv_done, o_hi, o_lo = in_loop("pv"), in_loop("out_t_hi"), in_loop("out_t_lo")
            wo_ps, x_add = in_loop("projected"), in_loop("added")
            pads = signal(st + "_pads")
            mask_in, mask_row = (signal(st + "_mask_in"), signal(st + "_mask_row")) if mask else (None, None)
            turn = turn_signals(st)

            def load(sp, p, sem):
                for i, (name, kind, off) in enumerate(weights):
                    if kind == "rows":
                        dst, src = raw[:, i, :], A[name][bass.ds(p * P, P), :]
                    else:
                        dst = raw[:, i, :].rearrange("p (c e) -> p c e", c=DC)
                        src = A[name].rearrange("(c p) e -> p c e", p=P)[:, :, bass.ds(p * P + off, P)]
                    sp.dma_start(dst, src).then_inc(sem, 16)

            @part(sp_parts, st)
            def _(sp, b):
                load(sp, 0, w_first)
                if mask:
                    sp.dma_start(mask8[:], A[mask][bass.ds(b, 1), :].broadcast_to([P, J])).then_inc(mask_in, 16)
                    sp.wait_ge(mask_in, 16)
                sp.wait_ge(w_first, 16 * n_w)
                with sp.Fori(1, pairs) as p:
                    sp.wait_ge(w_lo, 1)
                    load(sp, p, w_in)
                    sp.wait_ge(w_in, 16 * n_w)
                    end_turn(sp, "sp", turn, loop_signals)
                end_turn(sp, "sp", turn, loop_signals)

            @part(pool_parts, st)
            def _(pool, b):
                if mask:
                    pool.memset(mpad[:, J:JP], 0.0).then_inc(mask_row, 1)
                    hi_of(pool, onesr[:], ones[:]).then_inc(mask_row, 1)
                    pool.wait_ge(mask_in, 16)
                    pool.wait_ge(mask_row, 1)
                    pool.tensor_scalar(mpad[:, 0:J], mask8[:], MASK_PART, -MASK_PART, ALU.mult, ALU.add
                                       ).then_inc(mask_row, 1)
                    pool.wait_ge(mask_row, 3)
                    hi_of(pool, mrow[:], mpad[:]).then_inc(mask_row, 1)
                pool.memset(V[:, KC - 1, :], 0.0)
                for p_ in PR:
                    ins = pool.memset(p_[:], 0.0)
                if Y is not None:
                    ins = pool.memset(Y[:], 0.0)
                ins.then_inc(pads, 1)
                if bias_row is not None:
                    pool.tensor_tensor(X[:], X[:], rowb[:, bias_row, :].unsqueeze(1).broadcast_to([P, TT, D]),
                                       ALU.add).then_inc(pads, 1)
                else:
                    pool.wait_ge(pads, 1)
                pool.wait_ge(w_first, 16 * n_w)
                with pool.Fori(0, pairs) as p:
                    pool.tensor_scalar(wh[:], raw[:], 1.0, 0.0, ALU.mult, ALU.add).then_inc(w_hi, 1)
                    pool.wait_ge(w_hi, 1)
                    pool.tensor_tensor(wl[:], raw[:], wh[:].bitcast(F32), ALU.subtract).then_inc(w_lo, 1)
                    for u in range(UNITS):
                        pool.wait_ge(i_done, u + 1)
                        pr = PR[u % NPB][:, 0:KEYS]
                        pool.tensor_scalar(pr, pr, rinv[:, u % NPB:u % NPB + 1], 0.0, ALU.mult, ALU.add
                                           ).then_inc(p_done, 1)
                    end_turn(pool, "pool", turn, loop_signals)

            SPS = [PA, PB]
            TBANK = [BANKS[2], PT]
            VBANK = [PV, BANKS[5]]
            CTX_BANKS = [(BANKS[2], 0, 6), (PT, 6, 11), (BANKS[5], 11, UNITS)]

            @part(pe_parts, st)
            def _(pe, b):
                pe.wait_ge(pads, 1 if bias_row is None else 2)
                if mask:
                    pe.wait_ge(mask_row, 4)
                with pe.Fori(0, pairs) as p:
                    pe.wait_ge(w_lo, 1)
                    IQ, IK, IV, IO = 0, 1, 2, 3
                    IKC, IVC = (4, 5) if own_ctx else (1, 2)
                    for dst, idx, done in ((PA, IK, k_ps), (PB, IQ, q_ps)):
                        for h in range(NHALF):
                            for c in range(DC):
                                e, tok = slice(c * P, (c + 1) * P), slice(h * HALF, (h + 1) * HALF)
                                ins = mm3(pe, dst[:, h * HALF:(h + 1) * HALF], wh[:, idx, e], wl[:, idx, e],
                                          XTh[:, c, tok], XTl[:, c, tok], c == 0, c == DC - 1)
                        if idx == IK:
                            for c in range(DC):
                                e = slice(c * P, (c + 1) * P)
                                ins = mm3(pe, PA[:, N:KEYSP], wh[:, IKC, e], wl[:, IKC, e],
                                          Ch[:, c, :], Cl[:, c, :], c == 0, c == DC - 1)
                        ins.then_inc(done, 1)
                    for t in range(KC):
                        acc = (PT[:, t * P:(t + 1) * P] if t < 4 else PV[:, (t - 4) * P:(t - 3) * P]
                               if t < TT else PB[0:JP, N:N + P])
                        for c in range(DC):
                            e, tok = slice(c * P, (c + 1) * P), slice(t * P, (t + 1) * P)
                            if t < TT:
                                ins = mm3(pe, acc, XTh[:, c, tok], XTl[:, c, tok], wh[:, IV, e], wl[:, IV, e],
                                          c == 0, c == DC - 1)
                            else:
                                ins = mm3(pe, acc, Ch[:, c, :], Cl[:, c, :], wh[:, IVC, e], wl[:, IVC, e],
                                          c == 0, c == DC - 1)
                    ins.then_inc(v_ps, 1)

                    def scores(u, n, acc, done):
                        t, hd = u // 2, u % 2
                        a, z = SEG[n]
                        tok = slice(t * P, (t + 1) * P)
                        last = n < 2 or not mask
                        pe.matmul(acc, QS[hd][:, tok], KH[hd][:, a:z], start=True, stop=False)
                        ins = pe.matmul(acc, QS[hd][:, tok], KL[hd][:, a:z], start=False, stop=last)
                        if not last:
                            ins = pe.matmul(acc, onesr[:], mrow[:], start=False, stop=True)
                        if done is not None:
                            ins.then_inc(done, 1)

                    def values(t, c0, c1):
                        for c in range(c0, c1):
                            for hd in range(2):
                                ins = pe.matmul(VBANK[t // 4][ROWS[hd], (t % 4) * P:(t % 4 + 1) * P], V[:, c, ROWS[hd]],
                                                PTS[t % 2][hd][:, c, :], start=c == 0, stop=c == KC - 1)
                        if c1 == KC:
                            ins.then_inc(pv_done, 1)

                    pe.wait_ge(kq_hi, 6)
                    pe.wait_ge(kq_lo, 6)
                    pe.wait_ge(v_sb, 3)
                    for bank, u0, u1 in CTX_BANKS:
                        for u in range(u0, u1):
                            scores(u, 2, bank[:, (u - u0) * JP:(u - u0 + 1) * JP], c_ps if u == u1 - 1 else None)
                    for i in range(UNITS + LAG + 2):
                        j = i - LAG
                        tv = (j - 2) // 2
                        for n in range(3):
                            if 0 <= j < UNITS:
                                if n == 0:
                                    pe.wait_ge(p_done, j + 1)
                                    if j:
                                        pe.wait_ge(t_dve, j)
                                    else:
                                        pe.wait_ge(c_sb, 3)
                                elif n == 1 and j:
                                    pe.wait_ge(t_act, 2 * j)
                                elif n == 2:
                                    pe.wait_ge(t_act, 2 * j + 1)
                                c0, c1 = ROUNDS[n]
                                for c in range(c0, c1):
                                    ins = pe.transpose(TBANK[(3 * j + n) % 2][:, (c - c0) * P:(c - c0 + 1) * P],
                                                       PR[j % NPB][:, c * P:(c + 1) * P], ident[:])
                                ins.then_inc(t_ps, 1)
                            if i < UNITS and n < 2:
                                if n == 0 and i >= 2:
                                    pe.wait_ge(e_done, i - 1)
                                scores(i, n, SPS[i % 2][:, n * HALF:(n + 1) * HALF], s_ps if n == 1 else None)
                            if 0 <= tv < TT and n < 2:
                                if j % 2 == 0 and n == 0:
                                    pe.wait_ge(t_act, 4 * (tv + 1))
                                    pe.wait_ge(t_dve, 2 * (tv + 1))
                                part_ = [(0, 2), (2, 4), (4, 7), (7, KC)][(j % 2) * 2 + n]
                                values(tv, *part_)
                    pe.wait_ge(o_lo, 2)
                    pe.wait_ge(e_done, UNITS)
                    for q in range(4):
                        bank = [BANKS[0], BANKS[1], BANKS[3], BANKS[4]][q]
                        for t in (2 * q, 2 * q + 1):
                            tok = slice(t * P, (t + 1) * P)
                            ins = mm3(pe, bank[:, (t % 2) * D:(t % 2 + 1) * D], OTh[:, tok], OTl[:, tok],
                                      wh[:, IO, :], wl[:, IO, :], True, True)
                        ins.then_inc(wo_ps, 1)
                    end_turn(pe, "pe", turn, loop_signals)

            @part(act_parts, st)
            def _(act, b):
                act.wait_ge(pads, 1)
                with act.Fori(0, pairs) as p:
                    act.wait_ge(k_ps, 1)
                    for hd in range(2):
                        for half in ROWS:
                            act.activation(KH[hd][half, :], PA[ROWS[hd], 0:KEYSP], ACT.Copy).then_inc(kq_hi, 1)
                    act.wait_ge(q_ps, 1)
                    for hd in range(2):
                        act.activation(QS[hd][ROWS[hd], :], PB[ROWS[hd], 0:N], ACT.Copy, scale=DH ** -0.5
                                       ).then_inc(kq_hi, 1)
                    act.wait_ge(v_ps, 1)
                    act.activation(V[:, 0:4, :].rearrange("p c e -> p (c e)"), PT[:], ACT.Copy).then_inc(v_sb, 1)
                    act.activation(V[:, 4:8, :].rearrange("p c e -> p (c e)"), PV[:], ACT.Copy).then_inc(v_sb, 1)
                    act.activation(V[0:JP, TT, :], PB[0:JP, N:N + P], ACT.Copy).then_inc(v_sb, 1)
                    for g, (bank, u0, u1) in enumerate(CTX_BANKS):
                        act.wait_ge(c_ps, g + 1)
                        act.activation(SCX[:, u0:u1, :].rearrange("p u j -> p (u j)"), bank[:, 0:(u1 - u0) * JP],
                                       ACT.Copy).then_inc(c_sb, 1)
                    for i in range(UNITS + LAG):
                        j = i - LAG
                        if i == UNITS // 2 + LAG + 3:
                            act.wait_ge(pv_done, 4)
                            act.activation(OTh[:, 0:HALF], PV[:], ACT.Copy).then_inc(o_hi, 1)
                        if 0 <= j < UNITS:
                            for n in (0, 2):
                                c0, c1 = ROUNDS[n]
                                act.wait_ge(t_ps, 3 * j + n + 1)
                                if n == 0 and j // 2 >= 2:
                                    act.wait_ge(pv_done, j // 2 - 1)
                                act.activation(PTS[(j // 2) % 2][j % 2][:, c0:c1, :].rearrange("p c q -> p (c q)"),
                                               TBANK[(3 * j + n) % 2][:, 0:(c1 - c0) * P], ACT.Copy
                                               ).then_inc(t_act, 1)
                        if i < UNITS:
                            exp(act, i)
                    act.wait_ge(pv_done, TT)
                    act.activation(OTh[:, HALF:N], VBANK[1], ACT.Copy).then_inc(o_hi, 1)
                    end_turn(act, "act", turn, loop_signals)

            def exp(act, u):
                s_ = u % NPB
                act.wait_ge(m_done, u + 1)
                if u >= NPB:
                    act.wait_ge(t_ps, 3 * (u - NPB + 1))
                act.activation(PR[s_][:, 0:N], SPS[u % 2][:, 0:N], ACT.Exp, bias=nmax[:, s_:s_ + 1],
                               accum_out=rsum[:, s_, 0:1]).then_inc(e_done, 1)
                act.activation(PR[s_][:, N:KEYS], SCX[:, u, 0:J], ACT.Exp, bias=nmax[:, s_:s_ + 1],
                               accum_out=rsum[:, s_, 1:2]).then_inc(ec_done, 1)

            @part(dve_parts, st)
            def _(dve, b):
                dve.wait_ge(pads, 1 if bias_row is None else 2)
                with dve.Fori(0, pairs) as p:
                    dve.wait_ge(k_ps, 1)
                    for hd in range(2):
                        for n, half in enumerate(ROWS):
                            dve.wait_ge(kq_hi, 2 * hd + 2)
                            dve.tensor_tensor(KL[hd][half, :], PA[ROWS[hd], 0:KEYSP],
                                              KH[hd][ROWS[hd], :].bitcast(F32), ALU.subtract).then_inc(kq_lo, 1)
                    for hd in range(2):
                        dve.wait_ge(kq_hi, 5 + hd)
                        dve.scalar_tensor_tensor(QS[hd][ROWS[1 - hd], :], PB[ROWS[hd], 0:N], DH ** -0.5,
                                                 QS[hd][ROWS[hd], :].bitcast(F32), ALU.mult, ALU.subtract
                                                 ).then_inc(kq_lo, 1)
                    dve.wait_ge(c_sb, 3)
                    dve.tensor_reduce(ncmax[:], SCX[:, :, 0:J], AX.X, ALU.max, negate=True).then_inc(c_max, 1)
                    dve.wait_ge(c_max, 1)
                    for i in range(UNITS + LAG + 1):
                        j = i - LAG
                        if i == UNITS // 2 + LAG + 3:
                            dve.wait_ge(o_hi, 1)
                            dve.tensor_tensor(OTl[:, 0:HALF], PV[:], OTh[:, 0:HALF].bitcast(F32), ALU.subtract
                                              ).then_inc(o_lo, 1)
                        if 0 <= j < UNITS:
                            c0, c1 = ROUNDS[1]
                            dve.wait_ge(t_ps, 3 * j + 2)
                            if j // 2 >= 2:
                                dve.wait_ge(pv_done, j // 2 - 1)
                            dve.tensor_copy(PTS[(j // 2) % 2][j % 2][:, c0:c1, :].rearrange("p c q -> p (c q)"),
                                            TBANK[(3 * j + 1) % 2][:, 0:(c1 - c0) * P]).then_inc(t_dve, 1)
                        if i < UNITS:
                            s_ = i % NPB
                            dve.wait_ge(s_ps, i + 1)
                            if i >= NPB:
                                dve.wait_ge(m_done, i - NPB + 1)
                            dve.tensor_reduce(ntmax[:, s_:s_ + 1], SPS[i % 2][:, 0:N], AX.X, ALU.max, negate=True
                                              ).then_inc(t_max, 1)
                            dve.wait_ge(t_max, i + 1)
                            if i >= NPB:
                                dve.wait_ge(ec_done, i - NPB + 1)
                            dve.tensor_tensor(nmax[:, s_:s_ + 1], ntmax[:, s_:s_ + 1], ncmax[:, i:i + 1], ALU.min
                                              ).then_inc(m_done, 1)
                        if 1 <= i <= UNITS:
                            s_ = (i - 1) % NPB
                            dve.wait_ge(ec_done, i)
                            if i - 1 >= NPB:
                                dve.wait_ge(i_done, i - NPB)
                            dve.tensor_tensor(rtot[:, s_:s_ + 1], rsum[:, s_, 0:1], rsum[:, s_, 1:2], ALU.add
                                              ).then_inc(total, 1)
                            dve.wait_ge(total, i)
                            if i - 1 >= NPB:
                                dve.wait_ge(p_done, i - NPB)
                            dve.reciprocal(rinv[:, s_:s_ + 1], rtot[:, s_:s_ + 1]).then_inc(i_done, 1)
                    dve.wait_ge(o_hi, 2)
                    dve.tensor_tensor(OTl[:, HALF:N], VBANK[1], OTh[:, HALF:N].bitcast(F32), ALU.subtract
                                      ).then_inc(o_lo, 1)
                    for q in range(4):
                        bank = [BANKS[0], BANKS[1], BANKS[3], BANKS[4]][q]
                        d_ = dest[:, 2 * q:2 * q + 2, :].rearrange("p t d -> p (t d)")
                        dve.wait_ge(wo_ps, q + 1)
                        scalar = 1.0 if gate is None else tg[:, gate:gate + 1]
                        dve.scalar_tensor_tensor(d_, bank, scalar, d_, ALU.mult, ALU.add).then_inc(x_add, 1)
                    end_turn(dve, "dve", turn, loop_signals)
            return Y

        ln_stage("ln1x")
        latent_attention(1, 8, [("L1_xattn_Wq1", "cols", 0), ("L1_xattn_Wk1", "cols", 0),
                                ("L1_xattn_Wv1", "cols", 0), ("L1_xattn_Wo", "rows", 0),
                                ("L1_xattn_Wk2", "cols", 0), ("L1_xattn_Wv2", "cols", 0)],
                         (CTh, CTl), X, 1, BO1)

        ln_stage("ln1f")
        moe_scope = ExitStack()
        scope = moe_scope
        GPT = 2
        TURNS = EXPERTS // (EG * GPT)
        GW = EG * INTER
        SC = sb("router_scores", [P, TT, EXPERTS])
        gwr = sb("router_w", [P, DC, EXPERTS])
        gwh = sb("router_w_hi", [P, DC, EXPERTS], F32R)
        gwl = sb("router_w_lo", [P, DC, EXPERTS], F32R)
        lmax = sb("router_max", [P, TT])
        lshift = sb("router_shifted", [P, TT, EXPERTS])
        ex = sb("router_exp", [P, TT, EXPERTS])
        cmp_ = sb("router_compare", [P, TT, EXPERTS, EXPERTS])
        rank = sb("router_rank", [P, TT, EXPERTS])
        rank2 = sb("router_rank_ties", [P, TT, EXPERTS])
        lower = sb("router_lower_index", [P, EXPERTS, EXPERTS])
        selsum = sb("router_selected_sum", [P, TT])
        selinv = sb("router_selected_inv", [P, TT])
        W1, W3, W2 = 0, 1, 2
        mraw = [sb(f"experts_raw{i}", [P, 3, DC * GW]) for i in range(GPT)]
        mwh = [sb(f"experts_hi{i}", [P, 3, DC * GW], F32R) for i in range(GPT)]
        mwl = [sb(f"experts_lo{i}", [P, 3, DC * GW], F32R) for i in range(GPT)]
        mth = [sb(f"expert_tanh{i}", [P, GW]) for i in range(2)]
        mga = [sb(f"expert_gate{i}", [P, GW]) for i in range(2)]
        mac = [sb(f"expert_act{i}", [P, GW]) for i in range(2)]
        math_ = [sb(f"expert_act_t_hi{i}", [P, GW], F32R) for i in range(2)]
        matl = [sb(f"expert_act_t_lo{i}", [P, GW], F32R) for i in range(2)]
        moe_scope.close()
        scope = life

        gw_in = signal("router_w_in")
        gw_split = signal("router_w_split")
        lower_set = signal("router_lower_set")
        logits = signal("router_logits")
        r_steps = signal("router_steps")
        r_shift = signal("router_shift")
        r_exp = signal("router_exp_done")

        @part(sp_parts, "router")
        def _(sp, b):
            sp.dma_start(gwr[:], A["L1_ffn_gateT"].rearrange("(c p) e -> p c e", p=P)).then_inc(gw_in, 16)

        @part(pool_parts, "router")
        def _(pool, b):
            pool.memset(lower[:], 1.0).then_inc(lower_set, 1)
            pool.wait_ge(lower_set, 1)
            pool.affine_select(out=lower[:], in_=lower[:], compare_op=ALU.is_ge, fill=0.0, base=-1,
                               pattern=[[1, EXPERTS], [-1, EXPERTS]], channel_multiplier=0).then_inc(lower_set, 1)
            pool.wait_ge(gw_in, 16)
            hi_of(pool, gwh[:], gwr[:]).then_inc(gw_split, 1)
            pool.wait_ge(gw_split, 1)
            pool.tensor_tensor(gwl[:], gwr[:], gwh[:].bitcast(F32), ALU.subtract).then_inc(gw_split, 1)

        @part(pe_parts, "router")
        def _(pe, b):
            pe.wait_ge(gw_split, 2)
            for t in range(TT):
                tok = slice(t * P, (t + 1) * P)
                for c in range(DC):
                    ins = mm3(pe, PT[:, t * EXPERTS:(t + 1) * EXPERTS], XTh[:, c, tok], XTl[:, c, tok],
                              gwh[:, c, :], gwl[:, c, :], c == 0, c == DC - 1)
            ins.then_inc(logits, 1)

        @part(act_parts, "router")
        def _(act, b):
            act.wait_ge(r_shift, 1)
            act.activation(ex[:], lshift[:], ACT.Exp).then_inc(r_exp, 1)

        @part(dve_parts, "router")
        def _(dve, b):
            chain = Chain(dve, r_steps)
            lg = PT[:, 0:TT * EXPERTS].rearrange("p (t e) -> p t e", t=TT)
            dve.wait_ge(logits, 1)
            chain.step(dve.tensor_reduce(lmax[:], lg, AX.X, ALU.max))
            chain.settle()
            dve.tensor_tensor(lshift[:], lg, lmax[:].unsqueeze(2).broadcast_to([P, TT, EXPERTS]),
                              ALU.subtract).then_inc(r_shift, 1)
            dve.wait_ge(r_exp, 1)
            four = [P, TT, EXPERTS, EXPERTS]
            mine = ex[:].unsqueeze(3).broadcast_to(four)
            other = ex[:].unsqueeze(2).broadcast_to(four)
            chain.step(dve.tensor_tensor(cmp_[:], other, mine, ALU.is_gt))
            chain.settle()
            chain.step(dve.tensor_reduce(rank[:], cmp_[:], AX.X, ALU.add))
            chain.settle()
            chain.step(dve.tensor_tensor(cmp_[:], other, mine, ALU.is_equal))
            dve.wait_ge(lower_set, 2)
            chain.settle()
            chain.step(dve.tensor_tensor(cmp_[:], cmp_[:], lower[:].unsqueeze(1).broadcast_to(four), ALU.mult))
            chain.settle()
            chain.step(dve.tensor_reduce(rank2[:], cmp_[:], AX.X, ALU.add))
            chain.settle()
            chain.step(dve.tensor_tensor(rank[:], rank[:], rank2[:], ALU.add))
            chain.settle()
            chain.step(dve.scalar_tensor_tensor(SC[:], rank[:], float(TOP_K), ex[:], ALU.is_lt, ALU.mult))
            chain.settle()
            chain.step(dve.tensor_reduce(selsum[:], SC[:], AX.X, ALU.add))
            chain.settle()
            chain.step(dve.reciprocal(selinv[:], selsum[:]))
            chain.settle()
            chain.step(dve.scalar_tensor_tensor(SC[:], SC[:], 0.5, selinv[:].unsqueeze(2).broadcast_to(
                [P, TT, EXPERTS]), ALU.mult, ALU.mult))

        moe_loop = []

        def in_moe(name):
            s = semaphore("moe_" + name)
            moe_loop.append(s)
            return s

        m_first = signal("moe_first_weights")
        m_in = in_moe("weights_in")
        m_hi = in_moe("first_hi")
        m_lo = in_moe("first_lo")
        m_split = in_moe("second_split")
        m_gu = in_moe("gate_up")
        m_tanh = in_moe("tanh")
        m_gate = in_moe("gate")
        m_act = in_moe("act")
        m_tps = in_moe("act_transposed")
        m_thi = in_moe("act_t_hi")
        m_tlo = in_moe("act_t_lo")
        m_out = in_moe("out")
        m_x = in_moe("residual")
        moe_turn = turn_signals("moe")
        STEPS = GPT * TT
        MG = [BANKS[0], BANKS[2]]
        MU = [BANKS[1], BANKS[3]]
        MT = [BANKS[4], BANKS[5]]
        MO = [BANKS[6], BANKS[7]]

        def moe_load(sp, p, sem):
            for i in range(GPT):
                for k, name in ((W1, "L1_ffn_w1"), (W3, "L1_ffn_w3")):
                    for c in range(DC):
                        sp.dma_start(mraw[i][:, k, c * GW:(c + 1) * GW].rearrange("p (e i) -> p e i", e=EG),
                                     A[name].rearrange("e (c p) i -> c p e i", p=P)[c][
                                         :, bass.ds(p * (EG * GPT) + i * EG, EG), :]).then_inc(sem, 16)
                sp.dma_start(mraw[i][:, W2, :].rearrange("p (e d) -> p e d", e=EG),
                             A["L1_ffn_w2"].rearrange("e p d -> p e d")[
                                 :, bass.ds(p * (EG * GPT) + i * EG, EG), :]).then_inc(sem, 16)
        M_LOADS = 16 * GPT * (2 * DC + 1)

        @part(sp_parts, "moe")
        def _(sp, b):
            moe_load(sp, 0, m_first)
            sp.wait_ge(m_first, M_LOADS)
            with sp.Fori(1, TURNS) as p:
                sp.wait_ge(m_lo, 1)
                sp.wait_ge(m_split, 2)
                moe_load(sp, p, m_in)
                sp.wait_ge(m_in, M_LOADS)
                end_turn(sp, "sp", moe_turn, moe_loop)
            end_turn(sp, "sp", moe_turn, moe_loop)

        @part(pool_parts, "moe")
        def _(pool, b):
            pool.wait_ge(m_first, M_LOADS)
            with pool.Fori(0, TURNS) as p:
                hi_of(pool, mwh[1][:], mraw[1][:]).then_inc(m_split, 1)
                pool.wait_ge(m_split, 1)
                pool.tensor_tensor(mwl[1][:], mraw[1][:], mwh[1][:].bitcast(F32), ALU.subtract).then_inc(m_split, 1)
                end_turn(pool, "pool", moe_turn, moe_loop)

        @part(pe_parts, "moe")
        def _(pe, b):
            with pe.Fori(0, TURNS) as p:
                for i in range(STEPS + 2):
                    if i < STEPS:
                        g, t = i // TT, i % TT
                        tok = slice(t * P, (t + 1) * P)
                        if i == 0:
                            pe.wait_ge(m_lo, 1)
                        if i == TT:
                            pe.wait_ge(m_split, 2)
                        if i >= 2:
                            pe.wait_ge(m_act, i - 1)
                        for acc, k in ((MG[i % 2], W1), (MU[i % 2], W3)):
                            for c in range(DC):
                                w = slice(c * GW, (c + 1) * GW)
                                ins = mm3(pe, acc, XTh[:, c, tok], XTl[:, c, tok], mwh[g][:, k, w], mwl[g][:, k, w],
                                          c == 0, c == DC - 1)
                        ins.then_inc(m_gu, 1)
                    j = i - 1
                    if 0 <= j < STEPS:
                        pe.wait_ge(m_act, j + 1)
                        if j >= 2:
                            pe.wait_ge(m_tlo, j - 1)
                        for e in range(EG):
                            ins = pe.transpose(MT[j % 2][:, e * P:(e + 1) * P], mac[j % 2][:, e * P:(e + 1) * P], ident[:])
                        ins.then_inc(m_tps, 1)
                    o = i - 2
                    if 0 <= o < STEPS:
                        pe.wait_ge(m_tlo, o + 1)
                        if o >= 2:
                            pe.wait_ge(m_x, o - 1)
                        for e in range(EG):
                            col, w = slice(e * P, (e + 1) * P), slice(e * D, (e + 1) * D)
                            ins = mm3(pe, MO[o % 2][:, 0:D], math_[o % 2][:, col], matl[o % 2][:, col],
                                      mwh[o // TT][:, W2, w], mwl[o // TT][:, W2, w], e == 0, e == EG - 1)
                        ins.then_inc(m_out, 1)
                end_turn(pe, "pe", moe_turn, moe_loop)

        @part(act_parts, "moe")
        def _(act, b):
            act.wait_ge(m_first, M_LOADS)
            with act.Fori(0, TURNS) as p:
                act.activation(mwh[0][:], mraw[0][:], ACT.Copy).then_inc(m_hi, 1)
                for i in range(STEPS + 1):
                    if i < STEPS:
                        act.wait_ge(m_gu, i + 1)
                        if i >= 2:
                            act.wait_ge(m_gate, i - 1)
                        act.activation(mth[i % 2][:], MG[i % 2], ACT.Tanh, scale=0.5).then_inc(m_tanh, 1)
                    j = i - 1
                    if 0 <= j < STEPS:
                        act.wait_ge(m_tps, j + 1)
                        if j >= 2:
                            act.wait_ge(m_out, j - 1)
                        act.activation(math_[j % 2][:], MT[j % 2], ACT.Copy).then_inc(m_thi, 1)
                end_turn(act, "act", moe_turn, moe_loop)

        @part(dve_parts, "moe")
        def _(dve, b):
            with dve.Fori(0, TURNS) as p:
                dve.wait_ge(m_hi, 1)
                dve.tensor_tensor(mwl[0][:], mraw[0][:], mwh[0][:].bitcast(F32), ALU.subtract).then_inc(m_lo, 1)
                for i in range(STEPS + 2):
                    if i < STEPS:
                        g, t = i // TT, i % TT
                        dve.wait_ge(m_tanh, i + 1)
                        if i >= 2:
                            dve.wait_ge(m_act, i - 1)
                        dve.scalar_tensor_tensor(mga[i % 2][:], mth[i % 2][:], 1.0, MG[i % 2], ALU.add, ALU.mult
                                                 ).then_inc(m_gate, 1)
                        dve.wait_ge(m_gate, i + 1)
                        if i >= 2:
                            dve.wait_ge(m_tps, i - 1)
                        for e in range(EG):
                            col = slice(e * P, (e + 1) * P)
                            ins = dve.scalar_tensor_tensor(mac[i % 2][:, col], mga[i % 2][:, col], SC[:, t, g * EG + e:g * EG + e + 1],
                                                           MU[i % 2][:, col], ALU.mult, ALU.mult)
                        ins.then_inc(m_act, 1)
                    j = i - 1
                    if 0 <= j < STEPS:
                        dve.wait_ge(m_thi, j + 1)
                        dve.tensor_tensor(matl[j % 2][:], MT[j % 2], math_[j % 2][:].bitcast(F32), ALU.subtract
                                          ).then_inc(m_tlo, 1)
                    o = i - 2
                    if 0 <= o < STEPS:
                        t = o % TT
                        dve.wait_ge(m_out, o + 1)
                        if o >= TT:
                            dve.wait_ge(m_x, o - TT + 1)
                        dve.scalar_tensor_tensor(X[:, t, :], MO[o % 2][:, 0:D], tg[:, LAYERS + 1:LAYERS + 2],
                                                 X[:, t, :], ALU.mult, ALU.add).then_inc(m_x, 1)
                dve.tensor_copy(SC[:, :, 0:GPT * EG], SC[:, :, EXPERTS - GPT * EG:])
                end_turn(dve, "dve", moe_turn, moe_loop)

        next_layer()
        with buffers():
            XFL = sb("latents_t", [P, DC, N])
        ln_stage("ln2x", XF=XFL, gamma=2)
        Y2 = latent_attention(2, 16, [("L2_xattn_Wq", "cols", 0), ("L2_xattn_Wkv", "cols", 0),
                                      ("L2_xattn_Wkv", "cols", INNER), ("L2_xattn_Wout", "rows", 0)],
                              (CNTh, CNTl), None, None, None, mask="mask_BxS2_bf1")
        out2_steps = signal("out2_steps")

        @part(dve_parts, "out2")
        def _(dve, b):
            chain = Chain(dve, out2_steps)
            norm_stats(dve, chain, lambda t: Y2[:, t, :], TT)
            for t in range(TT):
                ins = dve.tensor_scalar(Y2[:, t, :], Y2[:, t, :], rstd[:, t:t + 1], nmr[:, t:t + 1], ALU.mult, ALU.add)
            chain.step(ins)
            chain.settle()
            all_rows = [P, TT, D]
            chain.step(dve.tensor_tensor(Y2[:], Y2[:], rowb[:, GO, :].unsqueeze(1).broadcast_to(all_rows), ALU.mult))
            chain.step(dve.tensor_tensor(X[:], X[:], rowb[:, BO, :].unsqueeze(1).broadcast_to(all_rows), ALU.add))
            chain.settle()
            chain.step(dve.tensor_tensor(X[:], X[:], Y2[:], ALU.add))

        WR, WK, WV = range(3)
        rwkv_scope = ExitStack()
        scope = rwkv_scope
        XF = sb("x_t", [P, DC, N])
        kraw = sb("mix_w_raw", [P, 3, DC * D])
        kwh = sb("mix_w_hi", [P, 3, DC * D], F32R)
        kwl = sb("mix_w_lo", [P, 3, DC * D], F32R)
        SH = [sb(f"mixed{m}", [P, DC, N]) for m in range(2)]
        SHh = [sb(f"mixed_hi{m}", [P, DC, N], F32R) for m in range(2)]
        SHl = [sb(f"mixed_lo{m}", [P, DC, N], F32R) for m in range(2)]
        KR = sb("k_relu", [P, DC, N])
        K2h = sb("k_squared_hi", [P, DC, N], F32R)
        K2l = sb("k_squared_lo", [P, DC, N], F32R)
        RT = sb("r_tanh", [P, TT, D])
        rwkv_scope.close()
        scope = life
        ln_stage("ln2f", XF=XF)

        MIX = [(m, c, h) for m in (1, 0) for c in range(DC) for h in range(NHALF)]
        kw_in = signal("mix_w_in")
        kw_split = signal("mix_w_split")
        s_zero = signal("mix_first_token_zero")
        s_prev = signal("mix_prev")
        s_mix = signal("mix_done")
        s_hi = signal("mix_hi")
        s_lo = signal("mix_lo")
        k_ps = signal("mix_k")
        k_relu = signal("mix_k_relu")
        k_hi = signal("mix_k_hi")
        k_sq = signal("mix_k_squared")
        k_lo = signal("mix_k_lo")
        r_ps = signal("mix_r")
        r_tanh = signal("mix_r_tanh")
        v_ps = signal("mix_v")
        v_gated = signal("mix_v_gated")
        v_x = signal("mix_residual")

        @part(sp_parts, "rwkv")
        def _(sp, b):
            for k, name in ((WR, "L2_ffn_rT"), (WK, "L2_ffn_kT"), (WV, "L2_ffn_vT")):
                sp.dma_start(kraw[:, k, :].rearrange("p (c d) -> p c d", c=DC),
                             A[name].rearrange("(c p) d -> p c d", p=P)).then_inc(kw_in, 16)

        @part(pool_parts, "rwkv")
        def _(pool, b):
            for m in range(2):
                ins = pool.memset(SH[m][:, :, 0:1], 0.0)
            ins.then_inc(s_zero, 1)
            pool.wait_ge(kw_in, 48)
            hi_of(pool, kwh[:], kraw[:]).then_inc(kw_split, 1)
            pool.wait_ge(kw_split, 1)
            pool.tensor_tensor(kwl[:], kraw[:], kwh[:].bitcast(F32), ALU.subtract).then_inc(kw_split, 1)

        @part(act_parts, "rwkv")
        def _(act, b):
            for m, c, h in MIX:
                a, z = max(h * HALF, 1), (h + 1) * HALF
                act.activation(SH[m][:, c, a:z], XF[:, c, a - 1:z - 1], ACT.Copy, scale=omm[:, c, m:m + 1]
                               ).then_inc(s_prev, 1)
            for q, (m, c, h) in enumerate(MIX):
                cols = slice(h * HALF, (h + 1) * HALF)
                act.wait_ge(s_mix, q + 1)
                act.activation(SHh[m][:, c, cols], SH[m][:, c, cols], ACT.Copy).then_inc(s_hi, 1)
            for q, (c, h) in enumerate(QUADS):
                cols = slice(h * HALF, (h + 1) * HALF)
                act.wait_ge(k_ps, q + 1)
                act.activation(KR[:, c, cols], BANKS[q], ACT.Relu).then_inc(k_relu, 1)
                act.wait_ge(k_relu, q + 1)
                act.activation(K2h[:, c, cols], KR[:, c, cols], ACT.Square).then_inc(k_hi, 1)
            for q in range(4):
                act.wait_ge(r_ps, q + 1)
                act.activation(RT[:, 2 * q:2 * q + 2, :].rearrange("p t d -> p (t d)"), BANKS[4 + q], ACT.Tanh,
                               scale=0.5).then_inc(r_tanh, 1)

        @part(dve_parts, "rwkv")
        def _(dve, b):
            dve.wait_ge(s_zero, 1)
            for q, (m, c, h) in enumerate(MIX):
                cols = slice(h * HALF, (h + 1) * HALF)
                dve.wait_ge(s_prev, q + 1)
                dve.scalar_tensor_tensor(SH[m][:, c, cols], XF[:, c, cols], mus[:, c, m:m + 1], SH[m][:, c, cols],
                                         ALU.mult, ALU.add).then_inc(s_mix, 1)
            for q, (m, c, h) in enumerate(MIX):
                cols = slice(h * HALF, (h + 1) * HALF)
                dve.wait_ge(s_hi, q + 1)
                dve.tensor_tensor(SHl[m][:, c, cols], SH[m][:, c, cols], SHh[m][:, c, cols].bitcast(F32),
                                  ALU.subtract).then_inc(s_lo, 1)
            for q, (c, h) in enumerate(QUADS):
                cols = slice(h * HALF, (h + 1) * HALF)
                dve.wait_ge(k_hi, q + 1)
                dve.tensor_tensor(KR[:, c, cols], KR[:, c, cols], KR[:, c, cols], ALU.mult).then_inc(k_sq, 1)
                dve.wait_ge(k_sq, q + 1)
                dve.tensor_tensor(K2l[:, c, cols], KR[:, c, cols], K2h[:, c, cols].bitcast(F32), ALU.subtract
                                  ).then_inc(k_lo, 1)
            for q in range(4):
                rt = RT[:, 2 * q:2 * q + 2, :].rearrange("p t d -> p (t d)")
                xt = X[:, 2 * q:2 * q + 2, :].rearrange("p t d -> p (t d)")
                dve.wait_ge(v_ps, q + 1)
                dve.wait_ge(r_tanh, q + 1)
                dve.scalar_tensor_tensor(rt, rt, 1.0, BANKS[q], ALU.add, ALU.mult).then_inc(v_gated, 1)
                dve.wait_ge(v_gated, q + 1)
                dve.scalar_tensor_tensor(xt, rt, htg2[:, 0:1], xt, ALU.mult, ALU.add).then_inc(v_x, 1)

        @part(pe_parts, "rwkv")
        def _(pe, b):
            pe.wait_ge(kw_split, 2)
            pe.wait_ge(s_lo, 4)
            for q, (d, h) in enumerate(QUADS):
                cols = slice(h * HALF, (h + 1) * HALF)
                for c in range(DC):
                    w = slice(c * D + d * P, c * D + (d + 1) * P)
                    ins = mm3(pe, BANKS[q], kwh[:, WK, w], kwl[:, WK, w], SHh[1][:, c, cols], SHl[1][:, c, cols],
                              c == 0, c == DC - 1)
                ins.then_inc(k_ps, 1)
            pe.wait_ge(s_lo, 8)
            for x_h, x_l, wi, b0, done in ((SHh[0], SHl[0], WR, 4, r_ps), (K2h, K2l, WV, 0, v_ps)):
                if done is v_ps:
                    pe.wait_ge(k_lo, 4)
                for t in range(TT):
                    tok = slice(t * P, (t + 1) * P)
                    for c in range(DC):
                        w = slice(c * D, (c + 1) * D)
                        ins = mm3(pe, BANKS[b0 + t // 2][:, (t % 2) * D:(t % 2 + 1) * D], x_h[:, c, tok],
                                  x_l[:, c, tok], kwh[:, wi, w], kwl[:, wi, w], c == 0, c == DC - 1)
                    if t % 2:
                        ins.then_inc(done, 1)

        next_layer()
        ln_stage("ln3x")
        with buffers():
            context_attention(3, 8, [by_cols("L3_xattn_wkT"), by_cols("L3_xattn_wvT"), by_rows("L3_xattn_wq")],
                              (D // HEADS) ** -0.5, 3, False, None)

        PAIRS = AE // 2
        WIDE = AE * AH
        ae_scope = ExitStack()
        scope = ae_scope
        XFA = sb("x_t_full", [P, DC, N])
        eraw = sb("enc_raw", [P, DC, WIDE])
        eh = sb("enc_hi", [P, DC, WIDE], F32R)
        el = sb("enc_lo", [P, DC, WIDE], F32R)
        draw = sb("dec_raw", [P, PAIRS, 2, D])
        dh = sb("dec_hi", [P, AE, D], F32R)
        dl = sb("dec_lo", [P, AE, D], F32R)
        hid = [sb(f"enc_hidden{i}", [P, HALF]) for i in range(2)]
        hidh = [sb(f"enc_hidden_hi{i}", [P, HALF], F32R) for i in range(2)]
        hidl = [sb(f"enc_hidden_lo{i}", [P, HALF], F32R) for i in range(2)]
        diff = [sb(f"recon_diff{i}", [P, HALF]) for i in range(2)]
        sqr = sb("recon_squares", [P, HALF])
        loss4 = sb("loss_parts", [P, AE, DC * NHALF])
        loss1 = sb("loss_sums", [P, AE])
        loss = sb("losses", [P, AE])
        lmin = sb("loss_min", [P, 1])
        iota = sb("adapter_numbers", [P, AE])
        iotab = sb("adapter_numbers_more", [P, AE])
        hot = sb("adapter_one_hot", [P, AE])
        top1 = sb("adapter_top1", [P, 1])
        adp = sb("adapter_connected", [P, 1])
        wrap = sb("adapter_wrap", [P, 1])
        braw = sb("base_raw", [P, DC, D])
        bh = sb("base_hi", [P, DC, D], F32R)
        bl = sb("base_lo", [P, DC, D], F32R)
        downs = sb("down_all", [P, DC, AE, AH])
        ups = sb("up_all", [P, AE, D])
        bups = sb("b_up_all", [P, AE, D])
        down = [sb(f"down{i}", [P, DC, AH]) for i in range(2)]
        up = [sb(f"up{i}", [P, D]) for i in range(2)]
        bup = [sb(f"b_up{i}", [P, D]) for i in range(2)]
        bdn = [sb(f"b_down{i}", [P, 1]) for i in range(2)]
        downh = sb("down_hi", [P, DC, 2, AH], F32R)
        downl = sb("down_lo", [P, DC, 2, AH], F32R)
        uph = sb("up_hi", [P, D], F32R)
        upl = sb("up_lo", [P, D], F32R)
        mid = sb("mid", [P, N])
        mids = sb("mid_stack", [P, N], F32R)
        ae_scope.close()
        scope = life
        ln_stage("ln3f", XF=XFA)

        UNITS3 = [(k, h) for k in range(PAIRS) for h in range(NHALF)]
        NU = len(UNITS3)
        ew_in = signal("enc_in")
        dw_in = signal("dec_in")
        ae_zero = signal("dec_zeros")
        ew_split = signal("enc_dec_split")
        e_ps = signal("enc_ready")
        e_relu = signal("enc_relu")
        e_hi = signal("enc_hidden_hi_ready")
        e_lo = signal("enc_hidden_lo_ready")
        d_ps = signal("dec_ready")
        d_diff = signal("dec_diff")
        d_sq = signal("dec_squared")
        iota_set = signal("adapter_numbers_set")
        l_sum = signal("loss_summed")
        l_all = signal("loss_over_partitions")
        a_steps = signal("adapter_steps")

        @part(sp_parts, "route")
        def _(sp, b):
            for c in range(DC):
                sp.dma_start(eraw[:, c, :].rearrange("p (n h) -> p n h", n=AE),
                             A["L3_ffn_W_enc"].rearrange("n (c p) h -> c p n h", p=P)[c]).then_inc(ew_in, 16)
            for r in range(2):
                sp.dma_start(draw[r * AH:(r + 1) * AH, :, r, :],
                             A["L3_ffn_W_dec"].rearrange("(k r) h d -> r h k d", r=2)[r]).then_inc(dw_in, 16)
            sp.wait_ge(ew_in, 16 * DC)

        @part(pool_parts, "route")
        def _(pool, b):
            for r in range(2):
                pool.memset(draw[r * AH:(r + 1) * AH, :, 1 - r, :], 0.0).then_inc(ae_zero, 1)
                pool.wait_ge(ae_zero, r + 1)
            pool.wait_ge(ew_in, 16 * DC)
            hi_of(pool, eh[:], eraw[:]).then_inc(ew_split, 1)
            pool.wait_ge(ew_split, 1)
            pool.tensor_tensor(el[:], eraw[:], eh[:].bitcast(F32), ALU.subtract).then_inc(ew_split, 1)
            pool.wait_ge(dw_in, 32)
            dr = draw[:].rearrange("p k r d -> p (k r) d")
            hi_of(pool, dh[:], dr).then_inc(ew_split, 1)
            pool.wait_ge(ew_split, 3)
            pool.tensor_tensor(dl[:], dr, dh[:].bitcast(F32), ALU.subtract).then_inc(ew_split, 1)
            for n in range(AE):
                pool.memset(iota[:, n:n + 1], float(n)).then_inc(iota_set, 1)

        @part(pe_parts, "route")
        def _(pe, b):
            pe.wait_ge(ew_split, 2)
            for u in range(NU + 1):
                if u < NU:
                    k, h = UNITS3[u]
                    cols = slice(h * HALF, (h + 1) * HALF)
                    if u >= 2:
                        pe.wait_ge(e_relu, u - 1)
                    for c in range(DC):
                        w = slice(k * P, (k + 1) * P)
                        ins = mm3(pe, BANKS[u % 2], eh[:, c, w], el[:, c, w], XTh[:, c, cols], XTl[:, c, cols],
                                  c == 0, c == DC - 1)
                    ins.then_inc(e_ps, 1)
                v = u - 1
                if v >= 0:
                    k, h = UNITS3[v]
                    if v == 0:
                        pe.wait_ge(ew_split, 4)
                    pe.wait_ge(e_lo, v + 1)
                    for q in range(4):
                        n, c = 2 * k + q // 2, q % 2
                        if v:
                            pe.wait_ge(d_diff, 4 * (v - 1) + q + 1)
                        w = slice(c * P, (c + 1) * P)
                        mm3(pe, BANKS[2 + q], dh[:, n, w], dl[:, n, w], hidh[v % 2][:], hidl[v % 2][:], True, True
                            ).then_inc(d_ps, 1)
            pe.wait_ge(l_sum, 1)
            pe.matmul(BANKS[6][:, 0:AE], ones[:], loss1[:], start=True, stop=True).then_inc(l_all, 1)

        @part(act_parts, "route")
        def _(act, b):
            for u in range(NU + 1):
                if u < NU:
                    k, h = UNITS3[u]
                    act.wait_ge(e_ps, u + 1)
                    if u >= 2:
                        act.wait_ge(e_lo, u - 1)
                    act.activation(hid[u % 2][:], BANKS[u % 2], ACT.Relu, bias=benc[:, k:k + 1]).then_inc(e_relu, 1)
                    act.wait_ge(e_relu, u + 1)
                    if u >= 2:
                        act.wait_ge(d_ps, 4 * (u - 1))
                    act.activation(hidh[u % 2][:], hid[u % 2][:], ACT.Copy).then_inc(e_hi, 1)
                v = u - 1
                if v >= 0:
                    k, h = UNITS3[v]
                    for q in range(4):
                        n, c = 2 * k + q // 2, q % 2
                        s = 4 * v + q
                        act.wait_ge(d_diff, s + 1)
                        if s:
                            act.wait_ge(d_sq, s)
                        act.activation(sqr[:], diff[s % 2][:], ACT.Square,
                                       accum_out=loss4[:, n, c * NHALF + h:c * NHALF + h + 1]).then_inc(d_sq, 1)

        @part(dve_parts, "route")
        def _(dve, b):
            for u in range(NU + 1):
                if u < NU:
                    dve.wait_ge(e_hi, u + 1)
                    if u >= 2:
                        dve.wait_ge(d_ps, 4 * (u - 1))
                    dve.tensor_tensor(hidl[u % 2][:], hid[u % 2][:], hidh[u % 2][:].bitcast(F32), ALU.subtract
                                      ).then_inc(e_lo, 1)
                v = u - 1
                if v >= 0:
                    k, h = UNITS3[v]
                    for q in range(4):
                        n, c = 2 * k + q // 2, q % 2
                        s = 4 * v + q
                        dve.wait_ge(d_ps, s + 1)
                        if s >= 2:
                            dve.wait_ge(d_sq, s - 1)
                        dve.scalar_tensor_tensor(diff[s % 2][:], BANKS[2 + q], bdec[:, n, c:c + 1],
                                                 XFA[:, c, h * HALF:(h + 1) * HALF], ALU.add, ALU.subtract
                                                 ).then_inc(d_diff, 1)
            dve.wait_ge(d_sq, 4 * NU)
            dve.tensor_reduce(loss1[:], loss4[:], AX.X, ALU.add).then_inc(l_sum, 1)
            chain = Chain(dve, a_steps)
            dve.wait_ge(l_all, 1)
            dve.wait_ge(iota_set, AE)
            chain.step(dve.tensor_copy(loss[:], BANKS[6][:, 0:AE]))
            chain.step(dve.tensor_scalar(iotab[:], iota[:], float(-AE), None, ALU.add))
            chain.settle()
            chain.step(dve.tensor_reduce(lmin[:], loss[:], AX.X, ALU.min))
            chain.settle()
            chain.step(dve.scalar_tensor_tensor(hot[:], loss[:], lmin[:, 0:1], iotab[:], ALU.is_equal, ALU.mult))
            chain.settle()
            chain.step(dve.tensor_reduce(top1[:], hot[:], AX.X, ALU.min))
            chain.settle()
            chain.step(dve.scalar_tensor_tensor(hot[:], iotab[:], top1[:, 0:1], cidx[:], ALU.is_equal, ALU.mult))
            chain.settle()
            chain.step(dve.tensor_reduce(adp[:], hot[:], AX.X, ALU.add))
            chain.settle()
            chain.step(dve.tensor_scalar(wrap[:], adp[:], 0.0, float(AE), ALU.is_lt, ALU.mult))
            chain.settle()
            chain.step(dve.tensor_tensor(adp[:], adp[:], wrap[:], ALU.add))
            chain.settle()
            chain.step(dve.tensor_scalar(adp[:], adp[:], 0.0, float(AE - 1), ALU.max, ALU.min))
            chain.settle()
            chain.step(dve.tensor_scalar(hot[:], iota[:], adp[:, 0:1], None, ALU.is_equal))

        aw_in = signal("base_in")
        aw_sel_in = signal("adapters_in")
        aw_split = signal("base_split")
        pick = signal("adapter_picks")
        pick_hi = signal("adapter_hi")
        pick_lo = signal("adapter_lo")
        mid_ps = signal("mid_ready")
        mid_relu = signal("mid_relu")
        mid_hi = signal("mid_hi")
        mid_lo = signal("mid_lo")
        ad_ps = signal("adapted_ready")
        ad_row = signal("adapted_bias")
        ad_x = signal("adapted_residual")

        @part(sp_parts, "adapt")
        def _(sp, b):
            sp.dma_start(braw[:], A["L3_ffn_W_base"].rearrange("(c p) e -> p c e", p=P)).then_inc(aw_in, 16)
            for c in range(DC):
                sp.dma_start(downs[:, c, :, :], A["L3_ffn_W_down"].rearrange("n (c p) h -> c p n h", p=P)[c]
                             ).then_inc(aw_sel_in, 16)
            for r in range(2):
                sp.dma_start(ups[r * AH:(r + 1) * AH, :, :], A["L3_ffn_W_up"].rearrange("n h d -> h n d")
                             ).then_inc(aw_sel_in, 16)
            sp.dma_start(bups[:].rearrange("p n d -> p (n d)"), A["L3_ffn_b_up"].rearrange(
                "(a n) d -> a (n d)", a=1).broadcast_to([P, AE * D])).then_inc(aw_sel_in, 16)

        @part(pool_parts, "adapt")
        def _(pool, b):
            pool.wait_ge(aw_in, 16)
            hi_of(pool, bh[:], braw[:]).then_inc(aw_split, 1)
            pool.wait_ge(aw_split, 1)
            pool.tensor_tensor(bl[:], braw[:], bh[:].bitcast(F32), ALU.subtract).then_inc(aw_split, 1)

        @part(dve_parts, "adapt")
        def _(dve, b):
            chain = Chain(dve, pick)
            dve.wait_ge(aw_sel_in, 16 * (DC + 3))
            sources = [(down, lambda n: downs[:, :, n, :]), (up, lambda n: ups[:, n, :]),
                       (bup, lambda n: bups[:, n, :]), (bdn, lambda n: bdown[:, n:n + 1])]
            for n in range(AE):
                for dst, src in sources:
                    d_, own = dst[n % 2][:], hot[:, n:n + 1]
                    chain.step(dve.tensor_scalar(d_, src(n), own, None, ALU.mult) if n == 0 else
                               dve.scalar_tensor_tensor(d_, src(n), own, dst[(n + 1) % 2][:], ALU.mult, ALU.add))
                chain.settle()
            dve.wait_ge(pick_hi, 2)
            twice = down[1][:].unsqueeze(2).broadcast_to([P, DC, 2, AH])
            dve.tensor_tensor(downl[:], twice, downh[:].bitcast(F32), ALU.subtract).then_inc(pick_lo, 1)
            dve.tensor_tensor(upl[:], up[1][:], uph[:].bitcast(F32), ALU.subtract).then_inc(pick_lo, 1)
            gate = tg[:, 2 * LAYERS - 1:2 * LAYERS]
            dve.tensor_tensor(bup[0][:], bup[1][:], rowb[:, BBASE, :], ALU.add).then_inc(ad_row, 1)
            dve.wait_ge(ad_row, 1)
            dve.scalar_tensor_tensor(X[:], bup[0][:].unsqueeze(1).broadcast_to([P, TT, D]), gate, X[:],
                                     ALU.mult, ALU.add).then_inc(ad_row, 1)
            for h in range(NHALF):
                cols = slice(h * HALF, (h + 1) * HALF)
                dve.wait_ge(mid_hi, h + 1)
                dve.tensor_tensor(mids[AH:P, cols], mid[AH:P, cols], mids[AH:P, cols].bitcast(F32), ALU.subtract
                                  ).then_inc(mid_lo, 1)
            dve.wait_ge(ad_row, 2)
            for q in range(4):
                xt = X[:, 2 * q:2 * q + 2, :].rearrange("p t d -> p (t d)")
                dve.wait_ge(ad_ps, q + 1)
                dve.scalar_tensor_tensor(xt, BANKS[q], gate, xt, ALU.mult, ALU.add).then_inc(ad_x, 1)

        @part(act_parts, "adapt")
        def _(act, b):
            act.wait_ge(pick, 4 * AE)
            for r in range(2):
                ins = act.activation(downh[:, :, r, :], down[1][:], ACT.Copy)
            ins.then_inc(pick_hi, 1)
            act.activation(uph[:], up[1][:], ACT.Copy).then_inc(pick_hi, 1)
            for h in range(NHALF):
                cols = slice(h * HALF, (h + 1) * HALF)
                act.wait_ge(mid_ps, h + 1)
                act.activation(mid[:, cols], BANKS[6 + h], ACT.Relu, bias=bdn[1][:, 0:1]).then_inc(mid_relu, 1)
                act.wait_ge(mid_relu, h + 1)
                act.activation(mids[:, cols], mid[:, cols], ACT.Copy).then_inc(mid_hi, 1)

        @part(pe_parts, "adapt")
        def _(pe, b):
            pe.wait_ge(pick_lo, 2)
            for h in range(NHALF):
                cols = slice(h * HALF, (h + 1) * HALF)
                for c in range(DC):
                    ins = mm3(pe, BANKS[6 + h], downh[:, c, :, :].rearrange("p r h -> p (r h)"),
                              downl[:, c, :, :].rearrange("p r h -> p (r h)"),
                              XTh[:, c, cols], XTl[:, c, cols], c == 0, c == DC - 1)
                ins.then_inc(mid_ps, 1)
            pe.wait_ge(aw_split, 2)
            pe.wait_ge(mid_lo, 2)
            for t in range(TT):
                tok = slice(t * P, (t + 1) * P)
                acc = BANKS[t // 2][:, (t % 2) * D:(t % 2 + 1) * D]
                for c in range(DC):
                    mm3(pe, acc, XTh[:, c, tok], XTl[:, c, tok], bh[:, c, :], bl[:, c, :], c == 0, False)
                pe.matmul(acc, mids[:, tok], uph[:], start=False, stop=False)
                ins = pe.matmul(acc, mids[:, tok], upl[:], start=False, stop=True)
                if t % 2:
                    ins.then_inc(ad_ps, 1)
        next_layer()
        stored = signal("x_stored")

        @part(sp_parts, "store")
        def _(sp, b):
            sp.dma_start(out[bass.ds(b * N, N), :].rearrange("(t p) d -> p t d", p=P), X[:]
                         ).then_inc(stored, 16)
            sp.wait_ge(stored, 16)

        next_layer()

        block = life.enter_context(nc.Block())

        @block.sync
        def _(sp):
            sp_ternary(sp)
            sp_consts(sp)
            sp.wait_ge(const_set, 7)
            with sp.Fori(0, NB) as b:
                run(sp, "sp", b, sp_parts)

        @block.gpsimd
        def _(pool):
            pool_consts(pool)
            with pool.Fori(0, NB) as b:
                run(pool, "pool", b, pool_parts)

        @block.scalar
        def _(act):
            act_consts(act)
            with act.Fori(0, NB) as b:
                run(act, "act", b, act_parts)

        @block.vector
        def _(dve):
            dve_consts(dve)
            dve_ternary(dve)
            with dve.Fori(0, NB) as b:
                run(dve, "dve", b, dve_parts)

        @block.tensor
        def _(pe):
            pe.wait_ge(const_set, 7)
            pe_ternary(pe)
            with pe.Fori(0, NB) as b:
                run(pe, "pe", b, pe_parts)


_FLAT = {"x": (NB * N, D), "ctx_1024": (NB * J, D), "mask_BxSxS2_bk1": (NB * N, J)}
_TRANSPOSED = {"L0_xattn_Wq": "L0_xattn_WqT", "L0_ffn_w_gate": "L0_ffn_gT", "L0_ffn_w_up": "L0_ffn_uT",
               "L0_ffn_w_down": "L0_ffn_dT", "L1_ffn_gate_w": "L1_ffn_gateT", "L2_ffn_W_r": "L2_ffn_rT",
               "L2_ffn_W_k": "L2_ffn_kT", "L2_ffn_W_v": "L2_ffn_vT", "L3_xattn_wk": "L3_xattn_wkT",
               "L3_xattn_wv": "L3_xattn_wvT"}


def kernel(**inputs):
    import numpy as _np
    import concourse.bacc as _bacc
    from concourse import mybir as _mybir
    from concourse.bass_utils import run_bass_kernel_spmd as _run

    nc = _bacc.Bacc("TRN2", target_bir_lowering=False, num_devices=1)
    arrays, args = {}, {}
    for name, a in inputs.items():
        a = _np.asarray(a)
        if name in _FLAT:
            a = a.reshape(_FLAT[name])
        if name in _TRANSPOSED:
            name, a = _TRANSPOSED[name], a.T
        a = _np.ascontiguousarray(a)
        arrays[f"in_{name}_dram"] = a
        args[name] = nc.dram_tensor(f"in_{name}_dram", a.shape, _mybir.dt.from_np(a.dtype),
                                    kind="ExternalInput").ap()
    out = nc.dram_tensor("out_0_dram", (NB * N, D), F32, kind="ExternalOutput").ap()
    flamingo_kernel(nc, args, out)
    r = _run(nc, [arrays], core_ids=[0])
    return r.results[0]["out_0_dram"].reshape(NB, N, D)
```

```python
from contextlib import ExitStack, contextmanager

import concourse.bass as bass
from concourse import mybir

ALU = mybir.AluOpType
ACT = mybir.ActivationFunctionType
AX = mybir.AxisListType
F32 = mybir.dt.float32
F32R = mybir.dt.float32r
BF16 = mybir.dt.bfloat16
I32 = mybir.dt.int32
U8 = mybir.dt.uint8

P = 128
NB = 2
N = 1024
D = 256
DC = D // P
TT = N // P
HALF = 512
NHALF = N // HALF
J = 77
JP = J + 1
HEADS = 16
HJ = HEADS * JP
HJC = -(-HJ // P)
BANK_HEADS = [(0, 6), (6, 11), (11, 16)]
KEYS = N + J
KEYSP = N + JP
KC = TT + 1
DH = 64
EPS = 1e-5
MAGIC = 12582912.0
RSQRT_SEED = 1597463007.0
NEWTON = 3
MASKED = 2.0 ** 127
NEG_MAX = -3.4028234663852886e38
STAT_STEPS = 4 + 3 * NEWTON + 1
EXPERTS = 16
TOP_K = 4
INTER = 128
EG = 4
AE = 8
AH = 64
INNER = 1024
LAYERS = 4


class Chain:

    def __init__(self, eng, sem):
        self.eng, self.sem, self.n = eng, sem, 0

    def step(self, ins):
        ins.then_inc(self.sem, 1)
        self.n += 1

    def settle(self):
        self.eng.wait_ge(self.sem, self.n)


def flamingo_kernel(nc, A, out):
    with ExitStack() as life:
        def sb(name, shape, dt=F32):
            return scope.enter_context(nc.sbuf_tensor(name, shape, dt))

        sem_scope = ExitStack()
        layer_signals = []

        def semaphore(name):
            return sem_scope.enter_context(nc.semaphore(name))

        def signal(name):
            s = semaphore(name)
            layer_signals.append(s)
            return s

        @contextmanager
        def buffers():
            nonlocal scope
            with ExitStack() as scope:
                yield
            scope = life

        scope = life
        X = sb("X", [P, TT, D])
        XN = sb("XN", [P, TT, D])
        XTh = sb("XTh", [P, DC, N], F32R)
        XTl = sb("XTl", [P, DC, N], F32R)
        C = sb("C", [P, D])
        CN = sb("CN", [P, D])
        CTh = sb("CTh", [P, DC, JP], F32R)
        CTl = sb("CTl", [P, DC, JP], F32R)
        CNT = sb("CNT", [P, DC, JP])
        CNTh = sb("CNTh", [P, DC, JP], F32R)
        CNTl = sb("CNTl", [P, DC, JP], F32R)
        ident = sb("ident", [P, P])
        identb = sb("identb", [P, P], BF16)
        ones = sb("ones", [P, P])
        gates = sb("gates", [P, 2 * LAYERS])
        tg = sb("tg", [P, 2 * LAYERS])
        stats = sb("stats", [P, TT, 6])
        mv = sb("mv", [P, TT, 2])
        var = sb("var", [P, TT])
        rstd = sb("rstd", [P, TT])
        ntmp = sb("ntmp", [P, TT])
        nmr = sb("nmr", [P, TT])
        gl = sb("gl", [P, DC, 4])
        mus = sb("mus", [P, DC, 2])
        htg2 = sb("half_gate2", [P, 1])
        omm = sb("omm", [P, DC, 2])
        benc = sb("b_enc_cols", [P, AE // 2])
        bdec = sb("b_dec_cols", [P, AE, DC])
        bdown = sb("b_down_cols", [P, AE])
        cidx_i = sb("connected_i", [P, AE], I32)
        cidx = sb("connected", [P, AE])
        rowb = sb("rowb", [P, 6, D])
        BO0, BO1, GO, BO, BBASE, SPARE = range(6)

        wq = [sb(f"ternary{n}", [P, DC * INNER], BF16) for n in range(3)]
        wabs = sb("weight_abs_sums", [P, 3])
        wmean = sb("weight_mean", [P, 3])
        winv = sb("weight_inv_mean", [P, 3])

        PA = life.enter_context(nc.psum_tensor("PA", [P, 3 * HALF], F32))
        PB = life.enter_context(nc.psum_tensor("PB", [P, 3 * HALF], F32))
        PT = life.enter_context(nc.psum_tensor("PT", [P, HALF], F32))
        PV = life.enter_context(nc.psum_tensor("PV", [P, HALF], F32))
        BANKS = [PA[:, 0:512], PA[:, 512:1024], PA[:, 1024:1536],
                 PB[:, 0:512], PB[:, 512:1024], PB[:, 1024:1536], PT[:, :], PV[:, :]]

        LAYER_STAGES = [["load", "ln0x", "prep0", "attn0", "ln0f", "bitq", "bit"],
                        ["ln1x", "attn1", "ln1f", "router", "moe"],
                        ["ln2x", "attn2", "out2", "ln2f", "rwkv"],
                        ["ln3x", "prep3", "attn3", "ln3f", "route", "adapt"]]
        LAYER_STAGES.append(["store"])
        ends = {k: life.enter_context(nc.semaphore(f"{k}_stage_end")) for k in ("pe", "act", "dve", "pool", "sp")}

        def turn_signals(name):
            return (semaphore(f"{name}_arrived"), {k: semaphore(f"{name}_go_{k}") for k in ends if k != "pool"})

        def end_turn(eng, me, turn, signals):
            arrived, go = turn
            eng.drain().then_inc(arrived, 1)
            if me == "pool":
                eng.wait_ge(arrived, len(ends))
                for s in (*signals, arrived):
                    eng.sem_clear(s)
                for k in go:
                    eng.sem_inc(go[k], 1)
            else:
                eng.wait_ge(go[me], 1)
                eng.sem_clear(go[me])

        layer_turn = (life.enter_context(nc.semaphore("layer_arrived")),
                      {k: life.enter_context(nc.semaphore(f"layer_go_{k}")) for k in ends if k != "pool"})
        signals_of = []

        def next_layer():
            nonlocal sem_scope, layer_signals
            signals_of.append(layer_signals + list(ends.values()))
            sem_scope.close()
            sem_scope, layer_signals = ExitStack(), []

        def run(eng, me, b, parts):
            for stages, signals in zip(LAYER_STAGES, signals_of[:len(LAYER_STAGES) - 1] + signals_of[-1:]):
                for s, name in enumerate(stages):
                    if s:
                        for other in ends:
                            if other != me:
                                eng.wait_ge(ends[other], s)
                    if name in parts:
                        parts[name](eng, b)
                    eng.drain().then_inc(ends[me], 1)
                end_turn(eng, me, layer_turn, signals)

        pe_parts, act_parts, dve_parts, pool_parts, sp_parts = {}, {}, {}, {}, {}

        def part(table, name):
            def keep(f):
                table[name] = f
                return f
            return keep

        def mm3(pe, acc, lh, ll, rh, rl, first, last):
            pe.matmul(acc, lh, rh, start=first, stop=False)
            pe.matmul(acc, ll, rh, start=False, stop=False)
            return pe.matmul(acc, lh, rl, start=False, stop=last)

        const_dma = life.enter_context(nc.semaphore("const_loaded"))
        const_set = life.enter_context(nc.semaphore("const_set"))
        omm_set = life.enter_context(nc.semaphore("omm_set"))
        tg_set = life.enter_context(nc.semaphore("tg_set"))

        def col(ap):
            return ap.rearrange("(c p) -> p c", p=P)

        const_loads = [
            (gates[:, 0:LAYERS], A["g_xattn"].rearrange("(a n) -> a n", a=1).broadcast_to([P, LAYERS])),
            (gates[:, LAYERS:], A["g_ffn"].rearrange("(a n) -> a n", a=1).broadcast_to([P, LAYERS])),
            (gl[:, :, 0], col(A["L2_xattn_g_x"])), (gl[:, :, 1], col(A["L2_xattn_b_x"])),
            (gl[:, :, 2], col(A["L2_xattn_g_l"])), (gl[:, :, 3], col(A["L2_xattn_b_l"])),
            (mus[:, :, 0], col(A["L2_ffn_mu_r"])), (mus[:, :, 1], col(A["L2_ffn_mu_k"])),
            (cidx_i[:], A["L3_ffn_connected_idx"].rearrange("(a n) -> a n", a=1).broadcast_to([P, AE])),
        ] + [(benc[r * AH:(r + 1) * AH, :], A["L3_ffn_b_enc"].rearrange("(k r) h -> r h k", r=2)[r])
             for r in range(2)
        ] + [(bdec[:, :, c], A["L3_ffn_b_dec"].rearrange("n (c p) -> c p n", p=P)[c]) for c in range(DC)
        ] + [(bdown[r * AH:(r + 1) * AH, :], A["L3_ffn_b_down"].rearrange("n h -> h n")) for r in range(2)
        ] + [(rowb[:, k, :], A[name].rearrange("(a n) -> a n", a=1).broadcast_to([P, D]))
             for k, name in ((BO0, "L0_xattn_bo"), (BO1, "L1_xattn_bo"), (GO, "L2_xattn_g_o"),
                             (BO, "L2_xattn_b_o"), (BBASE, "L3_ffn_b_base"))]

        def sp_consts(sp):
            for dst, src in const_loads:
                sp.dma_start(dst, src, allow_slow_non_contiguous=True).then_inc(const_dma, 16)

        def pool_consts(pool):
            pool.memset(ident[:], 0.0).then_inc(const_set, 1)
            pool.memset(ones[:], 1.0).then_inc(const_set, 1)
            pool.memset(C[:], 0.0).then_inc(const_set, 1)
            pool.memset(CN[:], 0.0).then_inc(const_set, 1)
            pool.memset(CNT[:], 0.0).then_inc(const_set, 1)
            pool.wait_ge(const_set, 5)
            pool.affine_select(out=ident[:], in_=ident[:], compare_op=ALU.not_equal, fill=1.0, base=0,
                               pattern=[[-1, P]], channel_multiplier=1).then_inc(const_set, 1)
            pool.wait_ge(const_set, 6)
            pool.tensor_copy(identb[:], ident[:]).then_inc(const_set, 1)

        def act_consts(act):
            act.wait_ge(const_dma, 16 * len(const_loads))
            act.activation(tg[:], gates[:], ACT.Tanh).then_inc(tg_set, 1)

        def dve_consts(dve):
            dve.wait_ge(const_dma, 16 * len(const_loads))
            dve.tensor_scalar(omm[:], mus[:], -1.0, 1.0, ALU.mult, ALU.add).then_inc(omm_set, 1)
            dve.wait_ge(tg_set, 1)
            dve.tensor_scalar(htg2[:], tg[:, LAYERS + 2:LAYERS + 3], 0.5, None, ALU.mult).then_inc(omm_set, 1)
            dve.tensor_copy(cidx[:], cidx_i[:]).then_inc(omm_set, 1)
            for k, g in ((BO0, 0), (BO1, 1), (GO, 2), (BO, 2)):
                dve.tensor_scalar(rowb[:, k, :], rowb[:, k, :], tg[:, g:g + 1], None,
                                  ALU.mult).then_inc(omm_set, 1)

        load_x = signal("x_loaded")
        load_c = signal("ctx_loaded")
        CTX_STEPS = STAT_STEPS + 1
        ctx_chain = signal("ctx_norm_steps")
        ctx_ps = signal("ctx_transposed")
        ctx_hi = signal("ctx_hi")
        ctx_lo = signal("ctx_lo")

        def norm_stats(dve, chain, src, tiles, rows=P):
            for t in range(tiles):
                ins = dve.bn_stats(stats[0:rows, t, :], src(t))
            chain.step(ins)
            chain.settle()
            for t in range(tiles):
                ins = dve.bn_aggr(mv[0:rows, t, :], stats[0:rows, t, :])
            chain.step(ins)
            chain.settle()
            v, y, w = var[0:rows, 0:tiles], rstd[0:rows, 0:tiles], ntmp[0:rows, 0:tiles]
            chain.step(dve.tensor_scalar(v, mv[0:rows, 0:tiles, 1], EPS, None, ALU.add))
            chain.settle()
            chain.step(dve.tensor_scalar(y.bitcast(I32), v.bitcast(I32), -0.5, RSQRT_SEED, ALU.mult, ALU.add))
            chain.settle()
            for _ in range(NEWTON):
                chain.step(dve.tensor_tensor(w, y, y, ALU.mult))
                chain.settle()
                chain.step(dve.scalar_tensor_tensor(w, w, -0.5, v, ALU.mult, ALU.mult))
                chain.settle()
                chain.step(dve.scalar_tensor_tensor(y, w, 1.5, y, ALU.add, ALU.mult))
                chain.settle()
            chain.step(dve.scalar_tensor_tensor(nmr[0:rows, 0:tiles], mv[0:rows, 0:tiles, 0], -1.0, y,
                                                ALU.mult, ALU.mult))
            chain.settle()

        @part(sp_parts, "load")
        def _(sp, b):
            sp.dma_start(X[:], A["x"][bass.ds(b * N, N), :].rearrange("(t p) d -> p t d", p=P)
                         ).then_inc(load_x, 16)
            sp.dma_start(C[0:J, :], A["ctx_1024"][bass.ds(b * J, J), :]).then_inc(load_c, 16)
            sp.wait_ge(load_x, 16)

        @part(dve_parts, "load")
        def _(dve, b):
            dve.wait_ge(load_c, 16)
            chain = Chain(dve, ctx_chain)
            norm_stats(dve, chain, lambda t: C[0:J, :], 1, J)
            chain.step(dve.tensor_scalar(CN[0:J, :], C[0:J, :], rstd[0:J, 0:1], nmr[0:J, 0:1], ALU.mult, ALU.add))
            dve.wait_ge(ctx_hi, 1)
            dve.tensor_tensor(CTl[:, :, :], PA[:, 0:DC * JP].rearrange("p (c j) -> p c j", c=DC),
                              CTh[:, :, :].bitcast(F32), ALU.subtract).then_inc(ctx_lo, 1)
            dve.wait_ge(ctx_hi, 3)
            dve.tensor_tensor(CNTl[:, :, :], CNT[:, :, :], CNTh[:, :, :].bitcast(F32),
                              ALU.subtract).then_inc(ctx_lo, 1)

        @part(pe_parts, "load")
        def _(pe, b):
            pe.wait_ge(load_c, 16)
            for c in range(DC):
                ins = pe.transpose(PA[:, c * JP:(c + 1) * JP], C[0:JP, c * P:(c + 1) * P], ident[0:JP, 0:JP])
            ins.then_inc(ctx_ps, 1)
            pe.wait_ge(ctx_chain, CTX_STEPS)
            for c in range(DC):
                ins = pe.transpose(PB[:, c * JP:(c + 1) * JP], CN[0:JP, c * P:(c + 1) * P], ident[0:JP, 0:JP])
            ins.then_inc(ctx_ps, 1)

        @part(act_parts, "load")
        def _(act, b):
            act.wait_ge(ctx_ps, 1)
            act.activation(CTh[:, :, :], PA[:, 0:DC * JP].rearrange("p (c j) -> p c j", c=DC),
                           ACT.Copy).then_inc(ctx_hi, 1)
            act.wait_ge(ctx_ps, 2)
            for c in range(DC):
                ins = act.activation(CNT[:, c, 0:J], PB[:, c * JP:c * JP + J], ACT.Identity,
                                     scale=gl[:, c, 0:1], bias=gl[:, c, 1:2])
            ins.then_inc(ctx_hi, 1)
            act.wait_ge(ctx_hi, 2)
            act.activation(CNTh[:, :, :], CNT[:, :, :], ACT.Copy).then_inc(ctx_hi, 1)

        QUADS = [(c, h) for c in range(DC) for h in range(NHALF)]
        LN_STEPS = STAT_STEPS + 1

        def apply_norm(dve, chain, src):
            for t in range(TT):
                ins = dve.tensor_scalar(XN[:, t, :], src[:, t, :], rstd[:, t:t + 1], nmr[:, t:t + 1],
                                        ALU.mult, ALU.add)
            chain.step(ins)

        def ln_stage(name, feature_major=True, XF=None, gamma=None):
            steps = LN_STEPS * (2 if gamma is not None else 1)
            chain_of = signal(name + "_steps")
            ps = signal(name + "_transposed")
            full = signal(name + "_full") if XF is not None else None
            hi = signal(name + "_hi")
            lo = signal(name + "_lo")

            @part(dve_parts, name)
            def _(dve, b):
                chain = Chain(dve, chain_of)
                norm_stats(dve, chain, lambda t: X[:, t, :], TT)
                apply_norm(dve, chain, X)
                if gamma is not None:
                    chain.settle()
                    norm_stats(dve, chain, lambda t: XN[:, t, :], TT)
                    apply_norm(dve, chain, XN)
                if feature_major:
                    for q, (c, h) in enumerate(QUADS):
                        cols = slice(h * HALF, (h + 1) * HALF)
                        dve.wait_ge(hi, q + 1)
                        dve.tensor_tensor(XTl[:, c, cols], BANKS[q] if XF is None else XF[:, c, cols],
                                          XTh[:, c, cols].bitcast(F32), ALU.subtract).then_inc(lo, 1)

            if not feature_major:
                return

            @part(pe_parts, name)
            def _(pe, b):
                pe.wait_ge(chain_of, steps)
                for q, (c, h) in enumerate(QUADS):
                    for i in range(4):
                        ins = pe.transpose(BANKS[q][:, i * P:(i + 1) * P],
                                           XN[:, 4 * h + i, c * P:(c + 1) * P], ident[:])
                    ins.then_inc(ps, 1)

            @part(act_parts, name)
            def _(act, b):
                for q, (c, h) in enumerate(QUADS):
                    cols = slice(h * HALF, (h + 1) * HALF)
                    act.wait_ge(ps, q + 1)
                    src = BANKS[q]
                    if XF is not None:
                        if gamma is not None:
                            ins = act.activation(XF[:, c, cols], src, ACT.Identity,
                                                 scale=gl[:, c, gamma:gamma + 1],
                                                 bias=gl[:, c, gamma + 1:gamma + 2])
                        else:
                            ins = act.activation(XF[:, c, cols], src, ACT.Copy)
                        ins.then_inc(full, 1)
                        act.wait_ge(full, q + 1)
                        src = XF[:, c, cols]
                    act.activation(XTh[:, c, cols], src, ACT.Copy).then_inc(hi, 1)

        def context_attention(k, group_heads, weights, scale, gate, masked, bias_row):
            prep, main = f"prep{k}", f"attn{k}"
            groups = HEADS // group_heads
            w = group_heads * JP
            segs = [(0, w)] if w <= HALF else [(0, w // 2), (w // 2, w)]
            n_parts = len(weights)
            AHi = sb(f"scores_w_hi{k}", [P, DC, HJ], F32R)
            ALo = sb(f"scores_w_lo{k}", [P, DC, HJ], F32R)
            VWh = sb(f"out_w_hi{k}", [P, HJC, D], F32R)
            VWl = sb(f"out_w_lo{k}", [P, HJC, D], F32R)
            with buffers():
                heads_of_rows = sb(f"head_mask{k}", [P, group_heads])
                raw = sb(f"prep_raw{k}", [P, n_parts, D])
                wh = sb(f"prep_wh{k}", [P, n_parts, D], F32R)
                wl = sb(f"prep_wl{k}", [P, n_parts, D], F32R)
                KB = sb(f"k_blocks{k}", [P, group_heads, JP])
                VB = sb(f"v_blocks{k}", [P, group_heads, JP])
                KBh = sb(f"k_blocks_hi{k}", [P, w], F32R)
                KBl = sb(f"k_blocks_lo{k}", [P, w], F32R)
                VBh = sb(f"v_blocks_hi{k}", [P, w], F32R)
                VBl = sb(f"v_blocks_lo{k}", [P, w], F32R)
                VWT = sb(f"out_w_t{k}", [P, DC, HJC * P])
            KBv, VBv = KB[:, :, :].rearrange("p h j -> p (h j)"), VB[:, :, :].rearrange("p h j -> p (h j)")
            has_wo = n_parts == 4
            raw_in = signal(prep + "_weights_in")
            mask_steps = signal(prep + "_mask_steps")
            split = signal(prep + "_weights_split")
            kv_ps = signal(prep + "_kv_ready")
            blocks = signal(prep + "_blocks")
            blocks_hi = signal(prep + "_blocks_hi")
            blocks_lo = signal(prep + "_blocks_lo")
            a_ps = signal(prep + "_products")
            a_hi = signal(prep + "_products_hi")
            a_lo = signal(prep + "_products_lo")
            vw_ps = signal(prep + "_vw_transposed")
            vw_hi = signal(prep + "_vw_hi")
            vw_lo = signal(prep + "_vw_lo")

            a_bank = {(c, s): [BANKS[0], BANKS[1], BANKS[3], BANKS[4]][c * len(segs) + s]
                      for c in range(DC) for s in range(len(segs))}
            v_bank = [BANKS[3], BANKS[4]]

            def group_loop(eng, body):
                for g in range(groups):
                    body(g)

            def cols(tensor, c, g, s0, s1):
                return tensor[:, c, g * w + s0:g * w + s1]

            @part(sp_parts, prep)
            def _(sp, b):
                def body(g):
                    if g:
                        sp.wait_ge(split, g * 2)
                    for i, source in enumerate(weights):
                        dst, src = source(raw, i, g)
                        sp.dma_start(dst, src).then_inc(raw_in, 16)
                group_loop(sp, body)

            @part(pool_parts, prep)
            def _(pool, b):
                m = heads_of_rows[:]
                rows = P // group_heads
                pool.memset(m, 1.0).then_inc(mask_steps, 1)
                pool.memset(VWT[:], 0.0).then_inc(mask_steps, 1)
                pool.wait_ge(mask_steps, 2)
                pool.affine_select(out=m, in_=m, compare_op=ALU.is_ge, fill=0.0, base=0,
                                   pattern=[[-rows, group_heads]], channel_multiplier=1
                                   ).then_inc(mask_steps, 1)
                pool.wait_ge(mask_steps, 3)
                pool.affine_select(out=m, in_=m, compare_op=ALU.is_ge, fill=0.0, base=rows - 1,
                                   pattern=[[rows, group_heads]], channel_multiplier=-1
                                   ).then_inc(mask_steps, 1)

                def body(g):
                    pool.wait_ge(raw_in, (g + 1) * (16 * n_parts))
                    if g:
                        pool.wait_ge(a_ps, g)
                    pool.tensor_scalar(wh[:], raw[:], 1.0, 0.0, ALU.mult, ALU.add).then_inc(split, 1)
                    pool.wait_ge(split, g * 2 + 1)
                    pool.tensor_tensor(wl[:], raw[:], wh[:].bitcast(F32), ALU.subtract).then_inc(split, 1)
                group_loop(pool, body)

            @part(pe_parts, prep)
            def _(pe, b):
                def body(g):
                    pe.wait_ge(split, g * 2 + 2)
                    if g:
                        pe.wait_ge(blocks, g * 2)
                    for i, col0 in ((0, 0), (1, P)):
                        for c in range(DC):
                            e = slice(c * P, (c + 1) * P)
                            ins = mm3(pe, PT[:, col0:col0 + JP], wh[:, i, e], wl[:, i, e],
                                      CTh[:, c, :], CTl[:, c, :], c == 0, c == DC - 1)
                    ins.then_inc(kv_ps, 1)
                    pe.wait_ge(blocks_lo, g * 2 + 2)
                    if g:
                        pe.wait_ge(a_lo, g)
                    for c in range(DC):
                        e = slice(c * P, (c + 1) * P)
                        for s, (s0, s1) in enumerate(segs):
                            ins = mm3(pe, a_bank[c, s][:, 0:s1 - s0], wh[:, 2, e], wl[:, 2, e],
                                      KBh[:, s0:s1], KBl[:, s0:s1], True, True)
                        if has_wo:
                            ins = mm3(pe, [BANKS[2], BANKS[5]][c][:, 0:w], wh[:, 3, e], wl[:, 3, e],
                                      VBh[:], VBl[:], True, True)
                    ins.then_inc(a_ps, 1)
                group_loop(pe, body)
                if has_wo:
                    pe.wait_ge(a_lo, groups)
                pe.wait_ge(a_hi, groups)
                pe.wait_ge(a_lo, groups)
                for n in range(HJC // 2):
                    for i in range(2):
                        for c in range(DC):
                            col0 = i * D + c * P
                            ins = pe.transpose(BANKS[n][:, col0:col0 + P],
                                               VWT[:, c, (2 * n + i) * P:(2 * n + i + 1) * P], ident[:])
                    ins.then_inc(vw_ps, 1)

            @part(dve_parts, prep)
            def _(dve, b):
                dve.wait_ge(mask_steps, 4)
                own = heads_of_rows[:, :].unsqueeze(2).broadcast_to([P, group_heads, JP])

                def body(g):
                    dve.wait_ge(kv_ps, g + 1)
                    if g:
                        dve.wait_ge(blocks_hi, g * 2)
                    if g:
                        dve.wait_ge(blocks_lo, g * 2)
                    for blk, col0 in ((KB, 0), (VB, P)):
                        dve.tensor_tensor(blk[:], PT[:, col0:col0 + JP].unsqueeze(1).broadcast_to(
                            [P, group_heads, JP]), own, ALU.mult).then_inc(blocks, 1)
                    for n, (lo, full, hi_) in enumerate(((KBl, KBv, KBh), (VBl, VBv, VBh))):
                        dve.wait_ge(blocks_hi, g * 2 + n + 1)
                        dve.tensor_tensor(lo[:], full, hi_[:].bitcast(F32), ALU.subtract
                                          ).then_inc(blocks_lo, 1)
                    dve.wait_ge(a_hi, g + 1)
                    for c in range(DC):
                        for s, (s0, s1) in enumerate(segs):
                            ins = dve.tensor_tensor(cols(ALo, c, g, s0, s1), a_bank[c, s][:, 0:s1 - s0],
                                                    cols(AHi, c, g, s0, s1).bitcast(F32), ALU.subtract)
                    ins.then_inc(a_lo, 1)
                group_loop(dve, body)
                for n in range(HJC // 2):
                    dve.wait_ge(vw_hi, n + 1)
                    dve.tensor_tensor(VWl[:, 2 * n:2 * n + 2, :], BANKS[n].rearrange("p (i d) -> p i d", i=2),
                                      VWh[:, 2 * n:2 * n + 2, :].bitcast(F32), ALU.subtract
                                      ).then_inc(vw_lo, 1)

            @part(act_parts, prep)
            def _(act, b):
                act.wait_ge(mask_steps, 2)

                def body(g):
                    if g:
                        act.wait_ge(a_ps, g)
                    for n, (hi_, full) in enumerate(((KBh, KBv), (VBh, VBv))):
                        act.wait_ge(blocks, g * 2 + n + 1)
                        act.activation(hi_[:], full, ACT.Copy).then_inc(blocks_hi, 1)
                    if not has_wo:
                        act.activation(cols(VWT, g, g, 0, w), VBv, ACT.Copy)
                    act.wait_ge(a_ps, g + 1)
                    for c in range(DC):
                        for s, (s0, s1) in enumerate(segs):
                            ins = act.activation(cols(AHi, c, g, s0, s1), a_bank[c, s][:, 0:s1 - s0], ACT.Copy)
                        if has_wo:
                            ins = act.activation(cols(VWT, c, g, 0, w), [BANKS[2], BANKS[5]][c][:, 0:w], ACT.Copy)
                    ins.then_inc(a_hi, 1)
                group_loop(act, body)
                for n in range(HJC // 2):
                    act.wait_ge(vw_ps, n + 1)
                    act.activation(VWh[:, 2 * n:2 * n + 2, :], BANKS[n].rearrange("p (i d) -> p i d", i=2),
                                   ACT.Copy).then_inc(vw_hi, 1)

            NP = 3
            with buffers():
                SB = [sb(f"scores{k}_{i}", [P, HEADS, JP]) for i in range(2)]
                PR = [sb(f"probs{k}_{i}", [P, HJC * P]) for i in range(NP)]
                PTh = [sb(f"probs_t_hi{k}_{i}", [P, HJC, P], F32R) for i in range(2)]
                PTl = [sb(f"probs_t_lo{k}_{i}", [P, HJC, P], F32R) for i in range(2)]
                mx = sb(f"row_max{k}", [P, 2, HEADS])
                sm = sb(f"row_sum{k}", [P, NP, HEADS])
                rs = sb(f"row_inv{k}", [P, NP, HEADS])
                mask8 = sb(f"mask_bytes{k}", [P, TT, J], U8) if masked else None
                mneg = sb(f"mask_add{k}", [P, TT, J]) if masked else None
            PRv = [p_[:, 0:HJ].rearrange("p (h j) -> p h j", h=HEADS) for p_ in PR]
            SPS = [PA, PB]
            ROUNDS = [(0, 4), (4, 8), (8, HJC)]
            mask_in = signal(main + "_mask_in")
            mask_done = signal(main + "_mask_ready")
            cleared = signal(main + "_probs_cleared")
            biased = signal(main + "_bias_added")
            s_ps = signal(main + "_scores_ready")
            s_out = signal(main + "_scores_copied")
            mx_done = signal(main + "_max")
            sub_done = signal(main + "_shifted")
            ex_done = signal(main + "_exp")
            sum_done = signal(main + "_sum")
            inv_done = signal(main + "_inv")
            p_done = signal(main + "_probs_ready")
            t_ps = signal(main + "_probs_transposed")
            t_hi = signal(main + "_probs_t_hi")
            t_lo = signal(main + "_probs_t_lo")
            o_ps = signal(main + "_out_ready")
            x_done = signal(main + "_residual")
            LAG = 2
            NR = len(ROUNDS)

            def bank_view(buf, n):
                h0, h1 = BANK_HEADS[n]
                return buf[:, n * HALF:n * HALF + (h1 - h0) * JP].rearrange("p (h j) -> p h j", j=JP)[:, :, 0:J]

            if masked:
                @part(sp_parts, main)
                def _(sp, b):
                    sp.dma_start(mask8[:], A["mask_BxSxS2_bk1"][bass.ds(b * N, N), :].rearrange(
                        "(t p) j -> p t j", p=P)).then_inc(mask_in, 16)

            @part(pe_parts, main)
            def _(pe, b):
                for i in range(TT + LAG + 1):
                    j, o = i - LAG, i - LAG - 1
                    for r in range(NR):
                        if 0 <= j < TT:
                            if r == 0:
                                pe.wait_ge(p_done, j + 1)
                            if j or r:
                                pe.wait_ge(t_lo, NR * j + r)
                            c0, c1 = ROUNDS[r]
                            for c in range(c0, c1):
                                ins = pe.transpose(PT[:, (c - c0) * P:(c - c0 + 1) * P],
                                                   PR[j % NP][:, c * P:(c + 1) * P], ident[:])
                            ins.then_inc(t_ps, 1)
                        if i < TT:
                            if r == 0 and i >= 2:
                                pe.wait_ge(s_out, i - 1)
                            h0, h1 = BANK_HEADS[r]
                            for c in range(DC):
                                tok = slice(i * P, (i + 1) * P)
                                ins = mm3(pe, SPS[i % 2][:, r * HALF:r * HALF + (h1 - h0) * JP],
                                          XTh[:, c, tok], XTl[:, c, tok],
                                          AHi[:, c, h0 * JP:h1 * JP], ALo[:, c, h0 * JP:h1 * JP],
                                          c == 0, c == DC - 1)
                            if r == NR - 1:
                                ins.then_inc(s_ps, 1)
                    if 0 <= o < TT:
                        pe.wait_ge(t_lo, NR * (o + 1))
                        if o:
                            pe.wait_ge(x_done, o)
                        for c in range(HJC):
                            ins = mm3(pe, PV[:, 0:D], PTh[o % 2][:, c, :], PTl[o % 2][:, c, :],
                                      VWh[:, c, :], VWl[:, c, :], c == 0, c == HJC - 1)
                        ins.then_inc(o_ps, 1)

            @part(act_parts, main)
            def _(act, b):
                act.wait_ge(cleared, 1)
                for i in range(TT + LAG):
                    j = i - LAG
                    if 0 <= j < TT:
                        for r, (c0, c1) in enumerate(ROUNDS):
                            act.wait_ge(t_ps, NR * j + r + 1)
                            if r == 0 and j >= 2:
                                act.wait_ge(o_ps, j - 1)
                            act.activation(PTh[j % 2][:, c0:c1, :].rearrange("p c q -> p (c q)"),
                                           PT[:, 0:(c1 - c0) * P], ACT.Copy).then_inc(t_hi, 1)
                    if i < TT and not masked:
                        act.wait_ge(s_ps, i + 1)
                        if i >= 2:
                            act.wait_ge(ex_done, i - 1)
                        for n, (h0, h1) in enumerate(BANK_HEADS):
                            ins = act.activation(SB[i % 2][:, h0:h1, 0:J], bank_view(SPS[i % 2], n), ACT.Copy)
                        ins.then_inc(s_out, 1)
                    if i < TT:
                        act.wait_ge(sub_done, i + 1)
                        if i >= NP:
                            act.wait_ge(t_ps, NR * (i - NP + 1))
                        act.activation(PRv[i % NP][:, :, 0:J], SB[i % 2][:, :, 0:J], ACT.Exp,
                                       scale=scale).then_inc(ex_done, 1)

            @part(dve_parts, main)
            def _(dve, b):
                if masked:
                    dve.wait_ge(mask_in, 16)
                    dve.tensor_scalar(mneg[:], mask8[:], NEG_MAX, None, ALU.mult).then_inc(mask_done, 1)
                    dve.wait_ge(mask_done, 1)
                if bias_row is not None:
                    dve.wait_ge(biased, 1)
                for i in range(TT + LAG + 1):
                    j = i - LAG
                    if 0 <= j < TT:
                        for r, (c0, c1) in enumerate(ROUNDS):
                            dve.wait_ge(t_hi, NR * j + r + 1)
                            dve.tensor_tensor(PTl[j % 2][:, c0:c1, :].rearrange("p c q -> p (c q)"),
                                              PT[:, 0:(c1 - c0) * P],
                                              PTh[j % 2][:, c0:c1, :].rearrange("p c q -> p (c q)").bitcast(F32),
                                              ALU.subtract).then_inc(t_lo, 1)
                    if i < TT:
                        if masked:
                            dve.wait_ge(s_ps, i + 1)
                            if i >= 2:
                                dve.wait_ge(ex_done, i - 1)
                            for n, (h0, h1) in enumerate(BANK_HEADS):
                                ins = dve.tensor_tensor(
                                    SB[i % 2][:, h0:h1, 0:J], bank_view(SPS[i % 2], n),
                                    mneg[:, i, :].unsqueeze(1).broadcast_to([P, h1 - h0, J]), ALU.add)
                            ins.then_inc(s_out, 1)
                        dve.wait_ge(s_out, i + 1)
                        if i >= 2:
                            dve.wait_ge(sub_done, i - 1)
                        dve.tensor_reduce(mx[:, i % 2, :], SB[i % 2][:, :, 0:J], AX.X, ALU.max
                                          ).then_inc(mx_done, 1)
                    if 1 <= i <= TT:
                        q = i - 1
                        dve.wait_ge(ex_done, q + 1)
                        if q >= NP:
                            dve.wait_ge(inv_done, q - NP + 1)
                        dve.tensor_reduce(sm[:, q % NP, :], PRv[q % NP][:, :, 0:J], AX.X, ALU.add
                                          ).then_inc(sum_done, 1)
                        dve.wait_ge(sum_done, q + 1)
                        if q >= NP:
                            dve.wait_ge(p_done, q - NP + 1)
                        dve.reciprocal(rs[:, q % NP, :], sm[:, q % NP, :]).then_inc(inv_done, 1)
                    o = i - LAG - 1
                    if 0 <= o < TT:
                        dve.wait_ge(o_ps, o + 1)
                        dve.scalar_tensor_tensor(X[:, o, :], PV[:, 0:D], tg[:, gate:gate + 1], X[:, o, :],
                                                 ALU.mult, ALU.add).then_inc(x_done, 1)

            @part(pool_parts, main)
            def _(pool, b):
                for p_ in PR:
                    ins = pool.memset(p_[:], 0.0)
                ins.then_inc(cleared, 1)
                if bias_row is not None:
                    pool.tensor_tensor(X[:], X[:], rowb[:, bias_row, :].unsqueeze(1).broadcast_to([P, TT, D]),
                                       ALU.add).then_inc(biased, 1)
                for i in range(TT + 1):
                    if i < TT:
                        pool.wait_ge(mx_done, i + 1)
                        s_ = SB[i % 2][:, :, 0:J]
                        pool.tensor_tensor(s_, s_, mx[:, i % 2, :].unsqueeze(2).broadcast_to([P, HEADS, J]),
                                           ALU.subtract).then_inc(sub_done, 1)
                    if i >= 1:
                        q = i - 1
                        pool.wait_ge(inv_done, q + 1)
                        p_ = PRv[q % NP][:, :, 0:J]
                        pool.tensor_tensor(p_, p_, rs[:, q % NP, :].unsqueeze(2).broadcast_to([P, HEADS, J]),
                                           ALU.mult).then_inc(p_done, 1)

        def by_rows(name):
            return lambda raw, i, g: (raw[:, i, :], A[name][g * P:(g + 1) * P, :])

        def by_cols(name):
            return lambda raw, i, g: (raw[:, i, :].rearrange("p (c e) -> p c e", c=DC),
                                      A[name].rearrange("(c p) e -> p c e", p=P)[:, :, g * P:(g + 1) * P])

        ln_stage("ln0x")
        with buffers():
            context_attention(0, 2, [by_cols("L0_xattn_Wk"), by_cols("L0_xattn_Wv"),
                                     by_rows("L0_xattn_WqT"), by_rows("L0_xattn_Wo")],
                              DH ** -0.5, 0, True, BO0)

        QW = [("L0_ffn_gT", DC, INNER), ("L0_ffn_uT", DC, INNER), ("L0_ffn_dT", INNER // P, D)]
        WCOLS = DC * INNER
        IC = INNER // P
        ln_stage("ln0f", feature_major=False)
        with buffers():
            wraw = [sb(f"ternary_raw{n}", [P, WCOLS]) for n in range(3)]
        bit_scope = ExitStack()
        scope = bit_scope
        XQ = sb("x_ints_f", [P, TT, D])
        XQb = sb("x_ints", [P, TT, D], BF16)
        XQT = sb("x_ints_t", [P, DC, N], BF16)
        amax = sb("x_abs_max", [P, TT])
        ainv = sb("x_inv_max", [P, TT])
        TH = [sb(f"bit_tanh{i}", [P, INNER]) for i in range(2)]
        GA = [sb(f"bit_gate{i}", [P, INNER]) for i in range(2)]
        HH = [sb(f"bit_hidden{i}", [P, INNER]) for i in range(2)]
        HQ = [sb(f"bit_hidden_ints{i}", [P, INNER], BF16) for i in range(2)]
        HT = [sb(f"bit_hidden_t{i}", [P, IC, P], BF16) for i in range(2)]
        cg = sb("bit_gate_scale", [P, TT])
        hcg = sb("bit_half_gate_scale", [P, TT])
        cgu = sb("bit_product_scale", [P, TT])
        hmax = sb("hidden_abs_max", [P, TT])
        hclip = sb("hidden_clipped_max", [P, TT])
        hinv = sb("hidden_inv_max", [P, TT])
        hout = sb("hidden_out_scale", [P, TT])
        bit_scope.close()
        scope = life

        bw_in = [life.enter_context(nc.semaphore(f"bit_weight{n}_in")) for n in range(3)]
        bw_sum = life.enter_context(nc.semaphore("bit_weight_sum"))
        bw_steps = life.enter_context(nc.semaphore("bit_weight_steps"))
        bq_steps = signal("bitq_dve_steps")
        bx_ints = signal("bit_x_ints")
        bx_ps = signal("bit_x_transposed")
        bx_t = signal("bit_x_t_copied")

        def sp_ternary(sp):
            for n, (name, c, w) in enumerate(QW):
                sp.dma_start(wraw[n][:].rearrange("p (c w) -> p c w", c=c),
                             A[name].rearrange("(c p) w -> p c w", p=P)).then_inc(bw_in[n], 16)

        def dve_ternary(dve):
            chain = Chain(dve, bw_steps)
            for n in range(3):
                dve.wait_ge(bw_in[n], 16)
                chain.step(dve.tensor_reduce(wabs[:, n:n + 1], wraw[n][:], AX.X, ALU.add,
                                             apply_absolute_value=True))
            dve.wait_ge(bw_sum, 1)
            chain.step(dve.tensor_scalar(wmean[:], PV[:, 0:3], 1.0 / (INNER * D), EPS, ALU.mult, ALU.max))
            chain.settle()
            chain.step(dve.reciprocal(winv[:], wmean[:]))
            chain.settle()
            for n in range(3):
                chain.step(dve.tensor_scalar(wraw[n][:], wraw[n][:], winv[:, n:n + 1], 1.0, ALU.mult, ALU.min))
            chain.settle()
            for n in range(3):
                chain.step(dve.tensor_scalar(wraw[n][:], wraw[n][:], -1.0, MAGIC, ALU.max, ALU.add))
            chain.settle()
            for n in range(3):
                chain.step(dve.tensor_scalar(wq[n][:], wraw[n][:], -MAGIC, None, ALU.add))
            chain.settle()

        def pe_ternary(pe):
            pe.wait_ge(bw_steps, 3)
            pe.matmul(PV[:, 0:3], ones[:], wabs[:], start=True, stop=True).then_inc(bw_sum, 1)

        @part(dve_parts, "bitq")
        def _(dve, b):
            chain = Chain(dve, bq_steps)
            chain.step(dve.tensor_reduce(amax[:], XN[:], AX.X, ALU.max, apply_absolute_value=True))
            chain.settle()
            chain.step(dve.tensor_scalar(amax[:], amax[:], EPS, None, ALU.max))
            chain.settle()
            chain.step(dve.reciprocal(ainv[:], amax[:]))
            chain.settle()
            chain.step(dve.tensor_scalar(ainv[:], ainv[:], 127.0, None, ALU.mult))
            chain.settle()
            for t in range(TT):
                ins = dve.tensor_scalar(XQ[:, t, :], XN[:, t, :], ainv[:, t:t + 1], MAGIC, ALU.mult, ALU.add)
            chain.step(ins)
            chain.settle()
            dve.tensor_scalar(XQb[:], XQ[:], -MAGIC, 127.0, ALU.add, ALU.min).then_inc(bx_ints, 1)
            chain.step(dve.tensor_scalar(cg[:], amax[:], wmean[:, 0:1], 1.0 / 127.0, ALU.mult, ALU.mult))
            chain.settle()
            chain.step(dve.tensor_scalar(hcg[:], cg[:], 0.5, None, ALU.mult))
            chain.settle()
            chain.step(dve.tensor_scalar(cgu[:], amax[:], wmean[:, 1:2], 1.0 / 127.0, ALU.mult, ALU.mult))
            chain.settle()
            chain.step(dve.tensor_tensor(cgu[:], cgu[:], hcg[:], ALU.mult))

        @part(pe_parts, "bitq")
        def _(pe, b):
            pe.wait_ge(bx_ints, 1)
            for q, (c, h) in enumerate(QUADS):
                for i in range(4):
                    ins = pe.transpose(BANKS[q + 1].bitcast(BF16)[:, i * P:(i + 1) * P],
                                       XQb[:, 4 * h + i, c * P:(c + 1) * P], identb[:])
                ins.then_inc(bx_ps, 1)

        @part(act_parts, "bitq")
        def _(act, b):
            for q, (c, h) in enumerate(QUADS):
                act.wait_ge(bx_ps, q + 1)
                act.activation(XQT[:, c, h * HALF:(h + 1) * HALF], BANKS[q + 1].bitcast(BF16)[:, 0:HALF],
                               ACT.Copy).then_inc(bx_t, 1)

        bg_ps = signal("bit_gate_up")
        b_tanh = signal("bit_tanh")
        b_gate = signal("bit_gate")
        b_hid = signal("bit_hidden")
        b_small = signal("bit_small_steps")
        b_hscale = signal("bit_hidden_scale")
        b_round = signal("bit_rounded")
        b_hq = signal("bit_hidden_ints")
        b_htp = signal("bit_hidden_transposed")
        b_ht = signal("bit_hidden_t")
        b_out = signal("bit_out")
        b_x = signal("bit_residual")

        @part(pe_parts, "bit")
        def _(pe, b):
            wv = [wq[n][:].rearrange("p (c w) -> p c w", c=c) for n, (_, c, _) in enumerate(QW)]
            for i in range(TT + 3):
                if i < TT:
                    if i:
                        pe.wait_ge(b_hid, i)
                    for n, buf in ((0, PA), (1, PB)):
                        for s in range(INNER // HALF):
                            for c in range(DC):
                                ins = pe.matmul(buf[:, s * HALF:(s + 1) * HALF], XQT[:, c, i * P:(i + 1) * P],
                                                wv[n][:, c, s * HALF:(s + 1) * HALF], start=c == 0, stop=c == DC - 1)
                    ins.then_inc(bg_ps, 1)
                j = i - 2
                if 0 <= j < TT:
                    pe.wait_ge(b_hq, j + 1)
                    if j:
                        pe.wait_ge(b_ht, j)
                    for c in range(IC):
                        ins = pe.transpose(PT[:].bitcast(BF16)[:, c * P:(c + 1) * P],
                                           HQ[j % 2][:, c * P:(c + 1) * P], identb[:])
                    ins.then_inc(b_htp, 1)
                o = i - 3
                if 0 <= o < TT:
                    pe.wait_ge(b_ht, o + 1)
                    if o:
                        pe.wait_ge(b_x, o)
                    for c in range(IC):
                        ins = pe.matmul(PV[:, 0:D], HT[o % 2][:, c, :], wv[2][:, c, :], start=c == 0, stop=c == IC - 1)
                    ins.then_inc(b_out, 1)

        @part(act_parts, "bit")
        def _(act, b):
            for i in range(TT + 2):
                j = i - 2
                if 0 <= j < TT:
                    act.wait_ge(b_htp, j + 1)
                    if j >= 2:
                        act.wait_ge(b_out, j - 1)
                    act.activation(HT[j % 2][:].rearrange("p c q -> p (c q)"), PT[:].bitcast(BF16), ACT.Copy
                                   ).then_inc(b_ht, 1)
                if i < TT:
                    act.wait_ge(bg_ps, i + 1)
                    if i >= 2:
                        act.wait_ge(b_gate, i - 1)
                    act.activation(TH[i % 2][:], PA[:, 0:INNER], ACT.Tanh, scale=hcg[:, i:i + 1]).then_inc(b_tanh, 1)

        @part(dve_parts, "bit")
        def _(dve, b):
            small = Chain(dve, b_small)
            for i in range(TT + 3):
                if i < TT:
                    t1 = slice(i, i + 1)
                    dve.wait_ge(b_tanh, i + 1)
                    if i >= 2:
                        dve.wait_ge(b_hid, i - 1)
                    dve.scalar_tensor_tensor(GA[i % 2][:], TH[i % 2][:], 1.0, PA[:, 0:INNER], ALU.add, ALU.mult
                                             ).then_inc(b_gate, 1)
                    dve.wait_ge(b_gate, i + 1)
                    if i >= 2:
                        dve.wait_ge(b_round, i - 1)
                    dve.scalar_tensor_tensor(HH[i % 2][:], GA[i % 2][:], cgu[:, t1], PB[:, 0:INNER],
                                             ALU.mult, ALU.mult).then_inc(b_hid, 1)
                    dve.wait_ge(b_hid, i + 1)
                    small.step(dve.tensor_reduce(hmax[:, t1], HH[i % 2][:], AX.X, ALU.max, apply_absolute_value=True))
                    small.settle()
                    small.step(dve.tensor_scalar(hclip[:, t1], hmax[:, t1], EPS, None, ALU.max))
                    small.settle()
                    small.step(dve.reciprocal(hinv[:, t1], hclip[:, t1]))
                    small.settle()
                    dve.tensor_scalar(hinv[:, t1], hinv[:, t1], 127.0, None, ALU.mult).then_inc(b_hscale, 1)
                    small.step(dve.tensor_scalar(hout[:, t1], hclip[:, t1], wmean[:, 2:3], 1.0 / 127.0,
                                                 ALU.mult, ALU.mult))
                    small.settle()
                    small.step(dve.tensor_scalar(hout[:, t1], hout[:, t1], tg[:, LAYERS:LAYERS + 1], None, ALU.mult))
                q = i - 1
                if 0 <= q < TT:
                    dve.wait_ge(b_round, q + 1)
                    if q >= 2:
                        dve.wait_ge(b_htp, q - 1)
                    dve.tensor_scalar(HQ[q % 2][:], HH[q % 2][:], -MAGIC, 127.0, ALU.add, ALU.min).then_inc(b_hq, 1)
                o = i - 3
                if 0 <= o < TT:
                    dve.wait_ge(b_out, o + 1)
                    dve.scalar_tensor_tensor(X[:, o, :], PV[:, 0:D], hout[:, o:o + 1], X[:, o, :],
                                             ALU.mult, ALU.add).then_inc(b_x, 1)

        @part(pool_parts, "bit")
        def _(pool, b):
            for i in range(TT):
                pool.wait_ge(b_hscale, i + 1)
                pool.tensor_scalar(HH[i % 2][:], HH[i % 2][:], hinv[:, i:i + 1], MAGIC, ALU.mult, ALU.add
                                   ).then_inc(b_round, 1)

        def hi_of(eng, hi, src):
            return eng.tensor_scalar(hi, src, 1.0, 0.0, ALU.mult, ALU.add)

        next_layer()
        def latent_attention(k, heads, weights, ctx, out_to, gate, bias_row, mask=None):
            st = f"attn{k}"
            pairs = heads // 2
            turns = pairs // 2
            n_q = len(weights) - 1
            IQ, IK, IV = 0, 1, 2
            IKC, IVC = (3, 4) if n_q == 5 else (1, 2)
            Ch, Cl = ctx
            SEG = [(0, HALF), (HALF, N), (N, KEYSP)]
            ROUNDS = [(0, 4), (4, 8), (8, KC)]
            LAG, NPB = 3, 4
            PU = 2 * TT
            UNITS = 2 * PU
            ROWS = [slice(0, DH), slice(DH, P)]
            CTX_UNITS = [(0, 6), (6, 11), (11, PU)]
            PIECES = {0: ("k", 0), 1: ("k", 1), 2: ("k", 2), 3: ("q", 0), 4: ("q", 1), 5: ("v", 0),
                      6: ("v", 1), 7: ("v", 2), 10: ("x", 0), 11: ("x", 1), 12: ("x", 2)}
            OUT_OWN = {15: 0}
            OUT_BEFORE = {8: 1, 9: 2, 13: 3}
            KQ = 10
            with buffers():
                raw = sb(f"qkv_raw{k}", [P, n_q, D])
                wh = sb(f"qkv_hi{k}", [P, n_q, D], F32R)
                wl = sb(f"qkv_lo{k}", [P, n_q, D], F32R)
                oraw = sb(f"wo_raw{k}", [P, D])
                oh = [sb(f"wo_hi{k}_{n}", [P, D], F32R) for n in range(2)]
                ol = [sb(f"wo_lo{k}_{n}", [P, D], F32R) for n in range(2)]
                OR = sb(f"o_t_piece{k}", [P, HALF])
                RB = [sb(f"kq_piece{k}_{i}", [P, HALF]) for i in range(2)]
                QS = [[sb(f"q_stack{k}_{n}_{i}", [P, N], F32R) for i in range(2)] for n in range(2)]
                KH = [[sb(f"k_hi{k}_{n}_{i}", [P, KEYSP], F32R) for i in range(2)] for n in range(2)]
                KL = [[sb(f"k_lo{k}_{n}_{i}", [P, KEYSP], F32R) for i in range(2)] for n in range(2)]
                V = [sb(f"v{k}_{n}", [P, KC, P]) for n in range(2)]
                SCX = [sb(f"ctx_scores{k}_{n}", [P, PU, JP]) for n in range(2)]
                ncmax = [sb(f"neg_max_ctx{k}_{n}", [P, PU]) for n in range(2)]
                PR = [sb(f"p{k}_{i}", [P, KC * P]) for i in range(NPB)]
                PTS = [[sb(f"p_t{k}_{i}_{h}", [P, KC, P]) for h in range(2)] for i in range(2)]
                OTh = sb(f"o_t_hi{k}", [P, N], F32R)
                OTl = sb(f"o_t_lo{k}", [P, N], F32R)
                nmax = sb(f"neg_max{k}", [P, NPB])
                ntmax = sb(f"neg_max_tok{k}", [P, NPB])
                rsum = sb(f"row_sums{k}", [P, NPB, 2])
                rtot = sb(f"row_totals{k}", [P, NPB])
                rinv = sb(f"row_invs{k}", [P, NPB])
                Y = sb(f"attn_out{k}", [P, TT, D]) if out_to is None else None
                mask8 = sb(f"ctx_mask{k}", [P, J], U8) if mask else None
                mrow = sb(f"ctx_mask_add{k}", [P, J]) if mask else None
            dest = X if out_to is not None else Y
            SPS = [PA[:, 0:N], PB[:, 0:N]]
            TBANK = [BANKS[2], PT]
            PJ = BANKS[5]
            loop_signals = []

            class Build:

                def __init__(self, prefix, make):
                    self.w_in = make(prefix + "weights_in")
                    self.w_hi, self.w_lo = make(prefix + "weights_hi"), make(prefix + "weights_lo")
                    self.k_ps, self.q_ps = make(prefix + "k_projected"), make(prefix + "q_projected")
                    self.v_ps, self.c_ps = make(prefix + "v_projected"), make(prefix + "ctx_scores")
                    self.kq_raw = make(prefix + "kq_raw")
                    self.kq_hi, self.kq_lo = make(prefix + "kq_hi"), make(prefix + "kq_lo")
                    self.k_dup = make(prefix + "k_doubled")
                    self.v_sb, self.c_sb = make(prefix + "v_copied"), make(prefix + "ctx_scores_copied")
                    self.c_masked = make(prefix + "ctx_masked") if mask else None
                    self.c_max = make(prefix + "ctx_max")

            def outside(name):
                return signal(f"{st}_{name}")

            def in_loop(name):
                s = semaphore(f"{st}_{name}")
                loop_signals.append(s)
                return s

            F = Build("first_", outside)
            L = Build("", in_loop)
            o_in, o_whi, o_wlo = in_loop("wo_in"), in_loop("wo_hi"), in_loop("wo_lo")
            s_ps, t_max, m_done = in_loop("scores"), in_loop("token_max"), in_loop("neg_max")
            e_done, ec_done = in_loop("exp"), in_loop("exp_ctx")
            total, i_done, p_done = in_loop("row_total"), in_loop("inv_sum"), in_loop("probs_scaled")
            t_ps, t_act, t_dve = in_loop("probs_t"), in_loop("probs_t_act"), in_loop("probs_t_dve")
            pv_done, o_raw = in_loop("pv"), in_loop("out_t_copied")
            o_hi, o_lo = in_loop("out_t_hi"), in_loop("out_t_lo")
            wo_ps, x_add = in_loop("projected"), in_loop("added")
            pads = signal(st + "_pads")
            mask_in, mask_row = (signal(st + "_mask_in"), signal(st + "_mask_row")) if mask else (None, None)
            turn = turn_signals(st)

            def load_qkv(sp, row, sem):
                for i, (name, off) in enumerate(weights[:n_q]):
                    sp.dma_start(raw[:, i, :].rearrange("p (c e) -> p c e", c=DC),
                                 A[name].rearrange("(c p) e -> p c e", p=P)[:, :, bass.ds(row + off, P)]
                                 ).then_inc(sem, 16)

            def double_k(sp, B, n):
                sp.wait_ge(B.kq_hi, KQ * n + 6)
                sp.wait_ge(B.kq_lo, KQ * n + 6)
                for t_ in (KH[1 - n], KL[1 - n]) if B is L else (KH[0], KL[0]):
                    for hd in range(2):
                        sp.dma_start(t_[hd][ROWS[1 - hd], :].bitcast(F32), t_[hd][ROWS[hd], :].bitcast(F32)).then_inc(B.k_dup, 16)

            def sp_turn(sp, row, next_row):
                load_qkv(sp, next_row, L.w_in)
                sp.dma_start(oraw[:], A[weights[n_q][0]][bass.ds(row, P), :]).then_inc(o_in, 16)
                double_k(sp, L, 0)
                sp.wait_ge(o_wlo, 1)
                sp.dma_start(oraw[:], A[weights[n_q][0]][bass.ds(row + P, P), :]).then_inc(o_in, 16)
                sp.wait_ge(L.w_lo, n_q)
                load_qkv(sp, next_row + P, L.w_in)
                double_k(sp, L, 1)
                end_turn(sp, "sp", turn, loop_signals)

            @part(sp_parts, st)
            def _(sp, b):
                load_qkv(sp, 0, F.w_in)
                if mask:
                    sp.dma_start(mask8[:], A[mask][bass.ds(b, 1), :].broadcast_to([P, J])).then_inc(mask_in, 16)
                sp.wait_ge(F.w_lo, n_q)
                load_qkv(sp, P, F.w_in)
                double_k(sp, F, 0)
                sp.wait_ge(F.w_lo, 2 * n_q)
                with sp.Fori(0, turns - 1) as p:
                    sp_turn(sp, p * (2 * P), p * (2 * P) + 2 * P)
                sp_turn(sp, (pairs - 2) * P, (pairs - 2) * P)

            def split_qkv(pool, B, n, i):
                pool.wait_ge(B.w_in, 16 * n_q * (n + 1))
                hi_of(pool, wh[:, i, :], raw[:, i, :]).then_inc(B.w_hi, 1)
                pool.wait_ge(B.w_hi, n_q * n + i + 1)
                pool.tensor_tensor(wl[:, i, :], raw[:, i, :], wh[:, i, :].bitcast(F32), ALU.subtract
                                   ).then_inc(B.w_lo, 1)

            def out_t_hi(pool, f):
                if f >= 2:
                    pool.wait_ge(wo_ps, 2 * (f - 1))
                pool.wait_ge(o_raw, f + 1)
                hi_of(pool, OTh[:, (f % 2) * HALF:(f % 2 + 1) * HALF], OR[:]).then_inc(o_hi, 1)

            def pool_piece(pool, B, n, q, kind, s):
                if kind in "kq":
                    m = KQ // 2 * n + s + (3 if kind == "q" else 0)
                    a, z = SEG[s]
                    pool.wait_ge(B.kq_raw, m + 1)
                    for hd in range(2):
                        dst = (KH if kind == "k" else QS)[q][hd][ROWS[hd], a:z]
                        hi_of(pool, dst, RB[m % 2][ROWS[hd], 0:z - a]).then_inc(B.kq_hi, 1)
                        pool.wait_ge(B.kq_hi, 2 * m + hd + 1)

            @part(pool_parts, st)
            def _(pool, b):
                if mask:
                    pool.wait_ge(mask_in, 16)
                    pool.tensor_scalar(mrow[:], mask8[:], MASKED, -MASKED, ALU.mult, ALU.add).then_inc(mask_row, 1)
                for i in range(n_q):
                    split_qkv(pool, F, 0, i)
                for v_ in V:
                    ins = pool.memset(v_[:, KC - 1, :], 0.0)
                ins.then_inc(pads, 1)
                for p_ in PR:
                    ins = pool.memset(p_[:, KEYS:KC * P], 0.0)
                if Y is not None:
                    ins = pool.memset(Y[:], 0.0)
                ins.then_inc(pads, 1)
                if bias_row is not None:
                    pool.tensor_tensor(X[:], X[:], rowb[:, bias_row, :].unsqueeze(1).broadcast_to([P, TT, D]),
                                       ALU.add).then_inc(pads, 1)
                pool.wait_ge(pads, 2 if bias_row is None else 3)
                for kind, s in PIECES.values():
                    pool_piece(pool, F, 0, 0, kind, s)
                pool.wait_ge(F.v_ps, 3)
                for i in range(n_q):
                    split_qkv(pool, F, 1, i)
                with pool.Fori(0, turns) as p:
                    for u in range(UNITS):
                        n, r = u // PU, u % PU
                        pool.wait_ge(i_done, u + 1)
                        pr = PR[u % NPB][:, 0:KEYS]
                        pool.tensor_scalar(pr, pr, rinv[:, u % NPB:u % NPB + 1], 0.0, ALU.mult, ALU.add
                                           ).then_inc(p_done, 1)
                        if r in PIECES and PIECES[r][0] in "kq":
                            pool.wait_ge(p_done, u + 1)
                            pool_piece(pool, L, n, 1 - n, *PIECES[r])
                        if r == 8:
                            pool.wait_ge(L.v_ps, 3 * (n + 1))
                        if 8 <= r < 8 + n_q:
                            split_qkv(pool, L, n, r - 8)
                        if r == 7:
                            pool.wait_ge(o_in, 16 * (n + 1))
                            hi_of(pool, oh[n][:], oraw[:]).then_inc(o_whi, 1)
                            pool.wait_ge(o_whi, n + 1)
                            pool.tensor_tensor(ol[n][:], oraw[:], oh[n][:].bitcast(F32), ALU.subtract
                                               ).then_inc(o_wlo, 1)
                        if u % 8 == 4 and u > 8:
                            out_t_hi(pool, (u - 12) // 8)
                    out_t_hi(pool, 3)
                    end_turn(pool, "pool", turn, loop_signals)

            def scores(pe, q, u, n, acc):
                t, hd = u // 2, u % 2
                a, z = SEG[n]
                tok = slice(t * P, (t + 1) * P)
                pe.matmul(acc, QS[q][hd][:, tok], KH[q][hd][:, a:z], start=True, stop=False)
                return pe.matmul(acc, QS[q][hd][:, tok], KL[q][hd][:, a:z], start=False, stop=True)

            def pe_piece(pe, B, n, q, kind, s):
                if kind == "k":
                    if s:
                        pe.wait_ge(B.kq_raw, KQ // 2 * n + s)
                    elif B is L and n:
                        pe.wait_ge(x_add, 1)
                        pe.wait_ge(B.w_lo, n_q)
                    idx, xh, xl = (IK, XTh, XTl) if s < 2 else (IKC, Ch, Cl)
                    tok = slice(s * HALF, (s + 1) * HALF) if s < 2 else slice(0, JP)
                    for c in range(DC):
                        e = slice(c * P, (c + 1) * P)
                        ins = mm3(pe, PJ[:, 0:tok.stop - tok.start], wh[:, idx, e], wl[:, idx, e],
                                  xh[:, c, tok], xl[:, c, tok], c == 0, c == DC - 1)
                    ins.then_inc(B.k_ps, 1)
                elif kind == "q":
                    pe.wait_ge(B.kq_raw, KQ // 2 * n + 3 + s)
                    tok = slice(s * HALF, (s + 1) * HALF)
                    for c in range(DC):
                        e = slice(c * P, (c + 1) * P)
                        ins = mm3(pe, PJ, wh[:, IQ, e], wl[:, IQ, e], XTh[:, c, tok], XTl[:, c, tok],
                                  c == 0, c == DC - 1)
                    ins.then_inc(B.q_ps, 1)
                elif kind == "v":
                    if s:
                        pe.wait_ge(B.v_sb, 3 * n + s)
                    else:
                        pe.wait_ge(B.kq_raw, KQ // 2 * (n + 1))
                    for t in (range(4 * s, 4 * s + 4) if s < 2 else (TT,)):
                        for c in range(DC):
                            e, tok = slice(c * P, (c + 1) * P), slice(t * P, (t + 1) * P)
                            if t < TT:
                                ins = mm3(pe, PJ[:, (t % 4) * P:(t % 4 + 1) * P], XTh[:, c, tok], XTl[:, c, tok],
                                          wh[:, IV, e], wl[:, IV, e], c == 0, c == DC - 1)
                            else:
                                ins = mm3(pe, PJ[0:JP, 0:P], Ch[:, c, :], Cl[:, c, :],
                                          wh[:, IVC, e], wl[:, IVC, e], c == 0, c == DC - 1)
                    ins.then_inc(B.v_ps, 1)
                else:
                    if s:
                        pe.wait_ge(B.c_sb, 3 * n + s)
                    else:
                        pe.wait_ge(B.v_sb, 3 * (n + 1))
                        if B is L and n:
                            pe.wait_ge(x_add, 3)
                        pe.wait_ge(B.k_dup, 64 * (n + 1))
                        pe.wait_ge(B.kq_lo, KQ * (n + 1))
                    u0, u1 = CTX_UNITS[s]
                    for u in range(u0, u1):
                        ins = scores(pe, q, u, 2, PJ[:, (u - u0) * JP:(u - u0 + 1) * JP])
                    ins.then_inc(B.c_ps, 1)

            def pe_out(pe, n, quarter):
                done = 4 * n + quarter
                if quarter == 0:
                    pe.wait_ge(o_wlo, n + 1)
                if n == 0 and quarter in (0, 3):
                    pe.wait_ge(L.c_sb, 3 + quarter)
                elif n == 0 and quarter == 1:
                    pe.wait_ge(L.v_sb, 6)
                else:
                    pe.wait_ge(x_add, done)
                pe.wait_ge(o_lo, 2 * n + quarter // 2 + 1)
                for t in (2 * quarter, 2 * quarter + 1):
                    tok = slice(t * P, (t + 1) * P)
                    ins = mm3(pe, PJ[:, (t % 2) * D:(t % 2 + 1) * D], OTh[:, tok], OTl[:, tok], oh[n][:], ol[n][:],
                              True, True)
                ins.then_inc(wo_ps, 1)

            @part(pe_parts, st)
            def _(pe, b):
                pe.wait_ge(F.w_lo, n_q)
                for kind, s in PIECES.values():
                    pe_piece(pe, F, 0, 0, kind, s)
                pe.wait_ge(F.w_lo, 2 * n_q)
                pe.wait_ge(F.c_sb, 3)
                with pe.Fori(0, turns) as p:
                    for i in range(UNITS + LAG + 2):
                        j = i - LAG
                        g = (j - 2) // 2
                        for r in range(3):
                            if 0 <= j < UNITS:
                                if r == 0:
                                    pe.wait_ge(p_done, j + 1)
                                    if j:
                                        pe.wait_ge(t_dve, j)
                                elif r == 1 and j:
                                    pe.wait_ge(t_act, 2 * j)
                                elif r == 2:
                                    pe.wait_ge(t_act, 2 * j + 1)
                                c0, c1 = ROUNDS[r]
                                for c in range(c0, c1):
                                    ins = pe.transpose(TBANK[(3 * j + r) % 2][:, (c - c0) * P:(c - c0 + 1) * P],
                                                       PR[j % NPB][:, c * P:(c + 1) * P], ident[:])
                                ins.then_inc(t_ps, 1)
                            if i < UNITS and r < 2:
                                if r == 0 and i >= 2:
                                    pe.wait_ge(e_done, i - 1)
                                ins = scores(pe, i // PU, i % PU, r, SPS[i % 2][:, r * HALF:(r + 1) * HALF])
                                if r:
                                    ins.then_inc(s_ps, 1)
                            if 0 <= g < 2 * TT and r < 2:
                                if j % 2 == 0 and r == 0:
                                    pe.wait_ge(t_act, 4 * (g + 1))
                                    pe.wait_ge(t_dve, 2 * (g + 1))
                                    if g and g % 4 == 0:
                                        pe.wait_ge(o_raw, g // 4)
                                c0, c1 = [(0, 2), (2, 4), (4, 7), (7, KC)][(j % 2) * 2 + r]
                                for c in range(c0, c1):
                                    for hd in range(2):
                                        ins = pe.matmul(PV[ROWS[hd], (g % 4) * P:(g % 4 + 1) * P],
                                                        V[g // TT][:, c, ROWS[hd]], PTS[g % 2][hd][:, c, :],
                                                        start=c == 0, stop=c == KC - 1)
                                if c1 == KC:
                                    ins.then_inc(pv_done, 1)
                        if i < UNITS:
                            n, slot = i // PU, i % PU
                            if slot in PIECES:
                                pe_piece(pe, L, n, 1 - n, *PIECES[slot])
                            if n and slot in OUT_BEFORE:
                                pe_out(pe, 0, OUT_BEFORE[slot])
                            if slot in OUT_OWN:
                                pe_out(pe, n, OUT_OWN[slot])
                    for quarter in (1, 2, 3):
                        pe_out(pe, 1, quarter)
                    end_turn(pe, "pe", turn, loop_signals)

            def act_piece(act, B, n, q, kind, s):
                if kind in "kq":
                    m = KQ // 2 * n + s + (3 if kind == "q" else 0)
                    if m >= 2:
                        act.wait_ge(B.kq_lo, 2 * (m - 1))
                    if kind == "k":
                        act.wait_ge(B.k_ps, 3 * n + s + 1)
                    else:
                        act.wait_ge(B.q_ps, 2 * n + s + 1)
                    a, z = SEG[s]
                    act.activation(RB[m % 2][:, 0:z - a], PJ[:, 0:z - a], ACT.Copy,
                                   scale=1.0 if kind == "k" else DH ** -0.5).then_inc(B.kq_raw, 1)
                elif kind == "v":
                    act.wait_ge(B.v_ps, 3 * n + s + 1)
                    if s < 2:
                        act.activation(V[q][:, 4 * s:4 * s + 4, :].rearrange("p c e -> p (c e)"), PJ, ACT.Copy
                                       ).then_inc(B.v_sb, 1)
                    else:
                        act.activation(V[q][0:JP, TT, :], PJ[0:JP, 0:P], ACT.Copy).then_inc(B.v_sb, 1)
                else:
                    u0, u1 = CTX_UNITS[s]
                    act.wait_ge(B.c_ps, 3 * n + s + 1)
                    act.activation(SCX[q][:, u0:u1, :].rearrange("p u j -> p (u j)"), PJ[:, 0:(u1 - u0) * JP],
                                   ACT.Copy).then_inc(B.c_sb, 1)

            def out_t_copy(act, f):
                if f:
                    act.wait_ge(o_lo, f)
                act.wait_ge(pv_done, 4 * (f + 1))
                act.activation(OR[:], PV[:], ACT.Copy).then_inc(o_raw, 1)

            @part(act_parts, st)
            def _(act, b):
                act.wait_ge(pads, 1)
                for kind, s in PIECES.values():
                    act_piece(act, F, 0, 0, kind, s)
                act.wait_ge(pads, 2)
                with act.Fori(0, turns) as p:
                    for i in range(UNITS + LAG):
                        j = i - LAG
                        if i >= 13 and (i - 13) % 8 == 0:
                            out_t_copy(act, (i - 13) // 8)
                        if 0 <= j < UNITS:
                            for r in (0, 2):
                                c0, c1 = ROUNDS[r]
                                if r == 2 and 1 <= i <= UNITS and (i - 1) % PU in PIECES:
                                    n = (i - 1) // PU
                                    act_piece(act, L, n, 1 - n, *PIECES[(i - 1) % PU])
                                act.wait_ge(t_ps, 3 * j + r + 1)
                                if r == 0 and j // 2 >= 2:
                                    act.wait_ge(pv_done, j // 2 - 1)
                                act.activation(PTS[(j // 2) % 2][j % 2][:, c0:c1, :].rearrange("p c q -> p (c q)"),
                                               TBANK[(3 * j + r) % 2][:, 0:(c1 - c0) * P], ACT.Copy
                                               ).then_inc(t_act, 1)
                        elif 1 <= i <= UNITS and (i - 1) % PU in PIECES:
                            n = (i - 1) // PU
                            act_piece(act, L, n, 1 - n, *PIECES[(i - 1) % PU])
                        if i < UNITS:
                            s_ = i % NPB
                            act.wait_ge(m_done, i + 1)
                            if i >= NPB:
                                act.wait_ge(t_ps, 3 * (i - NPB + 1))
                            act.activation(PR[s_][:, 0:N], SPS[i % 2], ACT.Exp, bias=nmax[:, s_:s_ + 1],
                                           accum_out=rsum[:, s_, 0:1]).then_inc(e_done, 1)
                            act.activation(PR[s_][:, N:KEYS], SCX[i // PU][:, i % PU, 0:J], ACT.Exp,
                                           bias=nmax[:, s_:s_ + 1], accum_out=rsum[:, s_, 1:2]).then_inc(ec_done, 1)
                    out_t_copy(act, 3)
                    end_turn(act, "act", turn, loop_signals)

            def dve_piece(dve, B, n, q, kind, s):
                if kind in "kq":
                    m = KQ // 2 * n + s + (3 if kind == "q" else 0)
                    a, z = SEG[s]
                    for hd in range(2):
                        dve.wait_ge(B.kq_hi, 2 * m + hd + 1)
                        own, other = ROWS[hd], ROWS[1 - hd]
                        hi, lo = ((KH[q][hd][own, a:z], KL[q][hd][own, a:z]) if kind == "k" else
                                  (QS[q][hd][own, a:z], QS[q][hd][other, a:z]))
                        dve.tensor_tensor(lo, RB[m % 2][own, 0:z - a], hi.bitcast(F32), ALU.subtract
                                          ).then_inc(B.kq_lo, 1)

            def ctx_max(dve, B, n, q):
                dve.wait_ge(B.c_sb, 3 * (n + 1))
                if mask:
                    dve.tensor_tensor(SCX[q][:, :, 0:J], SCX[q][:, :, 0:J], mrow[:].unsqueeze(1).broadcast_to(
                        [P, PU, J]), ALU.add).then_inc(B.c_masked, 1)
                    dve.wait_ge(B.c_masked, n + 1)
                dve.tensor_reduce(ncmax[q][:], SCX[q][:, :, 0:J], AX.X, ALU.max, negate=True).then_inc(B.c_max, 1)

            def out_t_lo(dve, f):
                cols = slice((f % 2) * HALF, (f % 2 + 1) * HALF)
                dve.wait_ge(o_hi, f + 1)
                dve.tensor_tensor(OTl[:, cols], OR[:], OTh[:, cols].bitcast(F32), ALU.subtract).then_inc(o_lo, 1)

            def add_out(dve, n, quarter):
                d_ = dest[:, 2 * quarter:2 * quarter + 2, :].rearrange("p t d -> p (t d)")
                dve.wait_ge(wo_ps, 4 * n + quarter + 1)
                if n:
                    dve.wait_ge(x_add, quarter + 1)
                scalar = 1.0 if gate is None else tg[:, gate:gate + 1]
                dve.scalar_tensor_tensor(d_, PJ, scalar, d_, ALU.mult, ALU.add).then_inc(x_add, 1)

            @part(dve_parts, st)
            def _(dve, b):
                for kind, s in PIECES.values():
                    dve_piece(dve, F, 0, 0, kind, s)
                if mask:
                    dve.wait_ge(mask_row, 1)
                ctx_max(dve, F, 0, 0)
                dve.wait_ge(F.c_max, 1)
                dve.wait_ge(pads, 2 if bias_row is None else 3)
                with dve.Fori(0, turns) as p:
                    for i in range(UNITS + LAG + 1):
                        j = i - LAG
                        if i >= 15 and (i - 15) % 8 == 0:
                            out_t_lo(dve, (i - 15) // 8)
                        if 0 <= j < UNITS:
                            c0, c1 = ROUNDS[1]
                            dve.wait_ge(t_ps, 3 * j + 2)
                            if j // 2 >= 2:
                                dve.wait_ge(pv_done, j // 2 - 1)
                            dve.tensor_copy(PTS[(j // 2) % 2][j % 2][:, c0:c1, :].rearrange("p c q -> p (c q)"),
                                            TBANK[(3 * j + 1) % 2][:, 0:(c1 - c0) * P]).then_inc(t_dve, 1)
                        if 1 <= i <= UNITS:
                            n, slot = (i - 1) // PU, (i - 1) % PU
                            if n and slot in OUT_BEFORE:
                                add_out(dve, 0, OUT_BEFORE[slot])
                            if slot in OUT_OWN:
                                add_out(dve, n, OUT_OWN[slot])
                            if slot == 13:
                                ctx_max(dve, L, n, 1 - n)
                        if i < UNITS:
                            s_ = i % NPB
                            dve.wait_ge(s_ps, i + 1)
                            if i >= NPB:
                                dve.wait_ge(m_done, i - NPB + 1)
                            dve.tensor_reduce(ntmax[:, s_:s_ + 1], SPS[i % 2], AX.X, ALU.max, negate=True
                                              ).then_inc(t_max, 1)
                            dve.wait_ge(t_max, i + 1)
                            if i == PU:
                                dve.wait_ge(L.c_max, 1)
                            if i >= NPB:
                                dve.wait_ge(ec_done, i - NPB + 1)
                            dve.tensor_tensor(nmax[:, s_:s_ + 1], ntmax[:, s_:s_ + 1],
                                              ncmax[i // PU][:, i % PU:i % PU + 1], ALU.min).then_inc(m_done, 1)
                        if 2 <= i <= UNITS + 1 and (i - 2) % PU in PIECES:
                            n = (i - 2) // PU
                            dve_piece(dve, L, n, 1 - n, *PIECES[(i - 2) % PU])
                        if 1 <= i <= UNITS:
                            s_ = (i - 1) % NPB
                            dve.wait_ge(ec_done, i)
                            if i - 1 >= NPB:
                                dve.wait_ge(i_done, i - NPB)
                            dve.tensor_tensor(rtot[:, s_:s_ + 1], rsum[:, s_, 0:1], rsum[:, s_, 1:2], ALU.add
                                              ).then_inc(total, 1)
                            dve.wait_ge(total, i)
                            if i - 1 >= NPB:
                                dve.wait_ge(p_done, i - NPB)
                            dve.reciprocal(rinv[:, s_:s_ + 1], rtot[:, s_:s_ + 1]).then_inc(i_done, 1)
                    out_t_lo(dve, 3)
                    for quarter in (1, 2, 3):
                        add_out(dve, 1, quarter)
                    end_turn(dve, "dve", turn, loop_signals)
            return Y

        ln_stage("ln1x")
        latent_attention(1, 8, [("L1_xattn_Wq1", 0), ("L1_xattn_Wk1", 0), ("L1_xattn_Wv1", 0),
                                ("L1_xattn_Wk2", 0), ("L1_xattn_Wv2", 0), ("L1_xattn_Wo", 0)],
                         (CTh, CTl), X, 1, BO1)

        ln_stage("ln1f")
        moe_scope = ExitStack()
        scope = moe_scope
        GPT = 2
        TURNS = EXPERTS // (EG * GPT)
        GW = EG * INTER
        SC = sb("router_scores", [P, TT, EXPERTS])
        gwr = sb("router_w", [P, DC, EXPERTS])
        gwh = sb("router_w_hi", [P, DC, EXPERTS], F32R)
        gwl = sb("router_w_lo", [P, DC, EXPERTS], F32R)
        lmax = sb("router_max", [P, TT])
        lshift = sb("router_shifted", [P, TT, EXPERTS])
        ex = sb("router_exp", [P, TT, EXPERTS])
        cmp_ = sb("router_compare", [P, TT, EXPERTS, EXPERTS])
        rank = sb("router_rank", [P, TT, EXPERTS])
        rank2 = sb("router_rank_ties", [P, TT, EXPERTS])
        lower = sb("router_lower_index", [P, EXPERTS, EXPERTS])
        selsum = sb("router_selected_sum", [P, TT])
        selinv = sb("router_selected_inv", [P, TT])
        W1, W3, W2 = 0, 1, 2
        mraw = [sb(f"experts_raw{i}", [P, 3, DC * GW]) for i in range(GPT)]
        mwh = [sb(f"experts_hi{i}", [P, 3, DC * GW], F32R) for i in range(GPT)]
        mwl = [sb(f"experts_lo{i}", [P, 3, DC * GW], F32R) for i in range(GPT)]
        mth = [sb(f"expert_tanh{i}", [P, GW]) for i in range(2)]
        mga = [sb(f"expert_gate{i}", [P, GW]) for i in range(2)]
        mac = [sb(f"expert_act{i}", [P, GW]) for i in range(2)]
        math_ = [sb(f"expert_act_t_hi{i}", [P, GW], F32R) for i in range(2)]
        matl = [sb(f"expert_act_t_lo{i}", [P, GW], F32R) for i in range(2)]
        moe_scope.close()
        scope = life

        gw_in = signal("router_w_in")
        gw_split = signal("router_w_split")
        lower_set = signal("router_lower_set")
        logits = signal("router_logits")
        r_steps = signal("router_steps")
        r_shift = signal("router_shift")
        r_exp = signal("router_exp_done")

        @part(sp_parts, "router")
        def _(sp, b):
            sp.dma_start(gwr[:], A["L1_ffn_gateT"].rearrange("(c p) e -> p c e", p=P)).then_inc(gw_in, 16)

        @part(pool_parts, "router")
        def _(pool, b):
            pool.memset(lower[:], 1.0).then_inc(lower_set, 1)
            pool.wait_ge(lower_set, 1)
            pool.affine_select(out=lower[:], in_=lower[:], compare_op=ALU.is_ge, fill=0.0, base=-1,
                               pattern=[[1, EXPERTS], [-1, EXPERTS]], channel_multiplier=0).then_inc(lower_set, 1)
            pool.wait_ge(gw_in, 16)
            hi_of(pool, gwh[:], gwr[:]).then_inc(gw_split, 1)
            pool.wait_ge(gw_split, 1)
            pool.tensor_tensor(gwl[:], gwr[:], gwh[:].bitcast(F32), ALU.subtract).then_inc(gw_split, 1)

        @part(pe_parts, "router")
        def _(pe, b):
            pe.wait_ge(gw_split, 2)
            for t in range(TT):
                tok = slice(t * P, (t + 1) * P)
                for c in range(DC):
                    ins = mm3(pe, PT[:, t * EXPERTS:(t + 1) * EXPERTS], XTh[:, c, tok], XTl[:, c, tok],
                              gwh[:, c, :], gwl[:, c, :], c == 0, c == DC - 1)
            ins.then_inc(logits, 1)

        @part(act_parts, "router")
        def _(act, b):
            act.wait_ge(r_shift, 1)
            act.activation(ex[:], lshift[:], ACT.Exp).then_inc(r_exp, 1)

        @part(dve_parts, "router")
        def _(dve, b):
            chain = Chain(dve, r_steps)
            lg = PT[:, 0:TT * EXPERTS].rearrange("p (t e) -> p t e", t=TT)
            dve.wait_ge(logits, 1)
            chain.step(dve.tensor_reduce(lmax[:], lg, AX.X, ALU.max))
            chain.settle()
            dve.tensor_tensor(lshift[:], lg, lmax[:].unsqueeze(2).broadcast_to([P, TT, EXPERTS]),
                              ALU.subtract).then_inc(r_shift, 1)
            dve.wait_ge(r_exp, 1)
            four = [P, TT, EXPERTS, EXPERTS]
            mine = ex[:].unsqueeze(3).broadcast_to(four)
            other = ex[:].unsqueeze(2).broadcast_to(four)
            chain.step(dve.tensor_tensor(cmp_[:], other, mine, ALU.is_gt))
            chain.settle()
            chain.step(dve.tensor_reduce(rank[:], cmp_[:], AX.X, ALU.add))
            chain.settle()
            chain.step(dve.tensor_tensor(cmp_[:], other, mine, ALU.is_equal))
            dve.wait_ge(lower_set, 2)
            chain.settle()
            chain.step(dve.tensor_tensor(cmp_[:], cmp_[:], lower[:].unsqueeze(1).broadcast_to(four), ALU.mult))
            chain.settle()
            chain.step(dve.tensor_reduce(rank2[:], cmp_[:], AX.X, ALU.add))
            chain.settle()
            chain.step(dve.tensor_tensor(rank[:], rank[:], rank2[:], ALU.add))
            chain.settle()
            chain.step(dve.scalar_tensor_tensor(SC[:], rank[:], float(TOP_K), ex[:], ALU.is_lt, ALU.mult))
            chain.settle()
            chain.step(dve.tensor_reduce(selsum[:], SC[:], AX.X, ALU.add))
            chain.settle()
            chain.step(dve.reciprocal(selinv[:], selsum[:]))
            chain.settle()
            chain.step(dve.scalar_tensor_tensor(SC[:], SC[:], 0.5, selinv[:].unsqueeze(2).broadcast_to(
                [P, TT, EXPERTS]), ALU.mult, ALU.mult))

        moe_loop = []

        def in_moe(name):
            s = semaphore("moe_" + name)
            moe_loop.append(s)
            return s

        m_first = signal("moe_first_weights")
        m_in = in_moe("weights_in")
        m_hi = in_moe("first_hi")
        m_lo = in_moe("first_lo")
        m_split = in_moe("second_split")
        m_gu = in_moe("gate_up")
        m_tanh = in_moe("tanh")
        m_gate = in_moe("gate")
        m_act = in_moe("act")
        m_tps = in_moe("act_transposed")
        m_thi = in_moe("act_t_hi")
        m_tlo = in_moe("act_t_lo")
        m_out = in_moe("out")
        m_x = in_moe("residual")
        moe_turn = turn_signals("moe")
        STEPS = GPT * TT
        MG = [BANKS[0], BANKS[2]]
        MU = [BANKS[1], BANKS[3]]
        MT = [BANKS[4], BANKS[5]]
        MO = [BANKS[6], BANKS[7]]

        def moe_load(sp, p, sem):
            for i in range(GPT):
                for k, name in ((W1, "L1_ffn_w1"), (W3, "L1_ffn_w3")):
                    for c in range(DC):
                        sp.dma_start(mraw[i][:, k, c * GW:(c + 1) * GW].rearrange("p (e i) -> p e i", e=EG),
                                     A[name].rearrange("e (c p) i -> c p e i", p=P)[c][
                                         :, bass.ds(p * (EG * GPT) + i * EG, EG), :]).then_inc(sem, 16)
                sp.dma_start(mraw[i][:, W2, :].rearrange("p (e d) -> p e d", e=EG),
                             A["L1_ffn_w2"].rearrange("e p d -> p e d")[
                                 :, bass.ds(p * (EG * GPT) + i * EG, EG), :]).then_inc(sem, 16)
        M_LOADS = 16 * GPT * (2 * DC + 1)

        @part(sp_parts, "moe")
        def _(sp, b):
            moe_load(sp, 0, m_first)
            sp.wait_ge(m_first, M_LOADS)
            with sp.Fori(1, TURNS) as p:
                sp.wait_ge(m_lo, 1)
                sp.wait_ge(m_split, 2)
                moe_load(sp, p, m_in)
                sp.wait_ge(m_in, M_LOADS)
                end_turn(sp, "sp", moe_turn, moe_loop)
            end_turn(sp, "sp", moe_turn, moe_loop)

        @part(pool_parts, "moe")
        def _(pool, b):
            pool.wait_ge(m_first, M_LOADS)
            with pool.Fori(0, TURNS) as p:
                hi_of(pool, mwh[1][:], mraw[1][:]).then_inc(m_split, 1)
                pool.wait_ge(m_split, 1)
                pool.tensor_tensor(mwl[1][:], mraw[1][:], mwh[1][:].bitcast(F32), ALU.subtract).then_inc(m_split, 1)
                end_turn(pool, "pool", moe_turn, moe_loop)

        @part(pe_parts, "moe")
        def _(pe, b):
            with pe.Fori(0, TURNS) as p:
                for i in range(STEPS + 2):
                    if i < STEPS:
                        g, t = i // TT, i % TT
                        tok = slice(t * P, (t + 1) * P)
                        if i == 0:
                            pe.wait_ge(m_lo, 1)
                        if i == TT:
                            pe.wait_ge(m_split, 2)
                        if i >= 2:
                            pe.wait_ge(m_act, i - 1)
                        for acc, k in ((MG[i % 2], W1), (MU[i % 2], W3)):
                            for c in range(DC):
                                w = slice(c * GW, (c + 1) * GW)
                                ins = mm3(pe, acc, XTh[:, c, tok], XTl[:, c, tok], mwh[g][:, k, w], mwl[g][:, k, w],
                                          c == 0, c == DC - 1)
                        ins.then_inc(m_gu, 1)
                    j = i - 1
                    if 0 <= j < STEPS:
                        pe.wait_ge(m_act, j + 1)
                        if j >= 2:
                            pe.wait_ge(m_tlo, j - 1)
                        for e in range(EG):
                            ins = pe.transpose(MT[j % 2][:, e * P:(e + 1) * P], mac[j % 2][:, e * P:(e + 1) * P], ident[:])
                        ins.then_inc(m_tps, 1)
                    o = i - 2
                    if 0 <= o < STEPS:
                        pe.wait_ge(m_tlo, o + 1)
                        if o >= 2:
                            pe.wait_ge(m_x, o - 1)
                        for e in range(EG):
                            col, w = slice(e * P, (e + 1) * P), slice(e * D, (e + 1) * D)
                            ins = mm3(pe, MO[o % 2][:, 0:D], math_[o % 2][:, col], matl[o % 2][:, col],
                                      mwh[o // TT][:, W2, w], mwl[o // TT][:, W2, w], e == 0, e == EG - 1)
                        ins.then_inc(m_out, 1)
                end_turn(pe, "pe", moe_turn, moe_loop)

        @part(act_parts, "moe")
        def _(act, b):
            act.wait_ge(m_first, M_LOADS)
            with act.Fori(0, TURNS) as p:
                act.activation(mwh[0][:], mraw[0][:], ACT.Copy).then_inc(m_hi, 1)
                for i in range(STEPS + 1):
                    if i < STEPS:
                        act.wait_ge(m_gu, i + 1)
                        if i >= 2:
                            act.wait_ge(m_gate, i - 1)
                        act.activation(mth[i % 2][:], MG[i % 2], ACT.Tanh, scale=0.5).then_inc(m_tanh, 1)
                    j = i - 1
                    if 0 <= j < STEPS:
                        act.wait_ge(m_tps, j + 1)
                        if j >= 2:
                            act.wait_ge(m_out, j - 1)
                        act.activation(math_[j % 2][:], MT[j % 2], ACT.Copy).then_inc(m_thi, 1)
                end_turn(act, "act", moe_turn, moe_loop)

        @part(dve_parts, "moe")
        def _(dve, b):
            with dve.Fori(0, TURNS) as p:
                dve.wait_ge(m_hi, 1)
                dve.tensor_tensor(mwl[0][:], mraw[0][:], mwh[0][:].bitcast(F32), ALU.subtract).then_inc(m_lo, 1)
                for i in range(STEPS + 2):
                    if i < STEPS:
                        g, t = i // TT, i % TT
                        dve.wait_ge(m_tanh, i + 1)
                        if i >= 2:
                            dve.wait_ge(m_act, i - 1)
                        dve.scalar_tensor_tensor(mga[i % 2][:], mth[i % 2][:], 1.0, MG[i % 2], ALU.add, ALU.mult
                                                 ).then_inc(m_gate, 1)
                        dve.wait_ge(m_gate, i + 1)
                        if i >= 2:
                            dve.wait_ge(m_tps, i - 1)
                        for e in range(EG):
                            col = slice(e * P, (e + 1) * P)
                            ins = dve.scalar_tensor_tensor(mac[i % 2][:, col], mga[i % 2][:, col], SC[:, t, g * EG + e:g * EG + e + 1],
                                                           MU[i % 2][:, col], ALU.mult, ALU.mult)
                        ins.then_inc(m_act, 1)
                    j = i - 1
                    if 0 <= j < STEPS:
                        dve.wait_ge(m_thi, j + 1)
                        dve.tensor_tensor(matl[j % 2][:], MT[j % 2], math_[j % 2][:].bitcast(F32), ALU.subtract
                                          ).then_inc(m_tlo, 1)
                    o = i - 2
                    if 0 <= o < STEPS:
                        t = o % TT
                        dve.wait_ge(m_out, o + 1)
                        if o >= TT:
                            dve.wait_ge(m_x, o - TT + 1)
                        dve.scalar_tensor_tensor(X[:, t, :], MO[o % 2][:, 0:D], tg[:, LAYERS + 1:LAYERS + 2],
                                                 X[:, t, :], ALU.mult, ALU.add).then_inc(m_x, 1)
                dve.tensor_copy(SC[:, :, 0:GPT * EG], SC[:, :, EXPERTS - GPT * EG:])
                end_turn(dve, "dve", moe_turn, moe_loop)

        next_layer()
        with buffers():
            XFL = sb("latents_t", [P, DC, N])
        ln_stage("ln2x", XF=XFL, gamma=2)
        Y2 = latent_attention(2, 16, [("L2_xattn_Wq", 0), ("L2_xattn_Wkv", 0), ("L2_xattn_Wkv", INNER),
                                      ("L2_xattn_Wout", 0)],
                              (CNTh, CNTl), None, None, None, mask="mask_BxS2_bf1")
        out2_steps = signal("out2_steps")

        @part(dve_parts, "out2")
        def _(dve, b):
            chain = Chain(dve, out2_steps)
            norm_stats(dve, chain, lambda t: Y2[:, t, :], TT)
            for t in range(TT):
                ins = dve.tensor_scalar(Y2[:, t, :], Y2[:, t, :], rstd[:, t:t + 1], nmr[:, t:t + 1], ALU.mult, ALU.add)
            chain.step(ins)
            chain.settle()
            all_rows = [P, TT, D]
            chain.step(dve.tensor_tensor(Y2[:], Y2[:], rowb[:, GO, :].unsqueeze(1).broadcast_to(all_rows), ALU.mult))
            chain.step(dve.tensor_tensor(X[:], X[:], rowb[:, BO, :].unsqueeze(1).broadcast_to(all_rows), ALU.add))
            chain.settle()
            chain.step(dve.tensor_tensor(X[:], X[:], Y2[:], ALU.add))

        WR, WK, WV = range(3)
        rwkv_scope = ExitStack()
        scope = rwkv_scope
        XF = sb("x_t", [P, DC, N])
        kraw = sb("mix_w_raw", [P, 3, DC * D])
        kwh = sb("mix_w_hi", [P, 3, DC * D], F32R)
        kwl = sb("mix_w_lo", [P, 3, DC * D], F32R)
        SH = [sb(f"mixed{m}", [P, DC, N]) for m in range(2)]
        SHh = [sb(f"mixed_hi{m}", [P, DC, N], F32R) for m in range(2)]
        SHl = [sb(f"mixed_lo{m}", [P, DC, N], F32R) for m in range(2)]
        KR = sb("k_relu", [P, DC, N])
        K2h = sb("k_squared_hi", [P, DC, N], F32R)
        K2l = sb("k_squared_lo", [P, DC, N], F32R)
        RT = sb("r_tanh", [P, TT, D])
        rwkv_scope.close()
        scope = life
        ln_stage("ln2f", XF=XF)

        MIX = [(m, c, h) for m in (1, 0) for c in range(DC) for h in range(NHALF)]
        kw_in = signal("mix_w_in")
        kw_split = signal("mix_w_split")
        s_zero = signal("mix_first_token_zero")
        s_prev = signal("mix_prev")
        s_mix = signal("mix_done")
        s_hi = signal("mix_hi")
        s_lo = signal("mix_lo")
        k_ps = signal("mix_k")
        k_relu = signal("mix_k_relu")
        k_hi = signal("mix_k_hi")
        k_sq = signal("mix_k_squared")
        k_lo = signal("mix_k_lo")
        r_ps = signal("mix_r")
        r_tanh = signal("mix_r_tanh")
        v_ps = signal("mix_v")
        v_gated = signal("mix_v_gated")
        v_x = signal("mix_residual")

        @part(sp_parts, "rwkv")
        def _(sp, b):
            for k, name in ((WR, "L2_ffn_rT"), (WK, "L2_ffn_kT"), (WV, "L2_ffn_vT")):
                sp.dma_start(kraw[:, k, :].rearrange("p (c d) -> p c d", c=DC),
                             A[name].rearrange("(c p) d -> p c d", p=P)).then_inc(kw_in, 16)

        @part(pool_parts, "rwkv")
        def _(pool, b):
            for m in range(2):
                ins = pool.memset(SH[m][:, :, 0:1], 0.0)
            ins.then_inc(s_zero, 1)
            pool.wait_ge(kw_in, 48)
            hi_of(pool, kwh[:], kraw[:]).then_inc(kw_split, 1)
            pool.wait_ge(kw_split, 1)
            pool.tensor_tensor(kwl[:], kraw[:], kwh[:].bitcast(F32), ALU.subtract).then_inc(kw_split, 1)

        @part(act_parts, "rwkv")
        def _(act, b):
            for m, c, h in MIX:
                a, z = max(h * HALF, 1), (h + 1) * HALF
                act.activation(SH[m][:, c, a:z], XF[:, c, a - 1:z - 1], ACT.Copy, scale=omm[:, c, m:m + 1]
                               ).then_inc(s_prev, 1)
            for q, (m, c, h) in enumerate(MIX):
                cols = slice(h * HALF, (h + 1) * HALF)
                act.wait_ge(s_mix, q + 1)
                act.activation(SHh[m][:, c, cols], SH[m][:, c, cols], ACT.Copy).then_inc(s_hi, 1)
            for q, (c, h) in enumerate(QUADS):
                cols = slice(h * HALF, (h + 1) * HALF)
                act.wait_ge(k_ps, q + 1)
                act.activation(KR[:, c, cols], BANKS[q], ACT.Relu).then_inc(k_relu, 1)
                act.wait_ge(k_relu, q + 1)
                act.activation(K2h[:, c, cols], KR[:, c, cols], ACT.Square).then_inc(k_hi, 1)
            for q in range(4):
                act.wait_ge(r_ps, q + 1)
                act.activation(RT[:, 2 * q:2 * q + 2, :].rearrange("p t d -> p (t d)"), BANKS[4 + q], ACT.Tanh,
                               scale=0.5).then_inc(r_tanh, 1)

        @part(dve_parts, "rwkv")
        def _(dve, b):
            dve.wait_ge(s_zero, 1)
            for q, (m, c, h) in enumerate(MIX):
                cols = slice(h * HALF, (h + 1) * HALF)
                dve.wait_ge(s_prev, q + 1)
                dve.scalar_tensor_tensor(SH[m][:, c, cols], XF[:, c, cols], mus[:, c, m:m + 1], SH[m][:, c, cols],
                                         ALU.mult, ALU.add).then_inc(s_mix, 1)
            for q, (m, c, h) in enumerate(MIX):
                cols = slice(h * HALF, (h + 1) * HALF)
                dve.wait_ge(s_hi, q + 1)
                dve.tensor_tensor(SHl[m][:, c, cols], SH[m][:, c, cols], SHh[m][:, c, cols].bitcast(F32),
                                  ALU.subtract).then_inc(s_lo, 1)
            for q, (c, h) in enumerate(QUADS):
                cols = slice(h * HALF, (h + 1) * HALF)
                dve.wait_ge(k_hi, q + 1)
                dve.tensor_tensor(KR[:, c, cols], KR[:, c, cols], KR[:, c, cols], ALU.mult).then_inc(k_sq, 1)
                dve.wait_ge(k_sq, q + 1)
                dve.tensor_tensor(K2l[:, c, cols], KR[:, c, cols], K2h[:, c, cols].bitcast(F32), ALU.subtract
                                  ).then_inc(k_lo, 1)
            for q in range(4):
                rt = RT[:, 2 * q:2 * q + 2, :].rearrange("p t d -> p (t d)")
                xt = X[:, 2 * q:2 * q + 2, :].rearrange("p t d -> p (t d)")
                dve.wait_ge(v_ps, q + 1)
                dve.wait_ge(r_tanh, q + 1)
                dve.scalar_tensor_tensor(rt, rt, 1.0, BANKS[q], ALU.add, ALU.mult).then_inc(v_gated, 1)
                dve.wait_ge(v_gated, q + 1)
                dve.scalar_tensor_tensor(xt, rt, htg2[:, 0:1], xt, ALU.mult, ALU.add).then_inc(v_x, 1)

        @part(pe_parts, "rwkv")
        def _(pe, b):
            pe.wait_ge(kw_split, 2)
            pe.wait_ge(s_lo, 4)
            for q, (d, h) in enumerate(QUADS):
                cols = slice(h * HALF, (h + 1) * HALF)
                for c in range(DC):
                    w = slice(c * D + d * P, c * D + (d + 1) * P)
                    ins = mm3(pe, BANKS[q], kwh[:, WK, w], kwl[:, WK, w], SHh[1][:, c, cols], SHl[1][:, c, cols],
                              c == 0, c == DC - 1)
                ins.then_inc(k_ps, 1)
            pe.wait_ge(s_lo, 8)
            for x_h, x_l, wi, b0, done in ((SHh[0], SHl[0], WR, 4, r_ps), (K2h, K2l, WV, 0, v_ps)):
                if done is v_ps:
                    pe.wait_ge(k_lo, 4)
                for t in range(TT):
                    tok = slice(t * P, (t + 1) * P)
                    for c in range(DC):
                        w = slice(c * D, (c + 1) * D)
                        ins = mm3(pe, BANKS[b0 + t // 2][:, (t % 2) * D:(t % 2 + 1) * D], x_h[:, c, tok],
                                  x_l[:, c, tok], kwh[:, wi, w], kwl[:, wi, w], c == 0, c == DC - 1)
                    if t % 2:
                        ins.then_inc(done, 1)

        next_layer()
        ln_stage("ln3x")
        with buffers():
            context_attention(3, 8, [by_cols("L3_xattn_wkT"), by_cols("L3_xattn_wvT"), by_rows("L3_xattn_wq")],
                              (D // HEADS) ** -0.5, 3, False, None)

        PAIRS = AE // 2
        WIDE = AE * AH
        ae_scope = ExitStack()
        scope = ae_scope
        XFA = sb("x_t_full", [P, DC, N])
        eraw = sb("enc_raw", [P, DC, WIDE])
        eh = sb("enc_hi", [P, DC, WIDE], F32R)
        el = sb("enc_lo", [P, DC, WIDE], F32R)
        draw = sb("dec_raw", [P, PAIRS, 2, D])
        dh = sb("dec_hi", [P, AE, D], F32R)
        dl = sb("dec_lo", [P, AE, D], F32R)
        hid = [sb(f"enc_hidden{i}", [P, HALF]) for i in range(2)]
        hidh = [sb(f"enc_hidden_hi{i}", [P, HALF], F32R) for i in range(2)]
        hidl = [sb(f"enc_hidden_lo{i}", [P, HALF], F32R) for i in range(2)]
        diff = [sb(f"recon_diff{i}", [P, HALF]) for i in range(2)]
        sqr = sb("recon_squares", [P, HALF])
        loss4 = sb("loss_parts", [P, AE, DC * NHALF])
        loss1 = sb("loss_sums", [P, AE])
        loss = sb("losses", [P, AE])
        lmin = sb("loss_min", [P, 1])
        iota = sb("adapter_numbers", [P, AE])
        iotab = sb("adapter_numbers_more", [P, AE])
        hot = sb("adapter_one_hot", [P, AE])
        top1 = sb("adapter_top1", [P, 1])
        adp = sb("adapter_connected", [P, 1])
        wrap = sb("adapter_wrap", [P, 1])
        braw = sb("base_raw", [P, DC, D])
        bh = sb("base_hi", [P, DC, D], F32R)
        bl = sb("base_lo", [P, DC, D], F32R)
        downs = sb("down_all", [P, DC, AE, AH])
        ups = sb("up_all", [P, AE, D])
        bups = sb("b_up_all", [P, AE, D])
        down = [sb(f"down{i}", [P, DC, AH]) for i in range(2)]
        up = [sb(f"up{i}", [P, D]) for i in range(2)]
        bup = [sb(f"b_up{i}", [P, D]) for i in range(2)]
        bdn = [sb(f"b_down{i}", [P, 1]) for i in range(2)]
        downh = sb("down_hi", [P, DC, 2, AH], F32R)
        downl = sb("down_lo", [P, DC, 2, AH], F32R)
        uph = sb("up_hi", [P, D], F32R)
        upl = sb("up_lo", [P, D], F32R)
        mid = sb("mid", [P, N])
        mids = sb("mid_stack", [P, N], F32R)
        ae_scope.close()
        scope = life
        ln_stage("ln3f", XF=XFA)

        UNITS3 = [(k, h) for k in range(PAIRS) for h in range(NHALF)]
        NU = len(UNITS3)
        ew_in = signal("enc_in")
        dw_in = signal("dec_in")
        ae_zero = signal("dec_zeros")
        ew_split = signal("enc_dec_split")
        e_ps = signal("enc_ready")
        e_relu = signal("enc_relu")
        e_hi = signal("enc_hidden_hi_ready")
        e_lo = signal("enc_hidden_lo_ready")
        d_ps = signal("dec_ready")
        d_diff = signal("dec_diff")
        d_sq = signal("dec_squared")
        iota_set = signal("adapter_numbers_set")
        l_sum = signal("loss_summed")
        l_all = signal("loss_over_partitions")
        a_steps = signal("adapter_steps")

        @part(sp_parts, "route")
        def _(sp, b):
            for c in range(DC):
                sp.dma_start(eraw[:, c, :].rearrange("p (n h) -> p n h", n=AE),
                             A["L3_ffn_W_enc"].rearrange("n (c p) h -> c p n h", p=P)[c]).then_inc(ew_in, 16)
            for r in range(2):
                sp.dma_start(draw[r * AH:(r + 1) * AH, :, r, :],
                             A["L3_ffn_W_dec"].rearrange("(k r) h d -> r h k d", r=2)[r]).then_inc(dw_in, 16)
            sp.wait_ge(ew_in, 16 * DC)

        @part(pool_parts, "route")
        def _(pool, b):
            for r in range(2):
                pool.memset(draw[r * AH:(r + 1) * AH, :, 1 - r, :], 0.0).then_inc(ae_zero, 1)
                pool.wait_ge(ae_zero, r + 1)
            pool.wait_ge(ew_in, 16 * DC)
            hi_of(pool, eh[:], eraw[:]).then_inc(ew_split, 1)
            pool.wait_ge(ew_split, 1)
            pool.tensor_tensor(el[:], eraw[:], eh[:].bitcast(F32), ALU.subtract).then_inc(ew_split, 1)
            pool.wait_ge(dw_in, 32)
            dr = draw[:].rearrange("p k r d -> p (k r) d")
            hi_of(pool, dh[:], dr).then_inc(ew_split, 1)
            pool.wait_ge(ew_split, 3)
            pool.tensor_tensor(dl[:], dr, dh[:].bitcast(F32), ALU.subtract).then_inc(ew_split, 1)
            for n in range(AE):
                pool.memset(iota[:, n:n + 1], float(n)).then_inc(iota_set, 1)

        @part(pe_parts, "route")
        def _(pe, b):
            pe.wait_ge(ew_split, 2)
            for u in range(NU + 1):
                if u < NU:
                    k, h = UNITS3[u]
                    cols = slice(h * HALF, (h + 1) * HALF)
                    if u >= 2:
                        pe.wait_ge(e_relu, u - 1)
                    for c in range(DC):
                        w = slice(k * P, (k + 1) * P)
                        ins = mm3(pe, BANKS[u % 2], eh[:, c, w], el[:, c, w], XTh[:, c, cols], XTl[:, c, cols],
                                  c == 0, c == DC - 1)
                    ins.then_inc(e_ps, 1)
                v = u - 1
                if v >= 0:
                    k, h = UNITS3[v]
                    if v == 0:
                        pe.wait_ge(ew_split, 4)
                    pe.wait_ge(e_lo, v + 1)
                    for q in range(4):
                        n, c = 2 * k + q // 2, q % 2
                        if v:
                            pe.wait_ge(d_diff, 4 * (v - 1) + q + 1)
                        w = slice(c * P, (c + 1) * P)
                        mm3(pe, BANKS[2 + q], dh[:, n, w], dl[:, n, w], hidh[v % 2][:], hidl[v % 2][:], True, True
                            ).then_inc(d_ps, 1)
            pe.wait_ge(l_sum, 1)
            pe.matmul(BANKS[6][:, 0:AE], ones[:], loss1[:], start=True, stop=True).then_inc(l_all, 1)

        @part(act_parts, "route")
        def _(act, b):
            for u in range(NU + 1):
                if u < NU:
                    k, h = UNITS3[u]
                    act.wait_ge(e_ps, u + 1)
                    if u >= 2:
                        act.wait_ge(e_lo, u - 1)
                    act.activation(hid[u % 2][:], BANKS[u % 2], ACT.Relu, bias=benc[:, k:k + 1]).then_inc(e_relu, 1)
                    act.wait_ge(e_relu, u + 1)
                    if u >= 2:
                        act.wait_ge(d_ps, 4 * (u - 1))
                    act.activation(hidh[u % 2][:], hid[u % 2][:], ACT.Copy).then_inc(e_hi, 1)
                v = u - 1
                if v >= 0:
                    k, h = UNITS3[v]
                    for q in range(4):
                        n, c = 2 * k + q // 2, q % 2
                        s = 4 * v + q
                        act.wait_ge(d_diff, s + 1)
                        if s:
                            act.wait_ge(d_sq, s)
                        act.activation(sqr[:], diff[s % 2][:], ACT.Square,
                                       accum_out=loss4[:, n, c * NHALF + h:c * NHALF + h + 1]).then_inc(d_sq, 1)

        @part(dve_parts, "route")
        def _(dve, b):
            for u in range(NU + 1):
                if u < NU:
                    dve.wait_ge(e_hi, u + 1)
                    if u >= 2:
                        dve.wait_ge(d_ps, 4 * (u - 1))
                    dve.tensor_tensor(hidl[u % 2][:], hid[u % 2][:], hidh[u % 2][:].bitcast(F32), ALU.subtract
                                      ).then_inc(e_lo, 1)
                v = u - 1
                if v >= 0:
                    k, h = UNITS3[v]
                    for q in range(4):
                        n, c = 2 * k + q // 2, q % 2
                        s = 4 * v + q
                        dve.wait_ge(d_ps, s + 1)
                        if s >= 2:
                            dve.wait_ge(d_sq, s - 1)
                        dve.scalar_tensor_tensor(diff[s % 2][:], BANKS[2 + q], bdec[:, n, c:c + 1],
                                                 XFA[:, c, h * HALF:(h + 1) * HALF], ALU.add, ALU.subtract
                                                 ).then_inc(d_diff, 1)
            dve.wait_ge(d_sq, 4 * NU)
            dve.tensor_reduce(loss1[:], loss4[:], AX.X, ALU.add).then_inc(l_sum, 1)
            chain = Chain(dve, a_steps)
            dve.wait_ge(l_all, 1)
            dve.wait_ge(iota_set, AE)
            chain.step(dve.tensor_copy(loss[:], BANKS[6][:, 0:AE]))
            chain.step(dve.tensor_scalar(iotab[:], iota[:], float(-AE), None, ALU.add))
            chain.settle()
            chain.step(dve.tensor_reduce(lmin[:], loss[:], AX.X, ALU.min))
            chain.settle()
            chain.step(dve.scalar_tensor_tensor(hot[:], loss[:], lmin[:, 0:1], iotab[:], ALU.is_equal, ALU.mult))
            chain.settle()
            chain.step(dve.tensor_reduce(top1[:], hot[:], AX.X, ALU.min))
            chain.settle()
            chain.step(dve.scalar_tensor_tensor(hot[:], iotab[:], top1[:, 0:1], cidx[:], ALU.is_equal, ALU.mult))
            chain.settle()
            chain.step(dve.tensor_reduce(adp[:], hot[:], AX.X, ALU.add))
            chain.settle()
            chain.step(dve.tensor_scalar(wrap[:], adp[:], 0.0, float(AE), ALU.is_lt, ALU.mult))
            chain.settle()
            chain.step(dve.tensor_tensor(adp[:], adp[:], wrap[:], ALU.add))
            chain.settle()
            chain.step(dve.tensor_scalar(adp[:], adp[:], 0.0, float(AE - 1), ALU.max, ALU.min))
            chain.settle()
            chain.step(dve.tensor_scalar(hot[:], iota[:], adp[:, 0:1], None, ALU.is_equal))

        aw_in = signal("base_in")
        aw_sel_in = signal("adapters_in")
        aw_split = signal("base_split")
        pick = signal("adapter_picks")
        pick_hi = signal("adapter_hi")
        pick_lo = signal("adapter_lo")
        mid_ps = signal("mid_ready")
        mid_relu = signal("mid_relu")
        mid_hi = signal("mid_hi")
        mid_lo = signal("mid_lo")
        ad_ps = signal("adapted_ready")
        ad_row = signal("adapted_bias")
        ad_x = signal("adapted_residual")

        @part(sp_parts, "adapt")
        def _(sp, b):
            sp.dma_start(braw[:], A["L3_ffn_W_base"].rearrange("(c p) e -> p c e", p=P)).then_inc(aw_in, 16)
            for c in range(DC):
                sp.dma_start(downs[:, c, :, :], A["L3_ffn_W_down"].rearrange("n (c p) h -> c p n h", p=P)[c]
                             ).then_inc(aw_sel_in, 16)
            for r in range(2):
                sp.dma_start(ups[r * AH:(r + 1) * AH, :, :], A["L3_ffn_W_up"].rearrange("n h d -> h n d")
                             ).then_inc(aw_sel_in, 16)
            sp.dma_start(bups[:].rearrange("p n d -> p (n d)"), A["L3_ffn_b_up"].rearrange(
                "(a n) d -> a (n d)", a=1).broadcast_to([P, AE * D])).then_inc(aw_sel_in, 16)

        @part(pool_parts, "adapt")
        def _(pool, b):
            pool.wait_ge(aw_in, 16)
            hi_of(pool, bh[:], braw[:]).then_inc(aw_split, 1)
            pool.wait_ge(aw_split, 1)
            pool.tensor_tensor(bl[:], braw[:], bh[:].bitcast(F32), ALU.subtract).then_inc(aw_split, 1)

        @part(dve_parts, "adapt")
        def _(dve, b):
            chain = Chain(dve, pick)
            dve.wait_ge(aw_sel_in, 16 * (DC + 3))
            sources = [(down, lambda n: downs[:, :, n, :]), (up, lambda n: ups[:, n, :]),
                       (bup, lambda n: bups[:, n, :]), (bdn, lambda n: bdown[:, n:n + 1])]
            for n in range(AE):
                for dst, src in sources:
                    d_, own = dst[n % 2][:], hot[:, n:n + 1]
                    chain.step(dve.tensor_scalar(d_, src(n), own, None, ALU.mult) if n == 0 else
                               dve.scalar_tensor_tensor(d_, src(n), own, dst[(n + 1) % 2][:], ALU.mult, ALU.add))
                chain.settle()
            dve.wait_ge(pick_hi, 2)
            twice = down[1][:].unsqueeze(2).broadcast_to([P, DC, 2, AH])
            dve.tensor_tensor(downl[:], twice, downh[:].bitcast(F32), ALU.subtract).then_inc(pick_lo, 1)
            dve.tensor_tensor(upl[:], up[1][:], uph[:].bitcast(F32), ALU.subtract).then_inc(pick_lo, 1)
            gate = tg[:, 2 * LAYERS - 1:2 * LAYERS]
            dve.tensor_tensor(bup[0][:], bup[1][:], rowb[:, BBASE, :], ALU.add).then_inc(ad_row, 1)
            dve.wait_ge(ad_row, 1)
            dve.scalar_tensor_tensor(X[:], bup[0][:].unsqueeze(1).broadcast_to([P, TT, D]), gate, X[:],
                                     ALU.mult, ALU.add).then_inc(ad_row, 1)
            for h in range(NHALF):
                cols = slice(h * HALF, (h + 1) * HALF)
                dve.wait_ge(mid_hi, h + 1)
                dve.tensor_tensor(mids[AH:P, cols], mid[AH:P, cols], mids[AH:P, cols].bitcast(F32), ALU.subtract
                                  ).then_inc(mid_lo, 1)
            dve.wait_ge(ad_row, 2)
            for q in range(4):
                xt = X[:, 2 * q:2 * q + 2, :].rearrange("p t d -> p (t d)")
                dve.wait_ge(ad_ps, q + 1)
                dve.scalar_tensor_tensor(xt, BANKS[q], gate, xt, ALU.mult, ALU.add).then_inc(ad_x, 1)

        @part(act_parts, "adapt")
        def _(act, b):
            act.wait_ge(pick, 4 * AE)
            for r in range(2):
                ins = act.activation(downh[:, :, r, :], down[1][:], ACT.Copy)
            ins.then_inc(pick_hi, 1)
            act.activation(uph[:], up[1][:], ACT.Copy).then_inc(pick_hi, 1)
            for h in range(NHALF):
                cols = slice(h * HALF, (h + 1) * HALF)
                act.wait_ge(mid_ps, h + 1)
                act.activation(mid[:, cols], BANKS[6 + h], ACT.Relu, bias=bdn[1][:, 0:1]).then_inc(mid_relu, 1)
                act.wait_ge(mid_relu, h + 1)
                act.activation(mids[:, cols], mid[:, cols], ACT.Copy).then_inc(mid_hi, 1)

        @part(pe_parts, "adapt")
        def _(pe, b):
            pe.wait_ge(pick_lo, 2)
            for h in range(NHALF):
                cols = slice(h * HALF, (h + 1) * HALF)
                for c in range(DC):
                    ins = mm3(pe, BANKS[6 + h], downh[:, c, :, :].rearrange("p r h -> p (r h)"),
                              downl[:, c, :, :].rearrange("p r h -> p (r h)"),
                              XTh[:, c, cols], XTl[:, c, cols], c == 0, c == DC - 1)
                ins.then_inc(mid_ps, 1)
            pe.wait_ge(aw_split, 2)
            pe.wait_ge(mid_lo, 2)
            for t in range(TT):
                tok = slice(t * P, (t + 1) * P)
                acc = BANKS[t // 2][:, (t % 2) * D:(t % 2 + 1) * D]
                for c in range(DC):
                    mm3(pe, acc, XTh[:, c, tok], XTl[:, c, tok], bh[:, c, :], bl[:, c, :], c == 0, False)
                pe.matmul(acc, mids[:, tok], uph[:], start=False, stop=False)
                ins = pe.matmul(acc, mids[:, tok], upl[:], start=False, stop=True)
                if t % 2:
                    ins.then_inc(ad_ps, 1)
        next_layer()
        stored = signal("x_stored")

        @part(sp_parts, "store")
        def _(sp, b):
            sp.dma_start(out[bass.ds(b * N, N), :].rearrange("(t p) d -> p t d", p=P), X[:]
                         ).then_inc(stored, 16)
            sp.wait_ge(stored, 16)

        next_layer()

        block = life.enter_context(nc.Block())

        @block.sync
        def _(sp):
            sp_ternary(sp)
            sp_consts(sp)
            sp.wait_ge(const_set, 7)
            with sp.Fori(0, NB) as b:
                run(sp, "sp", b, sp_parts)

        @block.gpsimd
        def _(pool):
            pool_consts(pool)
            with pool.Fori(0, NB) as b:
                run(pool, "pool", b, pool_parts)

        @block.scalar
        def _(act):
            act_consts(act)
            with act.Fori(0, NB) as b:
                run(act, "act", b, act_parts)

        @block.vector
        def _(dve):
            dve_consts(dve)
            dve_ternary(dve)
            with dve.Fori(0, NB) as b:
                run(dve, "dve", b, dve_parts)

        @block.tensor
        def _(pe):
            pe.wait_ge(const_set, 7)
            pe_ternary(pe)
            with pe.Fori(0, NB) as b:
                run(pe, "pe", b, pe_parts)


_FLAT = {"x": (NB * N, D), "ctx_1024": (NB * J, D), "mask_BxSxS2_bk1": (NB * N, J)}
_TRANSPOSED = {"L0_xattn_Wq": "L0_xattn_WqT", "L0_ffn_w_gate": "L0_ffn_gT", "L0_ffn_w_up": "L0_ffn_uT",
               "L0_ffn_w_down": "L0_ffn_dT", "L1_ffn_gate_w": "L1_ffn_gateT", "L2_ffn_W_r": "L2_ffn_rT",
               "L2_ffn_W_k": "L2_ffn_kT", "L2_ffn_W_v": "L2_ffn_vT", "L3_xattn_wk": "L3_xattn_wkT",
               "L3_xattn_wv": "L3_xattn_wvT"}


def kernel(**inputs):
    import numpy as _np
    import concourse.bacc as _bacc
    from concourse import mybir as _mybir
    from concourse.bass_utils import run_bass_kernel_spmd as _run

    nc = _bacc.Bacc("TRN2", target_bir_lowering=False, num_devices=1)
    arrays, args = {}, {}
    for name, a in inputs.items():
        a = _np.asarray(a)
        if name in _FLAT:
            a = a.reshape(_FLAT[name])
        if name in _TRANSPOSED:
            name, a = _TRANSPOSED[name], a.T
        a = _np.ascontiguousarray(a)
        arrays[f"in_{name}_dram"] = a
        args[name] = nc.dram_tensor(f"in_{name}_dram", a.shape, _mybir.dt.from_np(a.dtype),
                                    kind="ExternalInput").ap()
    out = nc.dram_tensor("out_0_dram", (NB * N, D), F32, kind="ExternalOutput").ap()
    flamingo_kernel(nc, args, out)
    r = _run(nc, [arrays], core_ids=[0])
    return r.results[0]["out_0_dram"].reshape(NB, N, D)
```

```python
from contextlib import ExitStack, contextmanager

import concourse.bass as bass
from concourse import mybir

ALU = mybir.AluOpType
ACT = mybir.ActivationFunctionType
AX = mybir.AxisListType
F32 = mybir.dt.float32
F32R = mybir.dt.float32r
BF16 = mybir.dt.bfloat16
I32 = mybir.dt.int32
U8 = mybir.dt.uint8

P = 128
NB = 2
N = 1024
D = 256
DC = D // P
TT = N // P
HALF = 512
NHALF = N // HALF
J = 77
JP = J + 1
HEADS = 16
HJ = HEADS * JP
HJC = -(-HJ // P)
BANK_HEADS = [(0, 6), (6, 11), (11, 16)]
KEYS = N + J
KEYSP = N + JP
KC = TT + 1
DH = 64
EPS = 1e-5
MAGIC = 12582912.0
RSQRT_SEED = 1597463007.0
NEWTON = 3
MASKED = 2.0 ** 127
NEG_MAX = -3.4028234663852886e38
STAT_STEPS = 4 + 3 * NEWTON + 1
EXPERTS = 16
TOP_K = 4
INTER = 128
EG = 4
AE = 8
AH = 64
INNER = 1024
LAYERS = 4


class Chain:

    def __init__(self, eng, sem):
        self.eng, self.sem, self.n = eng, sem, 0

    def step(self, ins):
        ins.then_inc(self.sem, 1)
        self.n += 1

    def settle(self):
        self.eng.wait_ge(self.sem, self.n)


def flamingo_kernel(nc, A, out):
    with ExitStack() as life:
        def sb(name, shape, dt=F32):
            return scope.enter_context(nc.sbuf_tensor(name, shape, dt))

        sem_scope = ExitStack()
        layer_signals = []

        def semaphore(name):
            return sem_scope.enter_context(nc.semaphore(name))

        def signal(name):
            s = semaphore(name)
            layer_signals.append(s)
            return s

        @contextmanager
        def buffers():
            nonlocal scope
            with ExitStack() as scope:
                yield
            scope = life

        scope = life
        X = sb("X", [P, TT, D])
        XN = sb("XN", [P, TT, D])
        XTh = sb("XTh", [P, DC, N], F32R)
        XTl = sb("XTl", [P, DC, N], F32R)
        C = sb("C", [P, D])
        CN = sb("CN", [P, D])
        CTh = sb("CTh", [P, DC, JP], F32R)
        CTl = sb("CTl", [P, DC, JP], F32R)
        CNT = sb("CNT", [P, DC, JP])
        CNTh = sb("CNTh", [P, DC, JP], F32R)
        CNTl = sb("CNTl", [P, DC, JP], F32R)
        ident = sb("ident", [P, P])
        identb = sb("identb", [P, P], BF16)
        ones = sb("ones", [P, P])
        gates = sb("gates", [P, 2 * LAYERS])
        tg = sb("tg", [P, 2 * LAYERS])
        stats = sb("stats", [P, TT, 6])
        mv = sb("mv", [P, TT, 2])
        var = sb("var", [P, TT])
        rstd = sb("rstd", [P, TT])
        ntmp = sb("ntmp", [P, TT])
        nmr = sb("nmr", [P, TT])
        gl = sb("gl", [P, DC, 4])
        mus = sb("mus", [P, DC, 2])
        htg2 = sb("half_gate2", [P, 1])
        omm = sb("omm", [P, DC, 2])
        benc = sb("b_enc_cols", [P, AE // 2])
        bdec = sb("b_dec_cols", [P, AE, DC])
        bdown = sb("b_down_cols", [P, AE])
        cidx_i = sb("connected_i", [P, AE], I32)
        cidx = sb("connected", [P, AE])
        rowb = sb("rowb", [P, 5, D])
        BO0, BO1, GO, BO, BBASE = range(5)

        wq = [sb(f"ternary{n}", [P, DC * INNER], BF16) for n in range(3)]
        wabs = sb("weight_abs_sums", [P, 3])
        wmean = sb("weight_mean", [P, 3])
        winv = sb("weight_inv_mean", [P, 3])

        PA = life.enter_context(nc.psum_tensor("PA", [P, 3 * HALF], F32))
        PB = life.enter_context(nc.psum_tensor("PB", [P, 3 * HALF], F32))
        PT = life.enter_context(nc.psum_tensor("PT", [P, HALF], F32))
        PV = life.enter_context(nc.psum_tensor("PV", [P, HALF], F32))
        BANKS = [PA[:, 0:512], PA[:, 512:1024], PA[:, 1024:1536],
                 PB[:, 0:512], PB[:, 512:1024], PB[:, 1024:1536], PT[:, :], PV[:, :]]

        LAYER_STAGES = [["load", "ln0x", "prep0", "attn0", "ln0f", "bitq", "bit"],
                        ["ln1x", "attn1", "ln1f", "router", "moe"],
                        ["ln2x", "attn2", "out2", "ln2f", "rwkv"],
                        ["ln3x", "prep3", "attn3", "ln3f", "route", "adapt"]]
        LAYER_STAGES.append(["store"])
        ends = {k: life.enter_context(nc.semaphore(f"{k}_stage_end")) for k in ("pe", "act", "dve", "pool", "sp")}

        def turn_signals(name):
            return (semaphore(f"{name}_arrived"), {k: semaphore(f"{name}_go_{k}") for k in ends if k != "pool"})

        def end_turn(eng, me, turn, signals):
            arrived, go = turn
            eng.drain().then_inc(arrived, 1)
            if me == "pool":
                eng.wait_ge(arrived, len(ends))
                for s in (*signals, arrived):
                    eng.sem_clear(s)
                for k in go:
                    eng.sem_inc(go[k], 1)
            else:
                eng.wait_ge(go[me], 1)
                eng.sem_clear(go[me])

        layer_turn = (life.enter_context(nc.semaphore("layer_arrived")),
                      {k: life.enter_context(nc.semaphore(f"layer_go_{k}")) for k in ends if k != "pool"})
        signals_of = []

        def next_layer():
            nonlocal sem_scope, layer_signals
            signals_of.append(layer_signals + list(ends.values()))
            sem_scope.close()
            sem_scope, layer_signals = ExitStack(), []

        def run(eng, me, b, parts):
            for stages, signals in zip(LAYER_STAGES, signals_of[:len(LAYER_STAGES) - 1] + signals_of[-1:]):
                for s, name in enumerate(stages):
                    if s:
                        for other in ends:
                            if other != me:
                                eng.wait_ge(ends[other], s)
                    if name in parts:
                        parts[name](eng, b)
                    eng.drain().then_inc(ends[me], 1)
                end_turn(eng, me, layer_turn, signals)

        pe_parts, act_parts, dve_parts, pool_parts, sp_parts = {}, {}, {}, {}, {}

        def part(table, name):
            def keep(f):
                table[name] = f
                return f
            return keep

        def mm3(pe, acc, lh, ll, rh, rl, first, last):
            pe.matmul(acc, lh, rh, start=first, stop=False)
            pe.matmul(acc, ll, rh, start=False, stop=False)
            return pe.matmul(acc, lh, rl, start=False, stop=last)

        const_dma = life.enter_context(nc.semaphore("const_loaded"))
        const_set = life.enter_context(nc.semaphore("const_set"))
        omm_set = life.enter_context(nc.semaphore("omm_set"))
        tg_set = life.enter_context(nc.semaphore("tg_set"))

        def col(ap):
            return ap.rearrange("(c p) -> p c", p=P)

        const_loads = [
            (gates[:, 0:LAYERS], A["g_xattn"].rearrange("(a n) -> a n", a=1).broadcast_to([P, LAYERS])),
            (gates[:, LAYERS:], A["g_ffn"].rearrange("(a n) -> a n", a=1).broadcast_to([P, LAYERS])),
            (gl[:, :, 0], col(A["L2_xattn_g_x"])), (gl[:, :, 1], col(A["L2_xattn_b_x"])),
            (gl[:, :, 2], col(A["L2_xattn_g_l"])), (gl[:, :, 3], col(A["L2_xattn_b_l"])),
            (mus[:, :, 0], col(A["L2_ffn_mu_r"])), (mus[:, :, 1], col(A["L2_ffn_mu_k"])),
            (cidx_i[:], A["L3_ffn_connected_idx"].rearrange("(a n) -> a n", a=1).broadcast_to([P, AE])),
        ] + [(benc[r * AH:(r + 1) * AH, :], A["L3_ffn_b_enc"].rearrange("(k r) h -> r h k", r=2)[r])
             for r in range(2)
        ] + [(bdec[:, :, c], A["L3_ffn_b_dec"].rearrange("n (c p) -> c p n", p=P)[c]) for c in range(DC)
        ] + [(bdown[r * AH:(r + 1) * AH, :], A["L3_ffn_b_down"].rearrange("n h -> h n")) for r in range(2)
        ] + [(rowb[:, k, :], A[name].rearrange("(a n) -> a n", a=1).broadcast_to([P, D]))
             for k, name in ((BO0, "L0_xattn_bo"), (BO1, "L1_xattn_bo"), (GO, "L2_xattn_g_o"),
                             (BO, "L2_xattn_b_o"), (BBASE, "L3_ffn_b_base"))]

        def sp_consts(sp):
            for dst, src in const_loads:
                sp.dma_start(dst, src, allow_slow_non_contiguous=True).then_inc(const_dma, 16)

        def pool_consts(pool):
            pool.memset(ident[:], 0.0).then_inc(const_set, 1)
            pool.memset(ones[:], 1.0).then_inc(const_set, 1)
            pool.memset(C[:], 0.0).then_inc(const_set, 1)
            pool.memset(CN[:], 0.0).then_inc(const_set, 1)
            pool.memset(CNT[:], 0.0).then_inc(const_set, 1)
            pool.wait_ge(const_set, 5)
            pool.affine_select(out=ident[:], in_=ident[:], compare_op=ALU.not_equal, fill=1.0, base=0,
                               pattern=[[-1, P]], channel_multiplier=1).then_inc(const_set, 1)
            pool.wait_ge(const_set, 6)
            pool.tensor_copy(identb[:], ident[:]).then_inc(const_set, 1)

        def act_consts(act):
            act.wait_ge(const_dma, 16 * len(const_loads))
            act.activation(tg[:], gates[:], ACT.Tanh).then_inc(tg_set, 1)

        def dve_consts(dve):
            dve.wait_ge(const_dma, 16 * len(const_loads))
            dve.tensor_scalar(omm[:], mus[:], -1.0, 1.0, ALU.mult, ALU.add).then_inc(omm_set, 1)
            dve.wait_ge(tg_set, 1)
            dve.tensor_scalar(htg2[:], tg[:, LAYERS + 2:LAYERS + 3], 0.5, None, ALU.mult).then_inc(omm_set, 1)
            dve.tensor_copy(cidx[:], cidx_i[:]).then_inc(omm_set, 1)
            for k, g in ((BO0, 0), (BO1, 1), (GO, 2), (BO, 2)):
                dve.tensor_scalar(rowb[:, k, :], rowb[:, k, :], tg[:, g:g + 1], None,
                                  ALU.mult).then_inc(omm_set, 1)

        load_x = signal("x_loaded")
        load_c = signal("ctx_loaded")
        CTX_STEPS = STAT_STEPS + 1
        ctx_chain = signal("ctx_norm_steps")
        ctx_ps = signal("ctx_transposed")
        ctx_hi = signal("ctx_hi")
        ctx_lo = signal("ctx_lo")

        def norm_stats(dve, chain, src, tiles, rows=P):
            for t in range(tiles):
                ins = dve.bn_stats(stats[0:rows, t, :], src(t))
            chain.step(ins)
            chain.settle()
            for t in range(tiles):
                ins = dve.bn_aggr(mv[0:rows, t, :], stats[0:rows, t, :])
            chain.step(ins)
            chain.settle()
            v, y, w = var[0:rows, 0:tiles], rstd[0:rows, 0:tiles], ntmp[0:rows, 0:tiles]
            chain.step(dve.tensor_scalar(v, mv[0:rows, 0:tiles, 1], EPS, None, ALU.add))
            chain.settle()
            chain.step(dve.tensor_scalar(y.bitcast(I32), v.bitcast(I32), -0.5, RSQRT_SEED, ALU.mult, ALU.add))
            chain.settle()
            for _ in range(NEWTON):
                chain.step(dve.tensor_tensor(w, y, y, ALU.mult))
                chain.settle()
                chain.step(dve.scalar_tensor_tensor(w, w, -0.5, v, ALU.mult, ALU.mult))
                chain.settle()
                chain.step(dve.scalar_tensor_tensor(y, w, 1.5, y, ALU.add, ALU.mult))
                chain.settle()
            chain.step(dve.scalar_tensor_tensor(nmr[0:rows, 0:tiles], mv[0:rows, 0:tiles, 0], -1.0, y,
                                                ALU.mult, ALU.mult))
            chain.settle()

        @part(sp_parts, "load")
        def _(sp, b):
            sp.dma_start(X[:], A["x"][bass.ds(b * N, N), :].rearrange("(t p) d -> p t d", p=P)
                         ).then_inc(load_x, 16)
            sp.dma_start(C[0:J, :], A["ctx_1024"][bass.ds(b * J, J), :]).then_inc(load_c, 16)
            sp.wait_ge(load_x, 16)

        @part(dve_parts, "load")
        def _(dve, b):
            dve.wait_ge(load_c, 16)
            chain = Chain(dve, ctx_chain)
            norm_stats(dve, chain, lambda t: C[0:J, :], 1, J)
            chain.step(dve.tensor_scalar(CN[0:J, :], C[0:J, :], rstd[0:J, 0:1], nmr[0:J, 0:1], ALU.mult, ALU.add))
            dve.wait_ge(ctx_hi, 1)
            dve.tensor_tensor(CTl[:, :, :], PA[:, 0:DC * JP].rearrange("p (c j) -> p c j", c=DC),
                              CTh[:, :, :].bitcast(F32), ALU.subtract).then_inc(ctx_lo, 1)
            dve.wait_ge(ctx_hi, 3)
            dve.tensor_tensor(CNTl[:, :, :], CNT[:, :, :], CNTh[:, :, :].bitcast(F32),
                              ALU.subtract).then_inc(ctx_lo, 1)

        @part(pe_parts, "load")
        def _(pe, b):
            pe.wait_ge(load_c, 16)
            for c in range(DC):
                ins = pe.transpose(PA[:, c * JP:(c + 1) * JP], C[0:JP, c * P:(c + 1) * P], ident[0:JP, 0:JP])
            ins.then_inc(ctx_ps, 1)
            pe.wait_ge(ctx_chain, CTX_STEPS)
            for c in range(DC):
                ins = pe.transpose(PB[:, c * JP:(c + 1) * JP], CN[0:JP, c * P:(c + 1) * P], ident[0:JP, 0:JP])
            ins.then_inc(ctx_ps, 1)

        @part(act_parts, "load")
        def _(act, b):
            act.wait_ge(ctx_ps, 1)
            act.activation(CTh[:, :, :], PA[:, 0:DC * JP].rearrange("p (c j) -> p c j", c=DC),
                           ACT.Copy).then_inc(ctx_hi, 1)
            act.wait_ge(ctx_ps, 2)
            for c in range(DC):
                ins = act.activation(CNT[:, c, 0:J], PB[:, c * JP:c * JP + J], ACT.Identity,
                                     scale=gl[:, c, 0:1], bias=gl[:, c, 1:2])
            ins.then_inc(ctx_hi, 1)
            act.wait_ge(ctx_hi, 2)
            act.activation(CNTh[:, :, :], CNT[:, :, :], ACT.Copy).then_inc(ctx_hi, 1)

        QUADS = [(c, h) for c in range(DC) for h in range(NHALF)]
        LN_STEPS = STAT_STEPS + 1

        def apply_norm(dve, chain, src):
            for t in range(TT // 2):
                ins = dve.tensor_scalar(XN[:, t, :], src[:, t, :], rstd[:, t:t + 1], nmr[:, t:t + 1],
                                        ALU.mult, ALU.add)
            chain.step(ins)

        def ln_stage(name, feature_major=True, XF=None, gamma=None):
            steps = LN_STEPS * (2 if gamma is not None else 1)
            chain_of = signal(name + "_steps")
            applied = signal(name + "_applied")
            rounds = 2 if gamma is not None else 1
            LQ = [(c, h) for h in range(NHALF) for c in range(DC)]
            ps = signal(name + "_transposed")
            full = signal(name + "_full") if XF is not None else None
            hi = signal(name + "_hi")
            lo = signal(name + "_lo")

            @part(dve_parts, name)
            def _(dve, b):
                chain = Chain(dve, chain_of)
                norm_stats(dve, chain, lambda t: X[:, t, :], TT)
                apply_norm(dve, chain, X)
                if gamma is not None:
                    chain.settle()
                    dve.wait_ge(applied, 1)
                    norm_stats(dve, chain, lambda t: XN[:, t, :], TT)
                    apply_norm(dve, chain, XN)
                if feature_major:
                    for q, (c, h) in enumerate(LQ):
                        cols = slice(h * HALF, (h + 1) * HALF)
                        dve.wait_ge(hi, q + 1)
                        dve.tensor_tensor(XTl[:, c, cols], BANKS[q] if XF is None else XF[:, c, cols],
                                          XTh[:, c, cols].bitcast(F32), ALU.subtract).then_inc(lo, 1)

            def apply_other_half(act):
                for r in range(rounds):
                    act.wait_ge(chain_of, LN_STEPS * r + STAT_STEPS)
                    src = XN if r else X
                    for t in range(TT // 2, TT):
                        ins = act.activation(XN[:, t, :], src[:, t, :], ACT.Identity, scale=rstd[:, t:t + 1],
                                             bias=nmr[:, t:t + 1])
                    ins.then_inc(applied, 1)

            if not feature_major:
                part(act_parts, name)(lambda act, b: apply_other_half(act))
                return

            @part(pe_parts, name)
            def _(pe, b):
                pe.wait_ge(chain_of, steps)
                for q, (c, h) in enumerate(LQ):
                    if q == DC:
                        pe.wait_ge(applied, rounds)
                    for i in range(4):
                        ins = pe.transpose(BANKS[q][:, i * P:(i + 1) * P],
                                           XN[:, 4 * h + i, c * P:(c + 1) * P], ident[:])
                    ins.then_inc(ps, 1)

            @part(act_parts, name)
            def _(act, b):
                apply_other_half(act)
                for q, (c, h) in enumerate(LQ):
                    cols = slice(h * HALF, (h + 1) * HALF)
                    act.wait_ge(ps, q + 1)
                    src = BANKS[q]
                    if XF is not None:
                        if gamma is not None:
                            ins = act.activation(XF[:, c, cols], src, ACT.Identity,
                                                 scale=gl[:, c, gamma:gamma + 1],
                                                 bias=gl[:, c, gamma + 1:gamma + 2])
                        else:
                            ins = act.activation(XF[:, c, cols], src, ACT.Copy)
                        ins.then_inc(full, 1)
                        act.wait_ge(full, q + 1)
                        src = XF[:, c, cols]
                    act.activation(XTh[:, c, cols], src, ACT.Copy).then_inc(hi, 1)

        def context_attention(k, group_heads, weights, scale, gate, masked, bias_row):
            prep, main = f"prep{k}", f"attn{k}"
            groups = HEADS // group_heads
            w = group_heads * JP
            segs = [(0, w)] if w <= HALF else [(0, w // 2), (w // 2, w)]
            n_parts = len(weights)
            AHi = sb(f"scores_w_hi{k}", [P, DC, HJ], F32R)
            ALo = sb(f"scores_w_lo{k}", [P, DC, HJ], F32R)
            VWh = sb(f"out_w_hi{k}", [P, HJC, D], F32R)
            VWl = sb(f"out_w_lo{k}", [P, HJC, D], F32R)
            with buffers():
                heads_of_rows = sb(f"head_mask{k}", [P, group_heads])
                raw = [sb(f"prep_raw{k}_{i}", [P, n_parts, D]) for i in range(2)]
                wh = [sb(f"prep_wh{k}_{i}", [P, n_parts, D], F32R) for i in range(3)]
                wl = [sb(f"prep_wl{k}_{i}", [P, n_parts, D], F32R) for i in range(3)]
                KB = sb(f"k_blocks{k}", [P, group_heads, JP])
                VB = sb(f"v_blocks{k}", [P, group_heads, JP])
                KBh = sb(f"k_blocks_hi{k}", [P, w], F32R)
                KBl = sb(f"k_blocks_lo{k}", [P, w], F32R)
                VBh = sb(f"v_blocks_hi{k}", [P, w], F32R)
                VBl = sb(f"v_blocks_lo{k}", [P, w], F32R)
                VWT = sb(f"out_w_t{k}", [P, DC, HJC * P])
            KBv, VBv = KB[:, :, :].rearrange("p h j -> p (h j)"), VB[:, :, :].rearrange("p h j -> p (h j)")
            has_wo = n_parts == 4
            raw_in = [signal(prep + f"_weights_in{i}") for i in range(2)]
            mask_steps = signal(prep + "_mask_steps")
            split = signal(prep + "_weights_split")
            kv_ps = signal(prep + "_kv_ready")
            blocks = signal(prep + "_blocks")
            blocks_hi = signal(prep + "_blocks_hi")
            blocks_lo = signal(prep + "_blocks_lo")
            a_ps = signal(prep + "_products")
            a_hi = signal(prep + "_products_hi")
            a_lo = signal(prep + "_products_lo")
            vw_ps = signal(prep + "_vw_transposed")
            vw_hi = signal(prep + "_vw_hi")
            vw_lo = signal(prep + "_vw_lo")

            a_bank = {(c, s): [BANKS[0], BANKS[1], BANKS[3], BANKS[4]][c * len(segs) + s]
                      for c in range(DC) for s in range(len(segs))}
            KVBANK = [PT, PV]

            before = f"ln{k}x"
            EARLY = min(2, groups)

            def group_loop(eng, body):
                for g in range(groups):
                    body(g)

            def cols(tensor, c, g, s0, s1):
                return tensor[:, c, g * w + s0:g * w + s1]

            def load_group(sp, g):
                if g >= 2:
                    sp.wait_ge(split, (g - 1) * 2)
                for i, source in enumerate(weights):
                    dst, src = source(raw[g % 2], i, g)
                    sp.dma_start(dst, src).then_inc(raw_in[g % 2], 16)

            def split_group(pool, g):
                pool.wait_ge(raw_in[g % 2], (g // 2 + 1) * (16 * n_parts))
                if g >= 3:
                    pool.wait_ge(a_ps, g - 2)
                h_, l_, r_ = wh[g % 3][:], wl[g % 3][:], raw[g % 2][:]
                pool.tensor_scalar(h_, r_, 1.0, 0.0, ALU.mult, ALU.add).then_inc(split, 1)
                pool.wait_ge(split, g * 2 + 1)
                pool.tensor_tensor(l_, r_, h_.bitcast(F32), ALU.subtract).then_inc(split, 1)

            @part(sp_parts, before)
            def _(sp, b):
                for g in range(EARLY):
                    load_group(sp, g)

            @part(sp_parts, prep)
            def _(sp, b):
                for g in range(EARLY, groups):
                    load_group(sp, g)

            @part(pool_parts, before)
            def _(pool, b):
                m = heads_of_rows[:]
                rows = P // group_heads
                pool.memset(m, 1.0).then_inc(mask_steps, 1)
                pool.memset(VWT[:], 0.0).then_inc(mask_steps, 1)
                pool.wait_ge(mask_steps, 2)
                pool.affine_select(out=m, in_=m, compare_op=ALU.is_ge, fill=0.0, base=0,
                                   pattern=[[-rows, group_heads]], channel_multiplier=1
                                   ).then_inc(mask_steps, 1)
                pool.wait_ge(mask_steps, 3)
                pool.affine_select(out=m, in_=m, compare_op=ALU.is_ge, fill=0.0, base=rows - 1,
                                   pattern=[[rows, group_heads]], channel_multiplier=-1
                                   ).then_inc(mask_steps, 1)
                for g in range(EARLY):
                    split_group(pool, g)

            @part(pool_parts, prep)
            def _(pool, b):
                for g in range(EARLY, groups):
                    split_group(pool, g)

            @part(pe_parts, prep)
            def _(pe, b):
                def keys_values(g):
                    pe.wait_ge(split, g * 2 + 2)
                    if g >= 2:
                        pe.wait_ge(blocks, (g - 1) * 2)
                    for i, col0 in ((0, 0), (1, P)):
                        for c in range(DC):
                            e = slice(c * P, (c + 1) * P)
                            ins = mm3(pe, KVBANK[g % 2][:, col0:col0 + JP], wh[g % 3][:, i, e], wl[g % 3][:, i, e],
                                      CTh[:, c, :], CTl[:, c, :], c == 0, c == DC - 1)
                    ins.then_inc(kv_ps, 1)

                def body(g):
                    if g == 0:
                        keys_values(0)
                    if g + 1 < groups:
                        keys_values(g + 1)
                    pe.wait_ge(blocks_lo, g * 2 + 2)
                    if g:
                        pe.wait_ge(a_lo, g)
                    h_, l_ = wh[g % 3], wl[g % 3]
                    for c in range(DC):
                        e = slice(c * P, (c + 1) * P)
                        for s, (s0, s1) in enumerate(segs):
                            ins = mm3(pe, a_bank[c, s][:, 0:s1 - s0], h_[:, 2, e], l_[:, 2, e],
                                      KBh[:, s0:s1], KBl[:, s0:s1], True, True)
                        if has_wo:
                            ins = mm3(pe, [BANKS[2], BANKS[5]][c][:, 0:w], h_[:, 3, e], l_[:, 3, e],
                                      VBh[:], VBl[:], True, True)
                    ins.then_inc(a_ps, 1)
                group_loop(pe, body)
                if has_wo:
                    pe.wait_ge(a_lo, groups)
                pe.wait_ge(a_hi, groups)
                pe.wait_ge(a_lo, groups)
                for n in range(HJC // 2):
                    for i in range(2):
                        for c in range(DC):
                            col0 = i * D + c * P
                            ins = pe.transpose(BANKS[n][:, col0:col0 + P],
                                               VWT[:, c, (2 * n + i) * P:(2 * n + i + 1) * P], ident[:])
                    ins.then_inc(vw_ps, 1)

            @part(dve_parts, prep)
            def _(dve, b):
                dve.wait_ge(mask_steps, 4)
                own = heads_of_rows[:, :].unsqueeze(2).broadcast_to([P, group_heads, JP])

                def body(g):
                    dve.wait_ge(kv_ps, g + 1)
                    if g:
                        dve.wait_ge(blocks_hi, g * 2)
                    if g:
                        dve.wait_ge(blocks_lo, g * 2)
                    for blk, col0 in ((KB, 0), (VB, P)):
                        dve.tensor_tensor(blk[:], KVBANK[g % 2][:, col0:col0 + JP].unsqueeze(1).broadcast_to(
                            [P, group_heads, JP]), own, ALU.mult).then_inc(blocks, 1)
                    for n, (lo, full, hi_) in enumerate(((KBl, KBv, KBh), (VBl, VBv, VBh))):
                        dve.wait_ge(blocks_hi, g * 2 + n + 1)
                        dve.tensor_tensor(lo[:], full, hi_[:].bitcast(F32), ALU.subtract
                                          ).then_inc(blocks_lo, 1)
                    dve.wait_ge(a_hi, g + 1)
                    for c in range(DC):
                        for s, (s0, s1) in enumerate(segs):
                            ins = dve.tensor_tensor(cols(ALo, c, g, s0, s1), a_bank[c, s][:, 0:s1 - s0],
                                                    cols(AHi, c, g, s0, s1).bitcast(F32), ALU.subtract)
                    ins.then_inc(a_lo, 1)
                group_loop(dve, body)
                for n in range(HJC // 2):
                    dve.wait_ge(vw_hi, n + 1)
                    dve.tensor_tensor(VWl[:, 2 * n:2 * n + 2, :], BANKS[n].rearrange("p (i d) -> p i d", i=2),
                                      VWh[:, 2 * n:2 * n + 2, :].bitcast(F32), ALU.subtract
                                      ).then_inc(vw_lo, 1)

            @part(act_parts, prep)
            def _(act, b):
                act.wait_ge(mask_steps, 2)

                def body(g):
                    if g:
                        act.wait_ge(a_ps, g)
                    for n, (hi_, full) in enumerate(((KBh, KBv), (VBh, VBv))):
                        act.wait_ge(blocks, g * 2 + n + 1)
                        act.activation(hi_[:], full, ACT.Copy).then_inc(blocks_hi, 1)
                    if not has_wo:
                        act.activation(cols(VWT, g, g, 0, w), VBv, ACT.Copy)
                    act.wait_ge(a_ps, g + 1)
                    for c in range(DC):
                        for s, (s0, s1) in enumerate(segs):
                            ins = act.activation(cols(AHi, c, g, s0, s1), a_bank[c, s][:, 0:s1 - s0], ACT.Copy)
                        if has_wo:
                            ins = act.activation(cols(VWT, c, g, 0, w), [BANKS[2], BANKS[5]][c][:, 0:w], ACT.Copy)
                    ins.then_inc(a_hi, 1)
                group_loop(act, body)
                for n in range(HJC // 2):
                    act.wait_ge(vw_ps, n + 1)
                    act.activation(VWh[:, 2 * n:2 * n + 2, :], BANKS[n].rearrange("p (i d) -> p i d", i=2),
                                   ACT.Copy).then_inc(vw_hi, 1)

            NP = 4
            with buffers():
                SB = [sb(f"scores{k}_{i}", [P, HEADS, JP]) for i in range(2)]
                PR = [sb(f"probs{k}_{i}", [P, HJC * P]) for i in range(NP)]
                PTh = [sb(f"probs_t_hi{k}_{i}", [P, HJC, P], F32R) for i in range(2)]
                PTl = [sb(f"probs_t_lo{k}_{i}", [P, HJC, P], F32R) for i in range(2)]
                mx = sb(f"row_max{k}", [P, 2, HEADS])
                sm = sb(f"row_sum{k}", [P, NP, HEADS])
                rs = sb(f"row_inv{k}", [P, NP, HEADS])
                mask8 = sb(f"mask_bytes{k}", [P, TT, J], U8) if masked else None
                mneg = sb(f"mask_add{k}", [P, TT, J]) if masked else None
            PRv = [p_[:, 0:HJ].rearrange("p (h j) -> p h j", h=HEADS) for p_ in PR]
            SPS = PA
            TBANK = [BANKS[3], BANKS[4], BANKS[5]]
            OBANK = [PT[:, 0:D], PV[:, 0:D]]
            ROUNDS = [(0, 4), (4, 8), (8, HJC)]
            mask_in = signal(main + "_mask_in")
            mask_done = signal(main + "_mask_ready")
            cleared = signal(main + "_probs_cleared")
            biased = signal(main + "_bias_added")
            s_ps = signal(main + "_scores_ready")
            s_out = signal(main + "_scores_copied")
            mx_done = signal(main + "_max")
            sub_done = signal(main + "_shifted")
            ex_done = signal(main + "_exp")
            sum_done = signal(main + "_sum")
            inv_done = signal(main + "_inv")
            p_done = signal(main + "_probs_ready")
            t_ps = signal(main + "_probs_transposed")
            t_hi = signal(main + "_probs_t_hi")
            t_lo = signal(main + "_probs_t_lo")
            o_ps = signal(main + "_out_ready")
            x_done = signal(main + "_residual")
            LAG = 3
            NR = len(ROUNDS)

            def bank_view(buf, n):
                h0, h1 = BANK_HEADS[n]
                return buf[:, n * HALF:n * HALF + (h1 - h0) * JP].rearrange("p (h j) -> p h j", j=JP)[:, :, 0:J]

            if masked:
                @part(sp_parts, main)
                def _(sp, b):
                    sp.dma_start(mask8[:], A["mask_BxSxS2_bk1"][bass.ds(b * N, N), :].rearrange(
                        "(t p) j -> p t j", p=P)).then_inc(mask_in, 16)

            @part(pe_parts, main)
            def _(pe, b):
                for i in range(TT + LAG + 1):
                    j, o = i - LAG, i - LAG - 1
                    if i < TT:
                        if i:
                            pe.wait_ge(s_out, i)
                        for r, (h0, h1) in enumerate(BANK_HEADS):
                            for c in range(DC):
                                tok = slice(i * P, (i + 1) * P)
                                ins = mm3(pe, SPS[:, r * HALF:r * HALF + (h1 - h0) * JP],
                                          XTh[:, c, tok], XTl[:, c, tok],
                                          AHi[:, c, h0 * JP:h1 * JP], ALo[:, c, h0 * JP:h1 * JP],
                                          c == 0, c == DC - 1)
                        ins.then_inc(s_ps, 1)
                    if 0 <= j < TT:
                        pe.wait_ge(p_done, j + 1)
                        for r, (c0, c1) in enumerate(ROUNDS):
                            if j:
                                pe.wait_ge(t_lo, NR * (j - 1) + r + 1)
                            for c in range(c0, c1):
                                ins = pe.transpose(TBANK[r][:, (c - c0) * P:(c - c0 + 1) * P],
                                                   PR[j % NP][:, c * P:(c + 1) * P], ident[:])
                            ins.then_inc(t_ps, 1)
                    if 0 <= o < TT:
                        pe.wait_ge(t_lo, NR * (o + 1))
                        if o >= 2:
                            pe.wait_ge(x_done, o - 1)
                        for c in range(HJC):
                            ins = mm3(pe, OBANK[o % 2], PTh[o % 2][:, c, :], PTl[o % 2][:, c, :],
                                      VWh[:, c, :], VWl[:, c, :], c == 0, c == HJC - 1)
                        ins.then_inc(o_ps, 1)

            @part(act_parts, main)
            def _(act, b):
                act.wait_ge(cleared, 1)
                for i in range(TT + LAG):
                    j = i - LAG
                    if i < TT and not masked:
                        act.wait_ge(s_ps, i + 1)
                        if i >= 2:
                            act.wait_ge(ex_done, i - 1)
                        for n, (h0, h1) in enumerate(BANK_HEADS):
                            ins = act.activation(SB[i % 2][:, h0:h1, 0:J], bank_view(SPS, n), ACT.Copy)
                        ins.then_inc(s_out, 1)
                    if 0 <= j < TT:
                        for r, (c0, c1) in enumerate(ROUNDS):
                            act.wait_ge(t_ps, NR * j + r + 1)
                            if r == 0 and j >= 2:
                                act.wait_ge(o_ps, j - 1)
                            act.activation(PTh[j % 2][:, c0:c1, :].rearrange("p c q -> p (c q)"),
                                           TBANK[r][:, 0:(c1 - c0) * P], ACT.Copy).then_inc(t_hi, 1)
                    if i < TT:
                        act.wait_ge(sub_done, i + 1)
                        if i >= NP:
                            act.wait_ge(t_ps, NR * (i - NP + 1))
                        act.activation(PRv[i % NP][:, :, 0:J], SB[i % 2][:, :, 0:J], ACT.Exp,
                                       scale=scale).then_inc(ex_done, 1)

            @part(dve_parts, main)
            def _(dve, b):
                if masked:
                    dve.wait_ge(mask_in, 16)
                    dve.tensor_scalar(mneg[:], mask8[:], NEG_MAX, None, ALU.mult).then_inc(mask_done, 1)
                    dve.wait_ge(mask_done, 1)
                if bias_row is not None:
                    dve.wait_ge(biased, 1)
                for i in range(TT + LAG + 1):
                    j = i - LAG
                    if i < TT:
                        if masked:
                            dve.wait_ge(s_ps, i + 1)
                            if i >= 2:
                                dve.wait_ge(ex_done, i - 1)
                            for n, (h0, h1) in enumerate(BANK_HEADS):
                                ins = dve.tensor_tensor(
                                    SB[i % 2][:, h0:h1, 0:J], bank_view(SPS, n),
                                    mneg[:, i, :].unsqueeze(1).broadcast_to([P, h1 - h0, J]), ALU.add)
                            ins.then_inc(s_out, 1)
                        dve.wait_ge(s_out, i + 1)
                        if i >= 2:
                            dve.wait_ge(sub_done, i - 1)
                        dve.tensor_reduce(mx[:, i % 2, :], SB[i % 2][:, :, 0:J], AX.X, ALU.max
                                          ).then_inc(mx_done, 1)
                    if 1 <= i <= TT:
                        q = i - 1
                        dve.wait_ge(ex_done, q + 1)
                        if q >= NP:
                            dve.wait_ge(inv_done, q - NP + 1)
                        dve.tensor_reduce(sm[:, q % NP, :], PRv[q % NP][:, :, 0:J], AX.X, ALU.add
                                          ).then_inc(sum_done, 1)
                        dve.wait_ge(sum_done, q + 1)
                        if q >= NP:
                            dve.wait_ge(p_done, q - NP + 1)
                        dve.reciprocal(rs[:, q % NP, :], sm[:, q % NP, :]).then_inc(inv_done, 1)
                    if 0 <= j < TT:
                        for r, (c0, c1) in enumerate(ROUNDS):
                            dve.wait_ge(t_hi, NR * j + r + 1)
                            dve.tensor_tensor(PTl[j % 2][:, c0:c1, :].rearrange("p c q -> p (c q)"),
                                              TBANK[r][:, 0:(c1 - c0) * P],
                                              PTh[j % 2][:, c0:c1, :].rearrange("p c q -> p (c q)").bitcast(F32),
                                              ALU.subtract).then_inc(t_lo, 1)
                    o = i - LAG - 1
                    if 0 <= o < TT:
                        dve.wait_ge(o_ps, o + 1)
                        dve.scalar_tensor_tensor(X[:, o, :], OBANK[o % 2], tg[:, gate:gate + 1], X[:, o, :],
                                                 ALU.mult, ALU.add).then_inc(x_done, 1)

            @part(pool_parts, main)
            def _(pool, b):
                for p_ in PR:
                    ins = pool.memset(p_[:], 0.0)
                ins.then_inc(cleared, 1)
                if bias_row is not None:
                    pool.tensor_tensor(X[:], X[:], rowb[:, bias_row, :].unsqueeze(1).broadcast_to([P, TT, D]),
                                       ALU.add).then_inc(biased, 1)
                for i in range(TT + 1):
                    if i < TT:
                        pool.wait_ge(mx_done, i + 1)
                        s_ = SB[i % 2][:, :, 0:J]
                        pool.tensor_tensor(s_, s_, mx[:, i % 2, :].unsqueeze(2).broadcast_to([P, HEADS, J]),
                                           ALU.subtract).then_inc(sub_done, 1)
                    if i >= 1:
                        q = i - 1
                        pool.wait_ge(inv_done, q + 1)
                        p_ = PRv[q % NP][:, :, 0:J]
                        pool.tensor_tensor(p_, p_, rs[:, q % NP, :].unsqueeze(2).broadcast_to([P, HEADS, J]),
                                           ALU.mult).then_inc(p_done, 1)

        def by_rows(name):
            return lambda raw, i, g: (raw[:, i, :], A[name][g * P:(g + 1) * P, :])

        def by_cols(name):
            return lambda raw, i, g: (raw[:, i, :].rearrange("p (c e) -> p c e", c=DC),
                                      A[name].rearrange("(c p) e -> p c e", p=P)[:, :, g * P:(g + 1) * P])

        ln_stage("ln0x")
        with buffers():
            context_attention(0, 2, [by_cols("L0_xattn_Wk"), by_cols("L0_xattn_Wv"),
                                     by_rows("L0_xattn_WqT"), by_rows("L0_xattn_Wo")],
                              DH ** -0.5, 0, True, BO0)

        QW = [("L0_ffn_gT", DC, INNER), ("L0_ffn_uT", DC, INNER), ("L0_ffn_dT", INNER // P, D)]
        WCOLS = DC * INNER
        IC = INNER // P
        ln_stage("ln0f", feature_major=False)
        with buffers():
            wraw = [sb(f"ternary_raw{n}", [P, WCOLS]) for n in range(3)]
        bit_scope = ExitStack()
        scope = bit_scope
        XQ = sb("x_ints_f", [P, TT, D])
        XQb = sb("x_ints", [P, TT, D], BF16)
        XQT = sb("x_ints_t", [P, DC, N], BF16)
        amax = sb("x_abs_max", [P, TT])
        ainv = sb("x_inv_max", [P, TT])
        TH = [sb(f"bit_tanh{i}", [P, INNER]) for i in range(2)]
        GA = [sb(f"bit_gate{i}", [P, INNER]) for i in range(2)]
        HH = [sb(f"bit_hidden{i}", [P, INNER]) for i in range(2)]
        HQ = [sb(f"bit_hidden_ints{i}", [P, INNER], BF16) for i in range(2)]
        HT = [sb(f"bit_hidden_t{i}", [P, IC, P], BF16) for i in range(2)]
        cg = sb("bit_gate_scale", [P, TT])
        hcg = sb("bit_half_gate_scale", [P, TT])
        cgu = sb("bit_product_scale", [P, TT])
        hmax = sb("hidden_abs_max", [P, TT])
        hclip = sb("hidden_clipped_max", [P, TT])
        hinv = sb("hidden_inv_max", [P, TT])
        hout = sb("hidden_out_scale", [P, TT])
        bit_scope.close()
        scope = life

        bw_in = [life.enter_context(nc.semaphore(f"bit_weight{n}_in")) for n in range(3)]
        bw_sum = life.enter_context(nc.semaphore("bit_weight_sum"))
        bw_steps = life.enter_context(nc.semaphore("bit_weight_steps"))
        bq_steps = signal("bitq_dve_steps")
        bx_ints = signal("bit_x_ints")
        bx_ps = signal("bit_x_transposed")
        bx_t = signal("bit_x_t_copied")

        def sp_ternary(sp):
            for n, (name, c, w) in enumerate(QW):
                sp.dma_start(wraw[n][:].rearrange("p (c w) -> p c w", c=c),
                             A[name].rearrange("(c p) w -> p c w", p=P)).then_inc(bw_in[n], 16)

        def dve_ternary(dve):
            chain = Chain(dve, bw_steps)
            for n in range(3):
                dve.wait_ge(bw_in[n], 16)
                chain.step(dve.tensor_reduce(wabs[:, n:n + 1], wraw[n][:], AX.X, ALU.add,
                                             apply_absolute_value=True))
            dve.wait_ge(bw_sum, 1)
            chain.step(dve.tensor_scalar(wmean[:], PV[:, 0:3], 1.0 / (INNER * D), EPS, ALU.mult, ALU.max))
            chain.settle()
            chain.step(dve.reciprocal(winv[:], wmean[:]))
            chain.settle()
            for n in range(3):
                chain.step(dve.tensor_scalar(wraw[n][:], wraw[n][:], winv[:, n:n + 1], 1.0, ALU.mult, ALU.min))
            chain.settle()
            for n in range(3):
                chain.step(dve.tensor_scalar(wraw[n][:], wraw[n][:], -1.0, MAGIC, ALU.max, ALU.add))
            chain.settle()
            for n in range(3):
                chain.step(dve.tensor_scalar(wq[n][:], wraw[n][:], -MAGIC, None, ALU.add))
            chain.settle()

        def pe_ternary(pe):
            pe.wait_ge(bw_steps, 3)
            pe.matmul(PV[:, 0:3], ones[:], wabs[:], start=True, stop=True).then_inc(bw_sum, 1)

        @part(dve_parts, "bitq")
        def _(dve, b):
            chain = Chain(dve, bq_steps)
            chain.step(dve.tensor_reduce(amax[:], XN[:], AX.X, ALU.max, apply_absolute_value=True))
            chain.settle()
            chain.step(dve.tensor_scalar(amax[:], amax[:], EPS, None, ALU.max))
            chain.settle()
            chain.step(dve.reciprocal(ainv[:], amax[:]))
            chain.settle()
            chain.step(dve.tensor_scalar(ainv[:], ainv[:], 127.0, None, ALU.mult))
            chain.settle()
            for t in range(TT):
                ins = dve.tensor_scalar(XQ[:, t, :], XN[:, t, :], ainv[:, t:t + 1], MAGIC, ALU.mult, ALU.add)
            chain.step(ins)
            chain.settle()
            dve.tensor_scalar(XQb[:], XQ[:], -MAGIC, 127.0, ALU.add, ALU.min).then_inc(bx_ints, 1)
            chain.step(dve.tensor_scalar(cg[:], amax[:], wmean[:, 0:1], 1.0 / 127.0, ALU.mult, ALU.mult))
            chain.settle()
            chain.step(dve.tensor_scalar(hcg[:], cg[:], 0.5, None, ALU.mult))
            chain.settle()
            chain.step(dve.tensor_scalar(cgu[:], amax[:], wmean[:, 1:2], 1.0 / 127.0, ALU.mult, ALU.mult))
            chain.settle()
            chain.step(dve.tensor_tensor(cgu[:], cgu[:], hcg[:], ALU.mult))

        @part(pe_parts, "bitq")
        def _(pe, b):
            pe.wait_ge(bx_ints, 1)
            for q, (c, h) in enumerate(QUADS):
                for i in range(4):
                    ins = pe.transpose(BANKS[q + 1].bitcast(BF16)[:, i * P:(i + 1) * P],
                                       XQb[:, 4 * h + i, c * P:(c + 1) * P], identb[:])
                ins.then_inc(bx_ps, 1)

        @part(act_parts, "bitq")
        def _(act, b):
            for q, (c, h) in enumerate(QUADS):
                act.wait_ge(bx_ps, q + 1)
                act.activation(XQT[:, c, h * HALF:(h + 1) * HALF], BANKS[q + 1].bitcast(BF16)[:, 0:HALF],
                               ACT.Copy).then_inc(bx_t, 1)

        bg_ps = signal("bit_gate_up")
        b_tanh = signal("bit_tanh")
        b_gate = signal("bit_gate")
        b_hid = signal("bit_hidden")
        b_small = signal("bit_small_steps")
        b_hscale = signal("bit_hidden_scale")
        b_round = signal("bit_rounded")
        b_hq = signal("bit_hidden_ints")
        b_htp = signal("bit_hidden_transposed")
        b_ht = signal("bit_hidden_t")
        b_out = signal("bit_out")
        b_x = signal("bit_residual")

        @part(pe_parts, "bit")
        def _(pe, b):
            wv = [wq[n][:].rearrange("p (c w) -> p c w", c=c) for n, (_, c, _) in enumerate(QW)]
            for i in range(TT + 3):
                if i < TT:
                    if i:
                        pe.wait_ge(b_hid, i)
                    for n, buf in ((0, PA), (1, PB)):
                        for s in range(INNER // HALF):
                            for c in range(DC):
                                ins = pe.matmul(buf[:, s * HALF:(s + 1) * HALF], XQT[:, c, i * P:(i + 1) * P],
                                                wv[n][:, c, s * HALF:(s + 1) * HALF], start=c == 0, stop=c == DC - 1)
                    ins.then_inc(bg_ps, 1)
                j = i - 2
                if 0 <= j < TT:
                    pe.wait_ge(b_hq, j + 1)
                    if j:
                        pe.wait_ge(b_ht, j)
                    for c in range(IC):
                        ins = pe.transpose(PT[:].bitcast(BF16)[:, c * P:(c + 1) * P],
                                           HQ[j % 2][:, c * P:(c + 1) * P], identb[:])
                    ins.then_inc(b_htp, 1)
                o = i - 3
                if 0 <= o < TT:
                    pe.wait_ge(b_ht, o + 1)
                    if o:
                        pe.wait_ge(b_x, o)
                    for c in range(IC):
                        ins = pe.matmul(PV[:, 0:D], HT[o % 2][:, c, :], wv[2][:, c, :], start=c == 0, stop=c == IC - 1)
                    ins.then_inc(b_out, 1)

        @part(act_parts, "bit")
        def _(act, b):
            for i in range(TT + 2):
                if i < TT:
                    act.wait_ge(bg_ps, i + 1)
                    if i >= 2:
                        act.wait_ge(b_gate, i - 1)
                    act.activation(TH[i % 2][:], PA[:, 0:INNER], ACT.Tanh, scale=hcg[:, i:i + 1]).then_inc(b_tanh, 1)
                j = i - 2
                if 0 <= j < TT:
                    act.wait_ge(b_htp, j + 1)
                    if j >= 2:
                        act.wait_ge(b_out, j - 1)
                    act.activation(HT[j % 2][:].rearrange("p c q -> p (c q)"), PT[:].bitcast(BF16), ACT.Copy
                                   ).then_inc(b_ht, 1)

        @part(dve_parts, "bit")
        def _(dve, b):
            small = Chain(dve, b_small)
            for i in range(TT + 3):
                if i < TT:
                    t1 = slice(i, i + 1)
                    dve.wait_ge(b_tanh, i + 1)
                    if i >= 2:
                        dve.wait_ge(b_hid, i - 1)
                    dve.scalar_tensor_tensor(GA[i % 2][:], TH[i % 2][:], 1.0, PA[:, 0:INNER], ALU.add, ALU.mult
                                             ).then_inc(b_gate, 1)
                    dve.wait_ge(b_gate, i + 1)
                    if i >= 2:
                        dve.wait_ge(b_round, i - 1)
                    dve.scalar_tensor_tensor(HH[i % 2][:], GA[i % 2][:], cgu[:, t1], PB[:, 0:INNER],
                                             ALU.mult, ALU.mult).then_inc(b_hid, 1)
                    dve.wait_ge(b_hid, i + 1)
                    small.step(dve.tensor_reduce(hmax[:, t1], HH[i % 2][:], AX.X, ALU.max, apply_absolute_value=True))
                    small.settle()
                    small.step(dve.tensor_scalar(hclip[:, t1], hmax[:, t1], EPS, None, ALU.max))
                    small.settle()
                    small.step(dve.reciprocal(hinv[:, t1], hclip[:, t1]))
                    small.settle()
                    dve.tensor_scalar(hinv[:, t1], hinv[:, t1], 127.0, None, ALU.mult).then_inc(b_hscale, 1)
                    small.step(dve.tensor_scalar(hout[:, t1], hclip[:, t1], wmean[:, 2:3], 1.0 / 127.0,
                                                 ALU.mult, ALU.mult))
                    small.settle()
                    small.step(dve.tensor_scalar(hout[:, t1], hout[:, t1], tg[:, LAYERS:LAYERS + 1], None, ALU.mult))
                q = i - 1
                if 0 <= q < TT:
                    dve.wait_ge(b_round, q + 1)
                    if q >= 2:
                        dve.wait_ge(b_htp, q - 1)
                    dve.tensor_scalar(HQ[q % 2][:], HH[q % 2][:], -MAGIC, 127.0, ALU.add, ALU.min).then_inc(b_hq, 1)
                o = i - 3
                if 0 <= o < TT:
                    dve.wait_ge(b_out, o + 1)
                    dve.scalar_tensor_tensor(X[:, o, :], PV[:, 0:D], hout[:, o:o + 1], X[:, o, :],
                                             ALU.mult, ALU.add).then_inc(b_x, 1)

        @part(pool_parts, "bit")
        def _(pool, b):
            for i in range(TT):
                pool.wait_ge(b_hscale, i + 1)
                pool.tensor_scalar(HH[i % 2][:], HH[i % 2][:], hinv[:, i:i + 1], MAGIC, ALU.mult, ALU.add
                                   ).then_inc(b_round, 1)

        def hi_of(eng, hi, src):
            return eng.tensor_scalar(hi, src, 1.0, 0.0, ALU.mult, ALU.add)

        next_layer()
        def latent_attention(k, heads, weights, ctx, out_to, gate, bias_row, mask=None):
            ln, st = f"ln{k}x", f"attn{k}"
            pairs = heads // 2
            PT_ = 4
            turns = pairs // PT_
            SPLITS = PT_ if turns > 1 else PT_ - 2
            BUILDS = PT_ if turns > 1 else PT_ - 1
            n_q = len(weights) - 1
            IQ, IK, IV = 0, 1, 2
            IKC, IVC = (3, 4) if n_q == 5 else (1, 2)
            Ch, Cl = ctx
            SEG = [(0, HALF), (HALF, N), (N, KEYSP)]
            ROUNDS = [(0, 4), (4, 8), (8, KC)]
            LAG, NPB = 3, 4
            PU = 2 * TT
            UNITS = PT_ * PU
            ROWS = [slice(0, DH), slice(DH, P)]
            CTX_UNITS = [(0, 6), (6, 11), (11, PU)]
            PIECES = {0: ("k", 0), 1: ("k", 1), 2: ("k", 2), 3: ("q", 0), 4: ("q", 1), 5: ("v", 0),
                      6: ("v", 1), 7: ("v", 2), 10: ("x", 0), 11: ("x", 1), 12: ("x", 2)}
            OUT_OWN = {15: 0}
            OUT_BEFORE = {8: 1, 9: 2, 13: 3}
            KQ = 10
            with buffers():
                raw = sb(f"qkv_raw{k}", [P, n_q, D])
                wh = sb(f"qkv_hi{k}", [P, n_q, D], F32R)
                wl = sb(f"qkv_lo{k}", [P, n_q, D], F32R)
                oraw = sb(f"wo_raw{k}", [P, D])
                oh = [sb(f"wo_hi{k}_{n}", [P, D], F32R) for n in range(2)]
                ol = [sb(f"wo_lo{k}_{n}", [P, D], F32R) for n in range(2)]
                OR = sb(f"o_t_piece{k}", [P, HALF])
                RB = [sb(f"kq_piece{k}_{i}", [P, HALF]) for i in range(2)]
                QS = [[sb(f"q_stack{k}_{n}_{i}", [P, N], F32R) for i in range(2)] for n in range(2)]
                KH = [[sb(f"k_hi{k}_{n}_{i}", [P, KEYSP], F32R) for i in range(2)] for n in range(2)]
                KL = [[sb(f"k_lo{k}_{n}_{i}", [P, KEYSP], F32R) for i in range(2)] for n in range(2)]
                V = [sb(f"v{k}_{n}", [P, KC, P]) for n in range(2)]
                SCX = [sb(f"ctx_scores{k}_{n}", [P, PU, JP]) for n in range(2)]
                ncmax = [sb(f"neg_max_ctx{k}_{n}", [P, PU]) for n in range(2)]
                PR = [sb(f"p{k}_{i}", [P, KC * P]) for i in range(NPB)]
                PTS = [[sb(f"p_t{k}_{i}_{h}", [P, KC, P]) for h in range(2)] for i in range(2)]
                OTh = sb(f"o_t_hi{k}", [P, N], F32R)
                OTl = sb(f"o_t_lo{k}", [P, N], F32R)
                nmax = sb(f"neg_max{k}", [P, NPB])
                ntmax = sb(f"neg_max_tok{k}", [P, NPB])
                rsum = sb(f"row_sums{k}", [P, NPB, 2])
                rtot = sb(f"row_totals{k}", [P, NPB])
                rinv = sb(f"row_invs{k}", [P, NPB])
                Y = sb(f"attn_out{k}", [P, TT, D]) if out_to is None else None
                mask8 = sb(f"ctx_mask{k}", [P, J], U8) if mask else None
                mrow = sb(f"ctx_mask_add{k}", [P, J]) if mask else None
            dest = X if out_to is not None else Y
            SPS = [PA[:, 0:N], PB[:, 0:N]]
            TBANK = [BANKS[2], PT]
            PJ = BANKS[5]
            FIRST_BANK = {("k", 0): 0, ("k", 1): 1, ("k", 2): 2, ("q", 0): 3, ("q", 1): 4, ("v", 0): 5,
                          ("v", 1): 6, ("v", 2): 7, ("x", 0): 0, ("x", 1): 1, ("x", 2): 2}

            def bank_of(B, kind, s):
                return PJ if B is L else BANKS[FIRST_BANK[kind, s]]

            loop_signals = []

            class Build:

                def __init__(self, prefix, make):
                    self.w_in = make(prefix + "weights_in")
                    self.w_hi, self.w_lo = make(prefix + "weights_hi"), make(prefix + "weights_lo")
                    self.k_ps, self.q_ps = make(prefix + "k_projected"), make(prefix + "q_projected")
                    self.v_ps, self.c_ps = make(prefix + "v_projected"), make(prefix + "ctx_scores")
                    self.kq_raw = make(prefix + "kq_raw")
                    self.kq_hi, self.kq_lo = make(prefix + "kq_hi"), make(prefix + "kq_lo")
                    self.k_dup = make(prefix + "k_doubled")
                    self.v_sb, self.c_sb = make(prefix + "v_copied"), make(prefix + "ctx_scores_copied")
                    self.c_masked = make(prefix + "ctx_masked") if mask else None
                    self.c_max = make(prefix + "ctx_max")

            def outside(name):
                return signal(f"{st}_{name}")

            def in_loop(name):
                s = semaphore(f"{st}_{name}")
                loop_signals.append(s)
                return s

            F = Build("first_", outside)
            L = Build("", in_loop)
            o_in, o_whi, o_wlo = in_loop("wo_in"), in_loop("wo_hi"), in_loop("wo_lo")
            s_ps, t_max, m_done = in_loop("scores"), in_loop("token_max"), in_loop("neg_max")
            e_done, ec_done = in_loop("exp"), in_loop("exp_ctx")
            total, i_done, p_done = in_loop("row_total"), in_loop("inv_sum"), in_loop("probs_scaled")
            t_ps, t_act, t_dve = in_loop("probs_t"), in_loop("probs_t_act"), in_loop("probs_t_dve")
            pv_done, o_raw = in_loop("pv"), in_loop("out_t_copied")
            o_hi, o_lo = in_loop("out_t_hi"), in_loop("out_t_lo")
            wo_ps, x_add = in_loop("projected"), in_loop("added")
            pads = signal(st + "_pads")
            mask_in, mask_row = (signal(st + "_mask_in"), signal(st + "_mask_row")) if mask else (None, None)
            turn = turn_signals(st)

            def load_qkv(sp, row, sem):
                for i, (name, off) in enumerate(weights[:n_q]):
                    sp.dma_start(raw[:, i, :].rearrange("p (c e) -> p c e", c=DC),
                                 A[name].rearrange("(c p) e -> p c e", p=P)[:, :, bass.ds(row + off, P)]
                                 ).then_inc(sem, 16)

            def double_k(sp, B, n):
                sp.wait_ge(B.kq_hi, KQ * n + 6)
                sp.wait_ge(B.kq_lo, KQ * n + 6)
                for t_ in (KH[(n + 1) % 2], KL[(n + 1) % 2]) if B is L else (KH[0], KL[0]):
                    for hd in range(2):
                        sp.dma_start(t_[hd][ROWS[1 - hd], :].bitcast(F32), t_[hd][ROWS[hd], :].bitcast(F32)
                                     ).then_inc(B.k_dup, 16)

            def sp_turn(sp, row, rows):
                for n in range(PT_):
                    if n < len(rows):
                        if n:
                            sp.wait_ge(L.w_lo, n_q * n)
                        load_qkv(sp, rows[n], L.w_in)
                    if n:
                        sp.wait_ge(o_wlo, n)
                    sp.dma_start(oraw[:], A[weights[n_q][0]][bass.ds(row + n * P, P), :]).then_inc(o_in, 16)
                    if n < BUILDS:
                        double_k(sp, L, n)
                end_turn(sp, "sp", turn, loop_signals)

            @part(sp_parts, ln)
            def _(sp, b):
                load_qkv(sp, 0, F.w_in)

            @part(sp_parts, st)
            def _(sp, b):
                if mask:
                    sp.dma_start(mask8[:], A[mask][bass.ds(b, 1), :].broadcast_to([P, J])).then_inc(mask_in, 16)
                sp.wait_ge(F.w_lo, n_q)
                load_qkv(sp, P, F.w_in)
                double_k(sp, F, 0)
                sp.wait_ge(F.w_lo, 2 * n_q)
                if turns > 1:
                    with sp.Fori(0, turns - 1) as p:
                        row = p * (PT_ * P)
                        sp_turn(sp, row, [row + (2 + n) * P for n in range(SPLITS)])
                sp_turn(sp, (pairs - PT_) * P, [min(pairs - PT_ + 2 + n, pairs - 1) * P for n in range(SPLITS)])

            def split_qkv(pool, B, n, i):
                pool.wait_ge(B.w_in, 16 * n_q * (n + 1))
                hi_of(pool, wh[:, i, :], raw[:, i, :]).then_inc(B.w_hi, 1)
                pool.wait_ge(B.w_hi, n_q * n + i + 1)
                pool.tensor_tensor(wl[:, i, :], raw[:, i, :], wh[:, i, :].bitcast(F32), ALU.subtract
                                   ).then_inc(B.w_lo, 1)

            def out_t_hi(pool, f):
                if f >= 2:
                    pool.wait_ge(wo_ps, 2 * (f - 1))
                pool.wait_ge(o_raw, f + 1)
                hi_of(pool, OTh[:, (f % 2) * HALF:(f % 2 + 1) * HALF], OR[:]).then_inc(o_hi, 1)

            def pool_piece(pool, B, n, q, kind, s):
                if kind in "kq":
                    m = KQ // 2 * n + s + (3 if kind == "q" else 0)
                    a, z = SEG[s]
                    pool.wait_ge(B.kq_raw, m + 1)
                    for hd in range(2):
                        dst = (KH if kind == "k" else QS)[q][hd][ROWS[hd], a:z]
                        hi_of(pool, dst, RB[m % 2][ROWS[hd], 0:z - a]).then_inc(B.kq_hi, 1)
                        pool.wait_ge(B.kq_hi, 2 * m + hd + 1)

            @part(pool_parts, ln)
            def _(pool, b):
                for i in range(n_q):
                    split_qkv(pool, F, 0, i)

            @part(pool_parts, st)
            def _(pool, b):
                if mask:
                    pool.wait_ge(mask_in, 16)
                    pool.tensor_scalar(mrow[:], mask8[:], MASKED, -MASKED, ALU.mult, ALU.add).then_inc(mask_row, 1)
                for v_ in V:
                    ins = pool.memset(v_[:, KC - 1, :], 0.0)
                ins.then_inc(pads, 1)
                for p_ in PR:
                    ins = pool.memset(p_[:, KEYS:KC * P], 0.0)
                if Y is not None:
                    ins = pool.memset(Y[:], 0.0)
                ins.then_inc(pads, 1)
                pool.wait_ge(pads, 2)
                for kind, s in PIECES.values():
                    pool_piece(pool, F, 0, 0, kind, s)
                pool.wait_ge(F.v_ps, 3)
                for i in range(n_q):
                    split_qkv(pool, F, 1, i)
                pool.tensor_tensor(X[:], X[:], rowb[:, bias_row, :].unsqueeze(1).broadcast_to([P, TT, D]),
                                   ALU.add).then_inc(pads, 1)
                pool.wait_ge(pads, 3)
                with pool.Fori(0, turns) as p:
                    for u in range(UNITS):
                        n, r = u // PU, u % PU
                        pool.wait_ge(i_done, u + 1)
                        pr = PR[u % NPB][:, 0:KEYS]
                        pool.tensor_scalar(pr, pr, rinv[:, u % NPB:u % NPB + 1], 0.0, ALU.mult, ALU.add
                                           ).then_inc(p_done, 1)
                        if n < BUILDS and r in PIECES and PIECES[r][0] in "kq":
                            pool.wait_ge(p_done, u + 1)
                            pool_piece(pool, L, n, (n + 1) % 2, *PIECES[r])
                        if r == 8 and n < SPLITS:
                            pool.wait_ge(L.v_ps, 3 * (n + 1))
                        if 8 <= r < 8 + n_q and n < SPLITS:
                            split_qkv(pool, L, n, r - 8)
                        if r == 7:
                            o_hi_, o_lo_ = oh[n % 2][:], ol[n % 2][:]
                            if n >= 2:
                                pool.wait_ge(wo_ps, 4 * (n - 1))
                            pool.wait_ge(o_in, 16 * (n + 1))
                            hi_of(pool, o_hi_, oraw[:]).then_inc(o_whi, 1)
                            pool.wait_ge(o_whi, n + 1)
                            pool.tensor_tensor(o_lo_, oraw[:], o_hi_.bitcast(F32), ALU.subtract).then_inc(o_wlo, 1)
                        if u % 8 == 4 and u > 8:
                            out_t_hi(pool, (u - 12) // 8)
                    out_t_hi(pool, 2 * PT_ - 1)
                    end_turn(pool, "pool", turn, loop_signals)

            def scores(pe, q, u, n, acc):
                t, hd = u // 2, u % 2
                a, z = SEG[n]
                tok = slice(t * P, (t + 1) * P)
                pe.matmul(acc, QS[q][hd][:, tok], KH[q][hd][:, a:z], start=True, stop=False)
                return pe.matmul(acc, QS[q][hd][:, tok], KL[q][hd][:, a:z], start=False, stop=True)

            def pe_piece(pe, B, n, q, kind, s):
                PJ = bank_of(B, kind, s)
                if kind == "k":
                    if B is F:
                        pass
                    elif s:
                        pe.wait_ge(B.kq_raw, KQ // 2 * n + s)
                    elif B is L and n:
                        pe.wait_ge(x_add, 4 * n - 3)
                        pe.wait_ge(B.w_lo, n_q * n)
                    idx, xh, xl = (IK, XTh, XTl) if s < 2 else (IKC, Ch, Cl)
                    tok = slice(s * HALF, (s + 1) * HALF) if s < 2 else slice(0, JP)
                    for c in range(DC):
                        e = slice(c * P, (c + 1) * P)
                        ins = mm3(pe, PJ[:, 0:tok.stop - tok.start], wh[:, idx, e], wl[:, idx, e],
                                  xh[:, c, tok], xl[:, c, tok], c == 0, c == DC - 1)
                    ins.then_inc(B.k_ps, 1)
                elif kind == "q":
                    if B is L:
                        pe.wait_ge(B.kq_raw, KQ // 2 * n + 3 + s)
                    tok = slice(s * HALF, (s + 1) * HALF)
                    for c in range(DC):
                        e = slice(c * P, (c + 1) * P)
                        ins = mm3(pe, PJ, wh[:, IQ, e], wl[:, IQ, e], XTh[:, c, tok], XTl[:, c, tok],
                                  c == 0, c == DC - 1)
                    ins.then_inc(B.q_ps, 1)
                elif kind == "v":
                    if B is L and s:
                        pe.wait_ge(B.v_sb, 3 * n + s)
                    elif B is L:
                        pe.wait_ge(B.kq_raw, KQ // 2 * (n + 1))
                    for t in (range(4 * s, 4 * s + 4) if s < 2 else (TT,)):
                        for c in range(DC):
                            e, tok = slice(c * P, (c + 1) * P), slice(t * P, (t + 1) * P)
                            if t < TT:
                                ins = mm3(pe, PJ[:, (t % 4) * P:(t % 4 + 1) * P], XTh[:, c, tok], XTl[:, c, tok],
                                          wh[:, IV, e], wl[:, IV, e], c == 0, c == DC - 1)
                            else:
                                ins = mm3(pe, PJ[0:JP, 0:P], Ch[:, c, :], Cl[:, c, :],
                                          wh[:, IVC, e], wl[:, IVC, e], c == 0, c == DC - 1)
                    ins.then_inc(B.v_ps, 1)
                else:
                    if B is L and s:
                        pe.wait_ge(B.c_sb, 3 * n + s)
                    elif s == 0:
                        pe.wait_ge(B.v_sb, 3 * (n + 1))
                        if B is L and n:
                            pe.wait_ge(x_add, 4 * n - 1)
                        pe.wait_ge(B.k_dup, 64 * (n + 1))
                        pe.wait_ge(B.kq_lo, KQ * (n + 1))
                    u0, u1 = CTX_UNITS[s]
                    for u in range(u0, u1):
                        ins = scores(pe, q, u, 2, PJ[:, (u - u0) * JP:(u - u0 + 1) * JP])
                    ins.then_inc(B.c_ps, 1)

            def pe_out(pe, n, quarter):
                done = 4 * n + quarter
                if quarter == 0:
                    pe.wait_ge(o_wlo, n + 1)
                if n == 0 and quarter == 0:
                    pe.wait_ge(L.c_sb, 3)
                elif n + 1 < BUILDS and quarter == 1:
                    pe.wait_ge(L.v_sb, 3 * (n + 2))
                elif n + 1 < BUILDS and quarter == 3:
                    pe.wait_ge(L.c_sb, 3 * (n + 2))
                else:
                    pe.wait_ge(x_add, done)
                pe.wait_ge(o_lo, 2 * n + quarter // 2 + 1)
                for t in (2 * quarter, 2 * quarter + 1):
                    tok = slice(t * P, (t + 1) * P)
                    ins = mm3(pe, PJ[:, (t % 2) * D:(t % 2 + 1) * D], OTh[:, tok], OTl[:, tok], oh[n % 2][:], ol[n % 2][:],
                              True, True)
                ins.then_inc(wo_ps, 1)

            @part(pe_parts, st)
            def _(pe, b):
                pe.wait_ge(F.w_lo, n_q)
                for kind, s in PIECES.values():
                    pe_piece(pe, F, 0, 0, kind, s)
                pe.wait_ge(F.w_lo, 2 * n_q)
                pe.wait_ge(F.c_sb, 3)
                with pe.Fori(0, turns) as p:
                    for i in range(UNITS + LAG + 2):
                        j = i - LAG
                        g = (j - 2) // 2
                        for r in range(3):
                            if 0 <= j < UNITS:
                                if r == 0:
                                    pe.wait_ge(p_done, j + 1)
                                    if j:
                                        pe.wait_ge(t_dve, j)
                                elif r == 1 and j:
                                    pe.wait_ge(t_act, 2 * j)
                                elif r == 2:
                                    pe.wait_ge(t_act, 2 * j + 1)
                                c0, c1 = ROUNDS[r]
                                for c in range(c0, c1):
                                    ins = pe.transpose(TBANK[(3 * j + r) % 2][:, (c - c0) * P:(c - c0 + 1) * P],
                                                       PR[j % NPB][:, c * P:(c + 1) * P], ident[:])
                                ins.then_inc(t_ps, 1)
                            if i < UNITS and r < 2:
                                if r == 0 and i >= 2:
                                    pe.wait_ge(e_done, i - 1)
                                ins = scores(pe, i // PU % 2, i % PU, r, SPS[i % 2][:, r * HALF:(r + 1) * HALF])
                                if r:
                                    ins.then_inc(s_ps, 1)
                            if 0 <= g < PT_ * TT and r < 2:
                                if j % 2 == 0 and r == 0:
                                    pe.wait_ge(t_act, 4 * (g + 1))
                                    pe.wait_ge(t_dve, 2 * (g + 1))
                                    if g and g % 4 == 0:
                                        pe.wait_ge(o_raw, g // 4)
                                c0, c1 = [(0, 2), (2, 4), (4, 7), (7, KC)][(j % 2) * 2 + r]
                                for c in range(c0, c1):
                                    for hd in range(2):
                                        ins = pe.matmul(PV[ROWS[hd], (g % 4) * P:(g % 4 + 1) * P],
                                                        V[g // TT % 2][:, c, ROWS[hd]], PTS[g % 2][hd][:, c, :],
                                                        start=c == 0, stop=c == KC - 1)
                                if c1 == KC:
                                    ins.then_inc(pv_done, 1)
                        if i < UNITS:
                            n, slot = i // PU, i % PU
                            if n < BUILDS and slot in PIECES:
                                pe_piece(pe, L, n, (n + 1) % 2, *PIECES[slot])
                            if n and slot in OUT_BEFORE:
                                pe_out(pe, n - 1, OUT_BEFORE[slot])
                            if slot in OUT_OWN:
                                pe_out(pe, n, OUT_OWN[slot])
                    for quarter in (1, 2, 3):
                        pe_out(pe, PT_ - 1, quarter)
                    end_turn(pe, "pe", turn, loop_signals)

            def act_piece(act, B, n, q, kind, s):
                PJ = bank_of(B, kind, s)
                if kind in "kq":
                    m = KQ // 2 * n + s + (3 if kind == "q" else 0)
                    if m >= 2:
                        act.wait_ge(B.kq_lo, 2 * (m - 1))
                    if kind == "k":
                        act.wait_ge(B.k_ps, 3 * n + s + 1)
                    else:
                        act.wait_ge(B.q_ps, 2 * n + s + 1)
                    a, z = SEG[s]
                    act.activation(RB[m % 2][:, 0:z - a], PJ[:, 0:z - a], ACT.Copy,
                                   scale=1.0 if kind == "k" else DH ** -0.5).then_inc(B.kq_raw, 1)
                elif kind == "v":
                    act.wait_ge(B.v_ps, 3 * n + s + 1)
                    if s < 2:
                        act.activation(V[q][:, 4 * s:4 * s + 4, :].rearrange("p c e -> p (c e)"), PJ, ACT.Copy
                                       ).then_inc(B.v_sb, 1)
                    else:
                        act.activation(V[q][0:JP, TT, :], PJ[0:JP, 0:P], ACT.Copy).then_inc(B.v_sb, 1)
                else:
                    u0, u1 = CTX_UNITS[s]
                    act.wait_ge(B.c_ps, 3 * n + s + 1)
                    act.activation(SCX[q][:, u0:u1, :].rearrange("p u j -> p (u j)"), PJ[:, 0:(u1 - u0) * JP],
                                   ACT.Copy).then_inc(B.c_sb, 1)

            @part(act_parts, st)
            def _(act, b):
                act.wait_ge(pads, 1)
                for kind, s in PIECES.values():
                    act_piece(act, F, 0, 0, kind, s)
                act.wait_ge(pads, 2)
                with act.Fori(0, turns) as p:
                    for i in range(UNITS + LAG):
                        j = i - LAG
                        if 0 <= j < UNITS:
                            for r in (0, 2):
                                c0, c1 = ROUNDS[r]
                                if r == 2 and 1 <= i <= BUILDS * PU and (i - 1) % PU in PIECES:
                                    n = (i - 1) // PU
                                    act_piece(act, L, n, (n + 1) % 2, *PIECES[(i - 1) % PU])
                                act.wait_ge(t_ps, 3 * j + r + 1)
                                if r == 0 and j // 2 >= 2:
                                    act.wait_ge(pv_done, j // 2 - 1)
                                act.activation(PTS[(j // 2) % 2][j % 2][:, c0:c1, :].rearrange("p c q -> p (c q)"),
                                               TBANK[(3 * j + r) % 2][:, 0:(c1 - c0) * P], ACT.Copy
                                               ).then_inc(t_act, 1)
                        elif 1 <= i < LAG and i - 1 in PIECES:
                            act_piece(act, L, 0, 1, *PIECES[i - 1])
                        if i < UNITS:
                            s_ = i % NPB
                            act.wait_ge(m_done, i + 1)
                            if i >= NPB:
                                act.wait_ge(t_ps, 3 * (i - NPB + 1))
                            act.activation(PR[s_][:, 0:N], SPS[i % 2], ACT.Exp, bias=nmax[:, s_:s_ + 1],
                                           accum_out=rsum[:, s_, 0:1]).then_inc(e_done, 1)
                            act.activation(PR[s_][:, N:KEYS], SCX[i // PU % 2][:, i % PU, 0:J], ACT.Exp,
                                           bias=nmax[:, s_:s_ + 1], accum_out=rsum[:, s_, 1:2]).then_inc(ec_done, 1)
                    end_turn(act, "act", turn, loop_signals)

            def dve_piece(dve, B, n, q, kind, s):
                if kind in "kq":
                    m = KQ // 2 * n + s + (3 if kind == "q" else 0)
                    a, z = SEG[s]
                    for hd in range(2):
                        dve.wait_ge(B.kq_hi, 2 * m + hd + 1)
                        own, other = ROWS[hd], ROWS[1 - hd]
                        hi, lo = ((KH[q][hd][own, a:z], KL[q][hd][own, a:z]) if kind == "k" else
                                  (QS[q][hd][own, a:z], QS[q][hd][other, a:z]))
                        dve.tensor_tensor(lo, RB[m % 2][own, 0:z - a], hi.bitcast(F32), ALU.subtract
                                          ).then_inc(B.kq_lo, 1)

            def ctx_max(dve, B, n, q):
                dve.wait_ge(B.c_sb, 3 * (n + 1))
                if mask:
                    dve.tensor_tensor(SCX[q][:, :, 0:J], SCX[q][:, :, 0:J], mrow[:].unsqueeze(1).broadcast_to(
                        [P, PU, J]), ALU.add).then_inc(B.c_masked, 1)
                    dve.wait_ge(B.c_masked, n + 1)
                dve.tensor_reduce(ncmax[q][:], SCX[q][:, :, 0:J], AX.X, ALU.max, negate=True).then_inc(B.c_max, 1)

            def out_t_copy(dve, f):
                if f:
                    dve.wait_ge(o_lo, f)
                dve.wait_ge(pv_done, 4 * (f + 1))
                dve.tensor_copy(OR[:], PV[:]).then_inc(o_raw, 1)

            def out_t_lo(dve, f):
                cols = slice((f % 2) * HALF, (f % 2 + 1) * HALF)
                dve.wait_ge(o_hi, f + 1)
                dve.tensor_tensor(OTl[:, cols], OR[:], OTh[:, cols].bitcast(F32), ALU.subtract).then_inc(o_lo, 1)

            def add_out(dve, n, quarter):
                d_ = dest[:, 2 * quarter:2 * quarter + 2, :].rearrange("p t d -> p (t d)")
                dve.wait_ge(wo_ps, 4 * n + quarter + 1)
                if n:
                    dve.wait_ge(x_add, 4 * (n - 1) + quarter + 1)
                else:
                    dve.wait_ge(pads, 3)
                scalar = 1.0 if gate is None else tg[:, gate:gate + 1]
                dve.scalar_tensor_tensor(d_, PJ, scalar, d_, ALU.mult, ALU.add).then_inc(x_add, 1)

            @part(dve_parts, st)
            def _(dve, b):
                for kind, s in PIECES.values():
                    dve_piece(dve, F, 0, 0, kind, s)
                if mask:
                    dve.wait_ge(mask_row, 1)
                ctx_max(dve, F, 0, 0)
                dve.wait_ge(F.c_max, 1)
                dve.wait_ge(pads, 2)
                with dve.Fori(0, turns) as p:
                    for i in range(UNITS + LAG + 1):
                        j = i - LAG
                        if i >= 13 and (i - 13) % 8 == 0:
                            out_t_copy(dve, (i - 13) // 8)
                        if i >= 15 and (i - 15) % 8 == 0:
                            out_t_lo(dve, (i - 15) // 8)
                        if 0 <= j < UNITS:
                            c0, c1 = ROUNDS[1]
                            dve.wait_ge(t_ps, 3 * j + 2)
                            if j // 2 >= 2:
                                dve.wait_ge(pv_done, j // 2 - 1)
                            dve.tensor_copy(PTS[(j // 2) % 2][j % 2][:, c0:c1, :].rearrange("p c q -> p (c q)"),
                                            TBANK[(3 * j + 1) % 2][:, 0:(c1 - c0) * P]).then_inc(t_dve, 1)
                        if 1 <= i <= UNITS:
                            n, slot = (i - 1) // PU, (i - 1) % PU
                            if n and slot in OUT_BEFORE:
                                add_out(dve, n - 1, OUT_BEFORE[slot])
                            if slot in OUT_OWN:
                                add_out(dve, n, OUT_OWN[slot])
                        if i < UNITS:
                            s_ = i % NPB
                            dve.wait_ge(s_ps, i + 1)
                            if i >= NPB:
                                dve.wait_ge(m_done, i - NPB + 1)
                            dve.tensor_reduce(ntmax[:, s_:s_ + 1], SPS[i % 2], AX.X, ALU.max, negate=True
                                              ).then_inc(t_max, 1)
                            dve.wait_ge(t_max, i + 1)
                            if i and i % PU == 0:
                                dve.wait_ge(L.c_max, i // PU)
                            if i >= NPB:
                                dve.wait_ge(ec_done, i - NPB + 1)
                            dve.tensor_tensor(nmax[:, s_:s_ + 1], ntmax[:, s_:s_ + 1],
                                              ncmax[i // PU % 2][:, i % PU:i % PU + 1], ALU.min).then_inc(m_done, 1)
                        if 2 <= i < BUILDS * PU + 2 and (i - 2) % PU in PIECES:
                            n = (i - 2) // PU
                            dve_piece(dve, L, n, (n + 1) % 2, *PIECES[(i - 2) % PU])
                        if 1 <= i <= UNITS:
                            s_ = (i - 1) % NPB
                            dve.wait_ge(ec_done, i)
                            if i - 1 >= NPB:
                                dve.wait_ge(i_done, i - NPB)
                            dve.tensor_tensor(rtot[:, s_:s_ + 1], rsum[:, s_, 0:1], rsum[:, s_, 1:2], ALU.add
                                              ).then_inc(total, 1)
                            dve.wait_ge(total, i)
                            if i - 1 >= NPB:
                                dve.wait_ge(p_done, i - NPB)
                            dve.reciprocal(rinv[:, s_:s_ + 1], rtot[:, s_:s_ + 1]).then_inc(i_done, 1)
                            if (i - 1) % PU == 13 and (i - 1) // PU < BUILDS:
                                n = (i - 1) // PU
                                ctx_max(dve, L, n, (n + 1) % 2)
                    out_t_copy(dve, 2 * PT_ - 1)
                    out_t_lo(dve, 2 * PT_ - 1)
                    for quarter in (1, 2, 3):
                        add_out(dve, PT_ - 1, quarter)
                    end_turn(dve, "dve", turn, loop_signals)
            return Y

        ln_stage("ln1x")
        latent_attention(1, 8, [("L1_xattn_Wq1", 0), ("L1_xattn_Wk1", 0), ("L1_xattn_Wv1", 0),
                                ("L1_xattn_Wk2", 0), ("L1_xattn_Wv2", 0), ("L1_xattn_Wo", 0)],
                         (CTh, CTl), X, 1, BO1)

        ln_stage("ln1f")
        moe_scope = ExitStack()
        scope = moe_scope
        GPT = 2
        TURNS = EXPERTS // (EG * GPT)
        GW = EG * INTER
        SC = sb("router_scores", [P, TT, EXPERTS])
        gwr = sb("router_w", [P, DC, EXPERTS])
        gwh = sb("router_w_hi", [P, DC, EXPERTS], F32R)
        gwl = sb("router_w_lo", [P, DC, EXPERTS], F32R)
        lmax = sb("router_max", [P, TT])
        lshift = sb("router_shifted", [P, TT, EXPERTS])
        ex = sb("router_exp", [P, TT, EXPERTS])
        cmp_ = sb("router_compare", [P, TT, EXPERTS, EXPERTS])
        rank = sb("router_rank", [P, TT, EXPERTS])
        rank2 = sb("router_rank_ties", [P, TT, EXPERTS])
        lower = sb("router_lower_index", [P, EXPERTS, EXPERTS])
        selsum = sb("router_selected_sum", [P, TT])
        selinv = sb("router_selected_inv", [P, TT])
        W1, W3, W2 = 0, 1, 2
        mraw = [sb(f"experts_raw{i}", [P, 3, DC * GW]) for i in range(GPT)]
        mwh = [sb(f"experts_hi{i}", [P, 3, DC * GW], F32R) for i in range(GPT)]
        mwl = [sb(f"experts_lo{i}", [P, 3, DC * GW], F32R) for i in range(GPT)]
        mth = [sb(f"expert_tanh{i}", [P, GW]) for i in range(2)]
        mga = [sb(f"expert_gate{i}", [P, GW]) for i in range(2)]
        mac = [sb(f"expert_act{i}", [P, GW]) for i in range(2)]
        math_ = [sb(f"expert_act_t_hi{i}", [P, GW], F32R) for i in range(2)]
        matl = [sb(f"expert_act_t_lo{i}", [P, GW], F32R) for i in range(2)]
        moe_scope.close()
        scope = life

        gw_in = signal("router_w_in")
        gw_split = signal("router_w_split")
        lower_set = signal("router_lower_set")
        logits = signal("router_logits")
        r_steps = signal("router_steps")
        r_shift = signal("router_shift")
        r_exp = signal("router_exp_done")

        @part(pool_parts, "ln1f")
        def _(pool, b):
            pool.memset(lower[:], 1.0).then_inc(lower_set, 1)
            pool.wait_ge(lower_set, 1)
            pool.affine_select(out=lower[:], in_=lower[:], compare_op=ALU.is_ge, fill=0.0, base=-1,
                               pattern=[[1, EXPERTS], [-1, EXPERTS]], channel_multiplier=0).then_inc(lower_set, 1)
            pool.wait_ge(gw_in, 16)
            hi_of(pool, gwh[:], gwr[:]).then_inc(gw_split, 1)
            pool.wait_ge(gw_split, 1)
            pool.tensor_tensor(gwl[:], gwr[:], gwh[:].bitcast(F32), ALU.subtract).then_inc(gw_split, 1)

        @part(pe_parts, "router")
        def _(pe, b):
            pe.wait_ge(gw_split, 2)
            for t in range(TT):
                tok = slice(t * P, (t + 1) * P)
                for c in range(DC):
                    ins = mm3(pe, PT[:, t * EXPERTS:(t + 1) * EXPERTS], XTh[:, c, tok], XTl[:, c, tok],
                              gwh[:, c, :], gwl[:, c, :], c == 0, c == DC - 1)
            ins.then_inc(logits, 1)

        @part(act_parts, "router")
        def _(act, b):
            act.wait_ge(r_shift, 1)
            act.activation(ex[:], lshift[:], ACT.Exp).then_inc(r_exp, 1)

        @part(dve_parts, "router")
        def _(dve, b):
            chain = Chain(dve, r_steps)
            lg = PT[:, 0:TT * EXPERTS].rearrange("p (t e) -> p t e", t=TT)
            dve.wait_ge(logits, 1)
            chain.step(dve.tensor_reduce(lmax[:], lg, AX.X, ALU.max))
            chain.settle()
            dve.tensor_tensor(lshift[:], lg, lmax[:].unsqueeze(2).broadcast_to([P, TT, EXPERTS]),
                              ALU.subtract).then_inc(r_shift, 1)
            dve.wait_ge(r_exp, 1)
            four = [P, TT, EXPERTS, EXPERTS]
            mine = ex[:].unsqueeze(3).broadcast_to(four)
            other = ex[:].unsqueeze(2).broadcast_to(four)
            chain.step(dve.tensor_tensor(cmp_[:], other, mine, ALU.is_gt))
            chain.settle()
            chain.step(dve.tensor_reduce(rank[:], cmp_[:], AX.X, ALU.add))
            chain.settle()
            chain.step(dve.tensor_tensor(cmp_[:], other, mine, ALU.is_equal))
            dve.wait_ge(lower_set, 2)
            chain.settle()
            chain.step(dve.tensor_tensor(cmp_[:], cmp_[:], lower[:].unsqueeze(1).broadcast_to(four), ALU.mult))
            chain.settle()
            chain.step(dve.tensor_reduce(rank2[:], cmp_[:], AX.X, ALU.add))
            chain.settle()
            chain.step(dve.tensor_tensor(rank[:], rank[:], rank2[:], ALU.add))
            chain.settle()
            chain.step(dve.scalar_tensor_tensor(SC[:], rank[:], float(TOP_K), ex[:], ALU.is_lt, ALU.mult))
            chain.settle()
            chain.step(dve.tensor_reduce(selsum[:], SC[:], AX.X, ALU.add))
            chain.settle()
            chain.step(dve.reciprocal(selinv[:], selsum[:]))
            chain.settle()
            chain.step(dve.scalar_tensor_tensor(SC[:], SC[:], 0.5, selinv[:].unsqueeze(2).broadcast_to(
                [P, TT, EXPERTS]), ALU.mult, ALU.mult))

        moe_loop = []

        def in_moe(name):
            s = semaphore("moe_" + name)
            moe_loop.append(s)
            return s

        m_first = [signal(f"moe_first_weights{i}") for i in range(GPT)]
        m_first_hi = signal("moe_first_hi")
        m_first_lo = signal("moe_first_lo")
        m_in = in_moe("weights_in")
        m_hi = in_moe("weights_hi")
        m_lo = in_moe("weights_lo")
        m_gu = in_moe("gate_up")
        m_tanh = in_moe("tanh")
        m_gate = in_moe("gate")
        m_act = in_moe("act")
        m_tps = in_moe("act_transposed")
        m_thi = in_moe("act_t_hi")
        m_tlo = in_moe("act_t_lo")
        m_out = in_moe("out")
        m_x = in_moe("residual")
        moe_turn = turn_signals("moe")
        STEPS = GPT * TT
        MG = [BANKS[0], BANKS[2]]
        MU = [BANKS[1], BANKS[3]]
        MT = [BANKS[4], BANKS[5]]
        MO = [BANKS[6], BANKS[7]]

        def moe_load(sp, i, e0, sem):
            for k, name in ((W1, "L1_ffn_w1"), (W3, "L1_ffn_w3")):
                for c in range(DC):
                    sp.dma_start(mraw[i][:, k, c * GW:(c + 1) * GW].rearrange("p (e i) -> p e i", e=EG),
                                 A[name].rearrange("e (c p) i -> c p e i", p=P)[c][:, bass.ds(e0, EG), :]
                                 ).then_inc(sem, 16)
            sp.dma_start(mraw[i][:, W2, :].rearrange("p (e d) -> p e d", e=EG),
                         A["L1_ffn_w2"].rearrange("e p d -> p e d")[:, bass.ds(e0, EG), :]).then_inc(sem, 16)
        M_LOADS = 16 * (2 * DC + 1)

        def moe_turn_loads(sp, e0):
            moe_load(sp, 0, e0, m_in)
            sp.wait_ge(m_lo, 1)
            moe_load(sp, 1, e0 + EG, m_in)
            sp.wait_ge(m_in, 2 * M_LOADS)
            end_turn(sp, "sp", moe_turn, moe_loop)

        @part(sp_parts, "ln1f")
        def _(sp, b):
            sp.dma_start(gwr[:], A["L1_ffn_gateT"].rearrange("(c p) e -> p c e", p=P)).then_inc(gw_in, 16)
            for i in range(GPT):
                moe_load(sp, i, i * EG, m_first[i])

        @part(sp_parts, "moe")
        def _(sp, b):
            sp.wait_ge(m_first_lo, 1)
            with sp.Fori(1, TURNS) as p:
                moe_turn_loads(sp, p * (EG * GPT))
            moe_turn_loads(sp, (TURNS - 1) * EG * GPT)

        @part(pool_parts, "router")
        def _(pool, b):
            pool.wait_ge(m_first[0], M_LOADS)
            hi_of(pool, mwh[0][:], mraw[0][:]).then_inc(m_first_hi, 1)
            pool.wait_ge(m_first_hi, 1)
            pool.tensor_tensor(mwl[0][:], mraw[0][:], mwh[0][:].bitcast(F32), ALU.subtract).then_inc(m_first_lo, 1)

        @part(pool_parts, "moe")
        def _(pool, b):
            pool.wait_ge(m_first[1], M_LOADS)
            with pool.Fori(0, TURNS) as p:
                for n, i in enumerate((1, 0)):
                    if i == 0:
                        pool.wait_ge(m_out, TT)
                        pool.wait_ge(m_in, 2 * M_LOADS)
                    hi_of(pool, mwh[i][:], mraw[i][:]).then_inc(m_hi, 1)
                    pool.wait_ge(m_hi, n + 1)
                    pool.tensor_tensor(mwl[i][:], mraw[i][:], mwh[i][:].bitcast(F32), ALU.subtract).then_inc(m_lo, 1)
                end_turn(pool, "pool", moe_turn, moe_loop)

        @part(pe_parts, "moe")
        def _(pe, b):
            with pe.Fori(0, TURNS) as p:
                for i in range(STEPS + 2):
                    if i < STEPS:
                        g, t = i // TT, i % TT
                        tok = slice(t * P, (t + 1) * P)
                        if i == TT:
                            pe.wait_ge(m_lo, 1)
                        if i >= 2:
                            pe.wait_ge(m_act, i - 1)
                        for acc, k in ((MG[i % 2], W1), (MU[i % 2], W3)):
                            for c in range(DC):
                                w = slice(c * GW, (c + 1) * GW)
                                ins = mm3(pe, acc, XTh[:, c, tok], XTl[:, c, tok], mwh[g][:, k, w], mwl[g][:, k, w],
                                          c == 0, c == DC - 1)
                        ins.then_inc(m_gu, 1)
                    j = i - 1
                    if 0 <= j < STEPS:
                        pe.wait_ge(m_act, j + 1)
                        if j >= 2:
                            pe.wait_ge(m_tlo, j - 1)
                        for e in range(EG):
                            ins = pe.transpose(MT[j % 2][:, e * P:(e + 1) * P], mac[j % 2][:, e * P:(e + 1) * P], ident[:])
                        ins.then_inc(m_tps, 1)
                    o = i - 2
                    if 0 <= o < STEPS:
                        pe.wait_ge(m_tlo, o + 1)
                        if o >= 2:
                            pe.wait_ge(m_x, o - 1)
                        for e in range(EG):
                            col, w = slice(e * P, (e + 1) * P), slice(e * D, (e + 1) * D)
                            ins = mm3(pe, MO[o % 2][:, 0:D], math_[o % 2][:, col], matl[o % 2][:, col],
                                      mwh[o // TT][:, W2, w], mwl[o // TT][:, W2, w], e == 0, e == EG - 1)
                        ins.then_inc(m_out, 1)
                end_turn(pe, "pe", moe_turn, moe_loop)

        @part(act_parts, "moe")
        def _(act, b):
            with act.Fori(0, TURNS) as p:
                for i in range(STEPS + 1):
                    if i < STEPS:
                        act.wait_ge(m_gu, i + 1)
                        if i >= 2:
                            act.wait_ge(m_gate, i - 1)
                        act.activation(mth[i % 2][:], MG[i % 2], ACT.Tanh, scale=0.5).then_inc(m_tanh, 1)
                    j = i - 1
                    if 0 <= j < STEPS:
                        act.wait_ge(m_tps, j + 1)
                        if j >= 2:
                            act.wait_ge(m_out, j - 1)
                        act.activation(math_[j % 2][:], MT[j % 2], ACT.Copy).then_inc(m_thi, 1)
                end_turn(act, "act", moe_turn, moe_loop)

        @part(dve_parts, "moe")
        def _(dve, b):
            with dve.Fori(0, TURNS) as p:
                for i in range(STEPS + 2):
                    if i < STEPS:
                        g, t = i // TT, i % TT
                        dve.wait_ge(m_tanh, i + 1)
                        if i >= 2:
                            dve.wait_ge(m_act, i - 1)
                        dve.scalar_tensor_tensor(mga[i % 2][:], mth[i % 2][:], 1.0, MG[i % 2], ALU.add, ALU.mult
                                                 ).then_inc(m_gate, 1)
                        dve.wait_ge(m_gate, i + 1)
                        if i >= 2:
                            dve.wait_ge(m_tps, i - 1)
                        for e in range(EG):
                            col = slice(e * P, (e + 1) * P)
                            ins = dve.scalar_tensor_tensor(mac[i % 2][:, col], mga[i % 2][:, col], SC[:, t, g * EG + e:g * EG + e + 1],
                                                           MU[i % 2][:, col], ALU.mult, ALU.mult)
                        ins.then_inc(m_act, 1)
                    j = i - 1
                    if 0 <= j < STEPS:
                        dve.wait_ge(m_thi, j + 1)
                        dve.tensor_tensor(matl[j % 2][:], MT[j % 2], math_[j % 2][:].bitcast(F32), ALU.subtract
                                          ).then_inc(m_tlo, 1)
                    o = i - 2
                    if 0 <= o < STEPS:
                        t = o % TT
                        dve.wait_ge(m_out, o + 1)
                        if o >= TT:
                            dve.wait_ge(m_x, o - TT + 1)
                        dve.scalar_tensor_tensor(X[:, t, :], MO[o % 2][:, 0:D], tg[:, LAYERS + 1:LAYERS + 2],
                                                 X[:, t, :], ALU.mult, ALU.add).then_inc(m_x, 1)
                dve.tensor_copy(SC[:, :, 0:GPT * EG], SC[:, :, EXPERTS - GPT * EG:])
                end_turn(dve, "dve", moe_turn, moe_loop)

        next_layer()
        Y2 = latent_attention(2, 16, [("L2_xattn_Wq", 0), ("L2_xattn_Wkv", 0), ("L2_xattn_Wkv", INNER),
                                      ("L2_xattn_Wout", 0)],
                              (CNTh, CNTl), None, None, BO, mask="mask_BxS2_bf1")
        ln_stage("ln2x", XF=Y2[:].rearrange("p t d -> p (t d)").rearrange("p (c n) -> p c n", c=DC), gamma=2)
        out2_steps = signal("out2_steps")

        @part(dve_parts, "out2")
        def _(dve, b):
            chain = Chain(dve, out2_steps)
            norm_stats(dve, chain, lambda t: Y2[:, t, :], TT)
            for t in range(TT):
                ins = dve.tensor_scalar(Y2[:, t, :], Y2[:, t, :], rstd[:, t:t + 1], nmr[:, t:t + 1], ALU.mult, ALU.add)
            chain.step(ins)
            chain.settle()
            all_rows = [P, TT, D]
            chain.step(dve.tensor_tensor(Y2[:], Y2[:], rowb[:, GO, :].unsqueeze(1).broadcast_to(all_rows), ALU.mult))
            chain.settle()
            chain.step(dve.tensor_tensor(X[:], X[:], Y2[:], ALU.add))

        WR, WK, WV = range(3)
        rwkv_scope = ExitStack()
        scope = rwkv_scope
        XF = sb("x_t", [P, DC, N])
        kraw = sb("mix_w_raw", [P, 3, DC * D])
        kwh = sb("mix_w_hi", [P, 3, DC * D], F32R)
        kwl = sb("mix_w_lo", [P, 3, DC * D], F32R)
        SH = [sb(f"mixed{m}", [P, DC, N]) for m in range(2)]
        SHh = [sb(f"mixed_hi{m}", [P, DC, N], F32R) for m in range(2)]
        SHl = [sb(f"mixed_lo{m}", [P, DC, N], F32R) for m in range(2)]
        KR = sb("k_relu", [P, DC, N])
        K2h = sb("k_squared_hi", [P, DC, N], F32R)
        K2l = sb("k_squared_lo", [P, DC, N], F32R)
        RT = sb("r_tanh", [P, TT, D])
        rwkv_scope.close()
        scope = life
        ln_stage("ln2f", XF=XF)

        MIX = [(m, c, h) for m in (1, 0) for c in range(DC) for h in range(NHALF)]
        kw_in = signal("mix_w_in")
        kw_split = signal("mix_w_split")
        s_zero = signal("mix_first_token_zero")
        s_prev = signal("mix_prev")
        s_mix = signal("mix_done")
        s_hi = signal("mix_hi")
        s_lo = signal("mix_lo")
        k_ps = signal("mix_k")
        k_relu = signal("mix_k_relu")
        k_hi = signal("mix_k_hi")
        k_sq = signal("mix_k_squared")
        k_lo = signal("mix_k_lo")
        r_ps = signal("mix_r")
        r_tanh = signal("mix_r_tanh")
        v_ps = signal("mix_v")
        v_gated = signal("mix_v_gated")
        v_x = signal("mix_residual")

        @part(sp_parts, "ln2f")
        def _(sp, b):
            for k, name in ((WR, "L2_ffn_rT"), (WK, "L2_ffn_kT"), (WV, "L2_ffn_vT")):
                sp.dma_start(kraw[:, k, :].rearrange("p (c d) -> p c d", c=DC),
                             A[name].rearrange("(c p) d -> p c d", p=P)).then_inc(kw_in, 16)

        @part(pool_parts, "ln2f")
        def _(pool, b):
            for m in range(2):
                ins = pool.memset(SH[m][:, :, 0:1], 0.0)
            ins.then_inc(s_zero, 1)
            pool.wait_ge(kw_in, 48)
            hi_of(pool, kwh[:], kraw[:]).then_inc(kw_split, 1)
            pool.wait_ge(kw_split, 1)
            pool.tensor_tensor(kwl[:], kraw[:], kwh[:].bitcast(F32), ALU.subtract).then_inc(kw_split, 1)

        @part(act_parts, "rwkv")
        def _(act, b):
            for q0 in (0, 4):
                for m, c, h in MIX[q0:q0 + 4]:
                    a, z = max(h * HALF, 1), (h + 1) * HALF
                    act.activation(SH[m][:, c, a:z], XF[:, c, a - 1:z - 1], ACT.Copy, scale=omm[:, c, m:m + 1]
                                   ).then_inc(s_prev, 1)
                for q, (m, c, h) in enumerate(MIX[q0:q0 + 4], q0):
                    cols = slice(h * HALF, (h + 1) * HALF)
                    act.wait_ge(s_mix, q + 1)
                    act.activation(SHh[m][:, c, cols], SH[m][:, c, cols], ACT.Copy).then_inc(s_hi, 1)
            for q, (c, h) in enumerate(QUADS):
                cols = slice(h * HALF, (h + 1) * HALF)
                act.wait_ge(k_ps, q + 1)
                act.activation(KR[:, c, cols], BANKS[q], ACT.Relu).then_inc(k_relu, 1)
                act.wait_ge(k_relu, q + 1)
                act.activation(K2h[:, c, cols], KR[:, c, cols], ACT.Square).then_inc(k_hi, 1)
            for q in range(4):
                act.wait_ge(r_ps, q + 1)
                act.activation(RT[:, 2 * q:2 * q + 2, :].rearrange("p t d -> p (t d)"), BANKS[4 + q], ACT.Tanh,
                               scale=0.5).then_inc(r_tanh, 1)

        @part(dve_parts, "rwkv")
        def _(dve, b):
            dve.wait_ge(s_zero, 1)
            for q0 in (0, 4):
                for q, (m, c, h) in enumerate(MIX[q0:q0 + 4], q0):
                    cols = slice(h * HALF, (h + 1) * HALF)
                    dve.wait_ge(s_prev, q + 1)
                    dve.scalar_tensor_tensor(SH[m][:, c, cols], XF[:, c, cols], mus[:, c, m:m + 1],
                                             SH[m][:, c, cols], ALU.mult, ALU.add).then_inc(s_mix, 1)
                for q, (m, c, h) in enumerate(MIX[q0:q0 + 4], q0):
                    cols = slice(h * HALF, (h + 1) * HALF)
                    dve.wait_ge(s_hi, q + 1)
                    dve.tensor_tensor(SHl[m][:, c, cols], SH[m][:, c, cols], SHh[m][:, c, cols].bitcast(F32),
                                      ALU.subtract).then_inc(s_lo, 1)
            for q, (c, h) in enumerate(QUADS):
                cols = slice(h * HALF, (h + 1) * HALF)
                dve.wait_ge(k_hi, q + 1)
                dve.tensor_tensor(KR[:, c, cols], KR[:, c, cols], KR[:, c, cols], ALU.mult).then_inc(k_sq, 1)
                dve.wait_ge(k_sq, q + 1)
                dve.tensor_tensor(K2l[:, c, cols], KR[:, c, cols], K2h[:, c, cols].bitcast(F32), ALU.subtract
                                  ).then_inc(k_lo, 1)
            for q in range(4):
                rt = RT[:, 2 * q:2 * q + 2, :].rearrange("p t d -> p (t d)")
                xt = X[:, 2 * q:2 * q + 2, :].rearrange("p t d -> p (t d)")
                dve.wait_ge(v_ps, q + 1)
                dve.wait_ge(r_tanh, q + 1)
                dve.scalar_tensor_tensor(rt, rt, 1.0, BANKS[q], ALU.add, ALU.mult).then_inc(v_gated, 1)
                dve.wait_ge(v_gated, q + 1)
                dve.scalar_tensor_tensor(xt, rt, htg2[:, 0:1], xt, ALU.mult, ALU.add).then_inc(v_x, 1)

        @part(pe_parts, "rwkv")
        def _(pe, b):
            pe.wait_ge(kw_split, 2)
            pe.wait_ge(s_lo, 4)
            for q, (d, h) in enumerate(QUADS):
                cols = slice(h * HALF, (h + 1) * HALF)
                for c in range(DC):
                    w = slice(c * D + d * P, c * D + (d + 1) * P)
                    ins = mm3(pe, BANKS[q], kwh[:, WK, w], kwl[:, WK, w], SHh[1][:, c, cols], SHl[1][:, c, cols],
                              c == 0, c == DC - 1)
                ins.then_inc(k_ps, 1)
            pe.wait_ge(s_lo, 8)
            for x_h, x_l, wi, b0, done in ((SHh[0], SHl[0], WR, 4, r_ps), (K2h, K2l, WV, 0, v_ps)):
                if done is v_ps:
                    pe.wait_ge(k_lo, 4)
                for t in range(TT):
                    tok = slice(t * P, (t + 1) * P)
                    for c in range(DC):
                        w = slice(c * D, (c + 1) * D)
                        ins = mm3(pe, BANKS[b0 + t // 2][:, (t % 2) * D:(t % 2 + 1) * D], x_h[:, c, tok],
                                  x_l[:, c, tok], kwh[:, wi, w], kwl[:, wi, w], c == 0, c == DC - 1)
                    if t % 2:
                        ins.then_inc(done, 1)

        next_layer()
        ln_stage("ln3x")
        with buffers():
            context_attention(3, 8, [by_cols("L3_xattn_wkT"), by_cols("L3_xattn_wvT"), by_rows("L3_xattn_wq")],
                              (D // HEADS) ** -0.5, 3, False, None)

        PAIRS = AE // 2
        WIDE = AE * AH
        ae_scope = ExitStack()
        scope = ae_scope
        XFA = sb("x_t_full", [P, DC, N])
        eraw = sb("enc_raw", [P, DC, WIDE])
        eh = sb("enc_hi", [P, DC, WIDE], F32R)
        el = sb("enc_lo", [P, DC, WIDE], F32R)
        draw = sb("dec_raw", [P, PAIRS, 2, D])
        dh = sb("dec_hi", [P, AE, D], F32R)
        dl = sb("dec_lo", [P, AE, D], F32R)
        hid = [sb(f"enc_hidden{i}", [P, HALF]) for i in range(2)]
        hidh = [sb(f"enc_hidden_hi{i}", [P, HALF], F32R) for i in range(2)]
        hidl = [sb(f"enc_hidden_lo{i}", [P, HALF], F32R) for i in range(2)]
        diff = [sb(f"recon_diff{i}", [P, HALF]) for i in range(4)]
        sqr = sb("recon_squares", [P, HALF])
        loss4 = sb("loss_parts", [P, AE, DC * NHALF])
        loss1 = sb("loss_sums", [P, AE])
        loss = sb("losses", [P, AE])
        lmin = sb("loss_min", [P, 1])
        iota = sb("adapter_numbers", [P, AE])
        iotab = sb("adapter_numbers_more", [P, AE])
        hot = sb("adapter_one_hot", [P, AE])
        top1 = sb("adapter_top1", [P, 1])
        adp = sb("adapter_connected", [P, 1])
        wrap = sb("adapter_wrap", [P, 1])
        braw = sb("base_raw", [P, DC, D])
        bh = sb("base_hi", [P, DC, D], F32R)
        bl = sb("base_lo", [P, DC, D], F32R)
        downs = sb("down_all", [P, DC, AE, AH])
        ups = sb("up_all", [P, AE, D])
        bups = sb("b_up_all", [P, AE, D])
        down = [sb(f"down{i}", [P, DC, AH]) for i in range(2)]
        up = [sb(f"up{i}", [P, D]) for i in range(2)]
        bup = [sb(f"b_up{i}", [P, D]) for i in range(2)]
        bdn = [sb(f"b_down{i}", [P, 1]) for i in range(2)]
        downh = sb("down_hi", [P, DC, 2, AH], F32R)
        downl = sb("down_lo", [P, DC, 2, AH], F32R)
        uph = sb("up_hi", [P, D], F32R)
        upl = sb("up_lo", [P, D], F32R)
        mid = sb("mid", [P, N])
        mids = sb("mid_stack", [P, N], F32R)
        ae_scope.close()
        scope = life
        ln_stage("ln3f", XF=XFA)

        UNITS3 = [(k, h) for k in range(PAIRS) for h in range(NHALF)]
        NU = len(UNITS3)
        ew_in = signal("enc_in")
        dw_in = signal("dec_in")
        ae_zero = signal("dec_zeros")
        ew_split = signal("enc_dec_split")
        e_ps = signal("enc_ready")
        e_relu = signal("enc_relu")
        e_hi = signal("enc_hidden_hi_ready")
        e_lo = signal("enc_hidden_lo_ready")
        d_ps = signal("dec_ready")
        d_diff = signal("dec_diff")
        d_sq = signal("dec_squared")
        iota_set = signal("adapter_numbers_set")
        l_sum = signal("loss_summed")
        l_all = signal("loss_over_partitions")
        a_steps = signal("adapter_steps")

        @part(sp_parts, "ln3f")
        def _(sp, b):
            for c in range(DC):
                sp.dma_start(eraw[:, c, :].rearrange("p (n h) -> p n h", n=AE),
                             A["L3_ffn_W_enc"].rearrange("n (c p) h -> c p n h", p=P)[c]).then_inc(ew_in, 16)
            for r in range(2):
                sp.dma_start(draw[r * AH:(r + 1) * AH, :, r, :],
                             A["L3_ffn_W_dec"].rearrange("(k r) h d -> r h k d", r=2)[r]).then_inc(dw_in, 16)
            sp.wait_ge(ew_in, 16 * DC)

        @part(pool_parts, "ln3f")
        def _(pool, b):
            for r in range(2):
                pool.memset(draw[r * AH:(r + 1) * AH, :, 1 - r, :], 0.0).then_inc(ae_zero, 1)
                pool.wait_ge(ae_zero, r + 1)
            pool.wait_ge(ew_in, 16 * DC)
            hi_of(pool, eh[:], eraw[:]).then_inc(ew_split, 1)
            pool.wait_ge(ew_split, 1)
            pool.tensor_tensor(el[:], eraw[:], eh[:].bitcast(F32), ALU.subtract).then_inc(ew_split, 1)
            pool.wait_ge(dw_in, 32)
            dr = draw[:].rearrange("p k r d -> p (k r) d")
            hi_of(pool, dh[:], dr).then_inc(ew_split, 1)
            pool.wait_ge(ew_split, 3)
            pool.tensor_tensor(dl[:], dr, dh[:].bitcast(F32), ALU.subtract).then_inc(ew_split, 1)
            for n in range(AE):
                pool.memset(iota[:, n:n + 1], float(n)).then_inc(iota_set, 1)

        @part(pe_parts, "route")
        def _(pe, b):
            pe.wait_ge(ew_split, 2)
            for u in range(NU + 1):
                if u < NU:
                    k, h = UNITS3[u]
                    cols = slice(h * HALF, (h + 1) * HALF)
                    if u >= 2:
                        pe.wait_ge(e_relu, u - 1)
                    for c in range(DC):
                        w = slice(k * P, (k + 1) * P)
                        ins = mm3(pe, BANKS[u % 2], eh[:, c, w], el[:, c, w], XTh[:, c, cols], XTl[:, c, cols],
                                  c == 0, c == DC - 1)
                    ins.then_inc(e_ps, 1)
                v = u - 1
                if v >= 0:
                    k, h = UNITS3[v]
                    if v == 0:
                        pe.wait_ge(ew_split, 4)
                    pe.wait_ge(e_lo, v + 1)
                    for q in range(4):
                        n, c = 2 * k + q // 2, q % 2
                        s = 4 * v + q
                        if s >= 6:
                            pe.wait_ge(d_diff, s - 5)
                        w = slice(c * P, (c + 1) * P)
                        mm3(pe, BANKS[2 + s % 6], dh[:, n, w], dl[:, n, w], hidh[v % 2][:], hidl[v % 2][:], True, True
                            ).then_inc(d_ps, 1)
            pe.wait_ge(l_sum, 1)
            pe.matmul(BANKS[6][:, 0:AE], ones[:], loss1[:], start=True, stop=True).then_inc(l_all, 1)

        @part(act_parts, "route")
        def _(act, b):
            for u in range(NU + 1):
                if u < NU:
                    k, h = UNITS3[u]
                    act.wait_ge(e_ps, u + 1)
                    if u >= 2:
                        act.wait_ge(e_lo, u - 1)
                    act.activation(hid[u % 2][:], BANKS[u % 2], ACT.Relu, bias=benc[:, k:k + 1]).then_inc(e_relu, 1)
                    act.wait_ge(e_relu, u + 1)
                    if u >= 2:
                        act.wait_ge(d_ps, 4 * (u - 1))
                    act.activation(hidh[u % 2][:], hid[u % 2][:], ACT.Copy).then_inc(e_hi, 1)
                v = u - 1
                if v >= 0:
                    k, h = UNITS3[v]
                    for q in range(4):
                        n, c = 2 * k + q // 2, q % 2
                        s = 4 * v + q
                        act.wait_ge(d_diff, s + 1)
                        if s:
                            act.wait_ge(d_sq, s)
                        act.activation(sqr[:], diff[s % 4][:], ACT.Square,
                                       accum_out=loss4[:, n, c * NHALF + h:c * NHALF + h + 1]).then_inc(d_sq, 1)

        @part(dve_parts, "route")
        def _(dve, b):
            for u in range(NU + 1):
                if u < NU:
                    dve.wait_ge(e_hi, u + 1)
                    if u >= 2:
                        dve.wait_ge(d_ps, 4 * (u - 1))
                    dve.tensor_tensor(hidl[u % 2][:], hid[u % 2][:], hidh[u % 2][:].bitcast(F32), ALU.subtract
                                      ).then_inc(e_lo, 1)
                v = u - 1
                if v >= 0:
                    k, h = UNITS3[v]
                    for q in range(4):
                        n, c = 2 * k + q // 2, q % 2
                        s = 4 * v + q
                        dve.wait_ge(d_ps, s + 1)
                        if s >= 4:
                            dve.wait_ge(d_sq, s - 3)
                        dve.scalar_tensor_tensor(diff[s % 4][:], BANKS[2 + s % 6], bdec[:, n, c:c + 1],
                                                 XFA[:, c, h * HALF:(h + 1) * HALF], ALU.add, ALU.subtract
                                                 ).then_inc(d_diff, 1)
            dve.wait_ge(d_sq, 4 * NU)
            dve.tensor_reduce(loss1[:], loss4[:], AX.X, ALU.add).then_inc(l_sum, 1)
            chain = Chain(dve, a_steps)
            dve.wait_ge(l_all, 1)
            dve.wait_ge(iota_set, AE)
            chain.step(dve.tensor_copy(loss[:], BANKS[6][:, 0:AE]))
            chain.step(dve.tensor_scalar(iotab[:], iota[:], float(-AE), None, ALU.add))
            chain.settle()
            chain.step(dve.tensor_reduce(lmin[:], loss[:], AX.X, ALU.min))
            chain.settle()
            chain.step(dve.scalar_tensor_tensor(hot[:], loss[:], lmin[:, 0:1], iotab[:], ALU.is_equal, ALU.mult))
            chain.settle()
            chain.step(dve.tensor_reduce(top1[:], hot[:], AX.X, ALU.min))
            chain.settle()
            chain.step(dve.scalar_tensor_tensor(hot[:], iotab[:], top1[:, 0:1], cidx[:], ALU.is_equal, ALU.mult))
            chain.settle()
            chain.step(dve.tensor_reduce(adp[:], hot[:], AX.X, ALU.add))
            chain.settle()
            chain.step(dve.tensor_scalar(wrap[:], adp[:], 0.0, float(AE), ALU.is_lt, ALU.mult))
            chain.settle()
            chain.step(dve.tensor_tensor(adp[:], adp[:], wrap[:], ALU.add))
            chain.settle()
            chain.step(dve.tensor_scalar(adp[:], adp[:], 0.0, float(AE - 1), ALU.max, ALU.min))
            chain.settle()
            chain.step(dve.tensor_scalar(hot[:], iota[:], adp[:, 0:1], None, ALU.is_equal))

        aw_in = signal("base_in")
        aw_sel_in = signal("adapters_in")
        aw_split = signal("base_split")
        pick = signal("adapter_picks")
        pick_hi = signal("adapter_hi")
        pick_lo = signal("adapter_lo")
        mid_ps = signal("mid_ready")
        mid_relu = signal("mid_relu")
        mid_hi = signal("mid_hi")
        mid_lo = signal("mid_lo")
        ad_ps = signal("adapted_ready")
        ad_row = signal("adapted_bias")
        ad_x = signal("adapted_residual")

        @part(sp_parts, "route")
        def _(sp, b):
            sp.dma_start(braw[:], A["L3_ffn_W_base"].rearrange("(c p) e -> p c e", p=P)).then_inc(aw_in, 16)
            for c in range(DC):
                sp.dma_start(downs[:, c, :, :], A["L3_ffn_W_down"].rearrange("n (c p) h -> c p n h", p=P)[c]
                             ).then_inc(aw_sel_in, 16)
            for r in range(2):
                sp.dma_start(ups[r * AH:(r + 1) * AH, :, :], A["L3_ffn_W_up"].rearrange("n h d -> h n d")
                             ).then_inc(aw_sel_in, 16)
            sp.dma_start(bups[:].rearrange("p n d -> p (n d)"), A["L3_ffn_b_up"].rearrange(
                "(a n) d -> a (n d)", a=1).broadcast_to([P, AE * D])).then_inc(aw_sel_in, 16)

        @part(pool_parts, "route")
        def _(pool, b):
            pool.wait_ge(aw_in, 16)
            hi_of(pool, bh[:], braw[:]).then_inc(aw_split, 1)
            pool.wait_ge(aw_split, 1)
            pool.tensor_tensor(bl[:], braw[:], bh[:].bitcast(F32), ALU.subtract).then_inc(aw_split, 1)

        @part(dve_parts, "adapt")
        def _(dve, b):
            chain = Chain(dve, pick)
            gate = tg[:, 2 * LAYERS - 1:2 * LAYERS]
            dve.wait_ge(aw_sel_in, 16 * (DC + 3))
            def choose(dsts):
                for n in range(AE):
                    own = hot[:, n:n + 1]
                    for dst, src in dsts:
                        d_ = dst[n % 2][:]
                        chain.step(dve.tensor_scalar(d_, src(n), own, None, ALU.mult) if n == 0 else
                                   dve.scalar_tensor_tensor(d_, src(n), own, dst[(n + 1) % 2][:], ALU.mult, ALU.add))
                    chain.settle()

            choose([(down, lambda n: downs[:, :, n, :]), (bdn, lambda n: bdown[:, n:n + 1])])
            dve.wait_ge(pick_hi, 1)
            twice = down[1][:].unsqueeze(2).broadcast_to([P, DC, 2, AH])
            dve.tensor_tensor(downl[:], twice, downh[:].bitcast(F32), ALU.subtract).then_inc(pick_lo, 1)
            choose([(up, lambda n: ups[:, n, :])])
            dve.wait_ge(pick_hi, 2)
            dve.tensor_tensor(upl[:], up[1][:], uph[:].bitcast(F32), ALU.subtract).then_inc(pick_lo, 1)
            for h in range(NHALF):
                cols = slice(h * HALF, (h + 1) * HALF)
                dve.wait_ge(mid_hi, h + 1)
                dve.tensor_tensor(mids[AH:P, cols], mid[AH:P, cols], mids[AH:P, cols].bitcast(F32), ALU.subtract
                                  ).then_inc(mid_lo, 1)
            choose([(bup, lambda n: bups[:, n, :])])
            dve.tensor_tensor(bup[0][:], bup[1][:], rowb[:, BBASE, :], ALU.add).then_inc(ad_row, 1)
            dve.wait_ge(ad_row, 1)
            dve.scalar_tensor_tensor(X[:], bup[0][:].unsqueeze(1).broadcast_to([P, TT, D]), gate, X[:],
                                     ALU.mult, ALU.add).then_inc(ad_row, 1)
            dve.wait_ge(ad_row, 2)
            for q in range(4):
                xt = X[:, 2 * q:2 * q + 2, :].rearrange("p t d -> p (t d)")
                dve.wait_ge(ad_ps, q + 1)
                dve.scalar_tensor_tensor(xt, BANKS[q], gate, xt, ALU.mult, ALU.add).then_inc(ad_x, 1)

        @part(act_parts, "adapt")
        def _(act, b):
            act.wait_ge(pick, 2 * AE)
            for r in range(2):
                ins = act.activation(downh[:, :, r, :], down[1][:], ACT.Copy)
            ins.then_inc(pick_hi, 1)
            act.wait_ge(pick, 3 * AE)
            act.activation(uph[:], up[1][:], ACT.Copy).then_inc(pick_hi, 1)
            for h in range(NHALF):
                cols = slice(h * HALF, (h + 1) * HALF)
                act.wait_ge(mid_ps, h + 1)
                act.activation(mid[:, cols], BANKS[6 + h], ACT.Relu, bias=bdn[1][:, 0:1]).then_inc(mid_relu, 1)
                act.wait_ge(mid_relu, h + 1)
                act.activation(mids[:, cols], mid[:, cols], ACT.Copy).then_inc(mid_hi, 1)

        @part(pe_parts, "adapt")
        def _(pe, b):
            acc = [BANKS[t // 2][:, (t % 2) * D:(t % 2 + 1) * D] for t in range(TT)]
            toks = [slice(t * P, (t + 1) * P) for t in range(TT)]
            pe.wait_ge(aw_split, 2)
            for t in range(TT):
                for c in range(DC):
                    mm3(pe, acc[t], XTh[:, c, toks[t]], XTl[:, c, toks[t]], bh[:, c, :], bl[:, c, :],
                        c == 0 and t % 2 == 0, False)
            pe.wait_ge(pick_lo, 1)
            for h in range(NHALF):
                cols = slice(h * HALF, (h + 1) * HALF)
                for c in range(DC):
                    ins = mm3(pe, BANKS[6 + h], downh[:, c, :, :].rearrange("p r h -> p (r h)"),
                              downl[:, c, :, :].rearrange("p r h -> p (r h)"),
                              XTh[:, c, cols], XTl[:, c, cols], c == 0, c == DC - 1)
                ins.then_inc(mid_ps, 1)
            pe.wait_ge(pick_lo, 2)
            for t in range(TT):
                if t % (TT // 2) == 0:
                    pe.wait_ge(mid_lo, t // (TT // 2) + 1)
                pe.matmul(acc[t], mids[:, toks[t]], uph[:], start=False, stop=False)
                ins = pe.matmul(acc[t], mids[:, toks[t]], upl[:], start=False, stop=bool(t % 2))
                if t % 2:
                    ins.then_inc(ad_ps, 1)
        next_layer()
        stored = signal("x_stored")

        @part(sp_parts, "store")
        def _(sp, b):
            sp.dma_start(out[bass.ds(b * N, N), :].rearrange("(t p) d -> p t d", p=P), X[:]
                         ).then_inc(stored, 16)
            sp.wait_ge(stored, 16)

        next_layer()

        block = life.enter_context(nc.Block())

        @block.sync
        def _(sp):
            sp_ternary(sp)
            sp_consts(sp)
            sp.wait_ge(const_set, 7)
            with sp.Fori(0, NB) as b:
                run(sp, "sp", b, sp_parts)

        @block.gpsimd
        def _(pool):
            pool_consts(pool)
            with pool.Fori(0, NB) as b:
                run(pool, "pool", b, pool_parts)

        @block.scalar
        def _(act):
            act_consts(act)
            with act.Fori(0, NB) as b:
                run(act, "act", b, act_parts)

        @block.vector
        def _(dve):
            dve_consts(dve)
            dve_ternary(dve)
            with dve.Fori(0, NB) as b:
                run(dve, "dve", b, dve_parts)

        @block.tensor
        def _(pe):
            pe.wait_ge(const_set, 7)
            pe_ternary(pe)
            with pe.Fori(0, NB) as b:
                run(pe, "pe", b, pe_parts)


_FLAT = {"x": (NB * N, D), "ctx_1024": (NB * J, D), "mask_BxSxS2_bk1": (NB * N, J)}
_TRANSPOSED = {"L0_xattn_Wq": "L0_xattn_WqT", "L0_ffn_w_gate": "L0_ffn_gT", "L0_ffn_w_up": "L0_ffn_uT",
               "L0_ffn_w_down": "L0_ffn_dT", "L1_ffn_gate_w": "L1_ffn_gateT", "L2_ffn_W_r": "L2_ffn_rT",
               "L2_ffn_W_k": "L2_ffn_kT", "L2_ffn_W_v": "L2_ffn_vT", "L3_xattn_wk": "L3_xattn_wkT",
               "L3_xattn_wv": "L3_xattn_wvT"}


def kernel(**inputs):
    import numpy as _np
    import concourse.bacc as _bacc
    from concourse import mybir as _mybir
    from concourse.bass_utils import run_bass_kernel_spmd as _run

    nc = _bacc.Bacc("TRN2", target_bir_lowering=False, num_devices=1)
    arrays, args = {}, {}
    for name, a in inputs.items():
        a = _np.asarray(a)
        if name in _FLAT:
            a = a.reshape(_FLAT[name])
        if name in _TRANSPOSED:
            name, a = _TRANSPOSED[name], a.T
        a = _np.ascontiguousarray(a)
        arrays[f"in_{name}_dram"] = a
        args[name] = nc.dram_tensor(f"in_{name}_dram", a.shape, _mybir.dt.from_np(a.dtype),
                                    kind="ExternalInput").ap()
    out = nc.dram_tensor("out_0_dram", (NB * N, D), F32, kind="ExternalOutput").ap()
    flamingo_kernel(nc, args, out)
    r = _run(nc, [arrays], core_ids=[0])
    return r.results[0]["out_0_dram"].reshape(NB, N, D)
```
